# Optimizing a Trainium2 kernel written in Bass

```python
import numpy as np
import jax
import jax.numpy as jnp

def _softmax(x, axis=-1):
    return jax.nn.softmax(x, axis=axis)
def _gelu(x):
    return jax.nn.gelu(x, approximate=True)
def _silu(x):
    return jax.nn.silu(x)
def _sigmoid(x):
    return jax.nn.sigmoid(x)
def _layernorm(x, axis=-1, eps=1e-5):
    m = jnp.mean(x, axis=axis, keepdims=True)
    v = jnp.var(x, axis=axis, keepdims=True)
    return (x - m) / jnp.sqrt(v + eps)
def _scatter_add(tgt, idx, src, axis=0):
    return tgt.at[idx].add(src)
def _segment_sum(src, seg, n):
    return jax.ops.segment_sum(src, seg, n)

kernel_name = 'mk_adj_preln_d4_adj_128_13c5c0'

def setup_inputs(seed: int = 0):
    np.random.seed(seed)
    _w = jnp.asarray
    def _rec_inputs():
        import jax
        import jax.numpy as jnp
        _gk = jax.random.key(seed)
        x = -0.0005207 + 1.001 * jax.random.normal(jax.random.fold_in(_gk, 1), (32, 512, 128), jnp.float32)
        _w = (1.0 + jnp.arange(512, dtype=jnp.float32)) ** -0.5
        _w = _w / _w.mean()
        _pij = jnp.clip(0.0625 * _w[:, None] * _w[None, :], 0.0, 1.0)
        _a = jax.random.uniform(jax.random.fold_in(_gk, 2), (512, 512)) < _pij
        _a = jnp.logical_or(_a, jnp.swapaxes(_a, -1, -2))
        _af = _a.astype(jnp.float32)
        adj = _af
        return x, adj
    x, adj = _rec_inputs()
    def _L0_gnn_setup():
        import jax, jax.numpy as jnp
        import numpy as np
        B, N, F_IN, F_OUT = (8, 2048, 128, 128)
        ALPHA = 0.1
        NEG_BIG = -9000000000000000.0

        def _pair_indices(n):
            m = jnp.arange(n)[:, None] * n + jnp.arange(n)[None, :]
            nn = n * n
            k1, k2 = (2 * m, 2 * m + 1)
            idx1 = jnp.where(k1 < nn, k1 // n, k1 % n)
            idx2 = jnp.where(k2 < nn, k2 // n, k2 % n)
            return (idx1, idx2)
        key = jax.random.key(seed)
        k1, k2, k3, k4 = jax.random.split(key, 4)
        x = jax.random.normal(k1, (B, N, F_IN), dtype=jnp.float32)
        adj = jnp.ones((N, N), dtype=jnp.float32) - jnp.eye(N, dtype=jnp.float32)
        others_weight = jax.random.normal(k2, (F_IN, F_OUT), dtype=jnp.float32) * (1.0 / np.sqrt(F_OUT))
        self_weight = jax.random.normal(k3, (F_IN, F_OUT), dtype=jnp.float32) * (1.0 / np.sqrt(F_OUT))
        att_weight = jax.random.normal(k4, (2 * F_OUT, 1), dtype=jnp.float32)
        return {'x': x, 'adj': adj, 'others_weight': others_weight, 'self_weight': self_weight, 'att_weight': att_weight}
    _L0_gnn_all = _L0_gnn_setup()
    _L0_gnn_in = {k: v for k, v in _L0_gnn_all.items() if k in ('others_weight', 'self_weight', 'att_weight', )}
    del _L0_gnn_all

    def _L1_gnn_setup():
        import jax, jax.numpy as jnp
        import numpy as np
        B, M, IN, HID, OUT = (8, 2048, 128, 128, 128)
        LN_EPS = 1e-05

        def _layernorm(x, g, b):
            mu = jnp.mean(x, axis=-1, keepdims=True)
            var = jnp.mean((x - mu) ** 2, axis=-1, keepdims=True)
            return (x - mu) * jax.lax.rsqrt(var + LN_EPS) * g + b
        key = jax.random.key(seed)
        ks = jax.random.split(key, 10)
        x = jax.random.normal(ks[0], (B, M, IN), dtype=jnp.float32)
        vals = jax.random.uniform(ks[1], (M, M), dtype=jnp.float32)
        keep = jax.random.uniform(ks[2], (M, M)) < 0.03
        A_final = jnp.where(keep, vals, 0.0) + jnp.eye(M, dtype=jnp.float32)
        s = 0.02
        return {'x': x, 'A_final': A_final, 'Wp': jax.random.normal(ks[3], (IN, HID), jnp.float32) * s, 'bp': jnp.zeros((HID,), jnp.float32), 'a_src': jax.random.normal(ks[4], (HID,), jnp.float32) * s, 'a_dst': jax.random.normal(ks[5], (HID,), jnp.float32) * s, 'gat_g': jnp.ones((HID,), jnp.float32), 'gat_b': jnp.zeros((HID,), jnp.float32), 'eps': jnp.zeros((1,), jnp.float32), 'W1': jax.random.normal(ks[6], (HID, HID), jnp.float32) * s, 'b1': jnp.zeros((HID,), jnp.float32), 'mlp_g': jnp.ones((HID,), jnp.float32), 'mlp_b': jnp.zeros((HID,), jnp.float32), 'W2': jax.random.normal(ks[7], (HID, OUT), jnp.float32) * s, 'b2': jnp.zeros((OUT,), jnp.float32)}
    _L1_gnn_all = _L1_gnn_setup()
    _L1_gnn_in = {k: v for k, v in _L1_gnn_all.items() if k in ('Wp', 'bp', 'a_src', 'a_dst', 'gat_g', 'gat_b', 'eps', 'W1', 'b1', 'mlp_g', 'mlp_b', 'W2', 'b2', )}
    del _L1_gnn_all

    def _L2_gnn_setup():
        import jax, jax.numpy as jnp
        import numpy as np
        NEG_INF = -9000000000000000.0
        ALPHA = 0.2
        key = jax.random.key(seed)
        k1, k2, k3, k4 = jax.random.split(key, 4)
        B, N, F_in, F_out = (8, 2048, 128, 128)
        h = jax.random.normal(k1, (B, N, F_in), dtype=jnp.float32)
        adj = jax.random.randint(k2, (N, N), 0, 2).astype(jnp.float32)
        W = jax.random.normal(k3, (F_in, F_out), dtype=jnp.float32) * 0.1
        a = jax.random.normal(k4, (2 * F_out, 1), dtype=jnp.float32) * 0.1
        bias = jnp.zeros((F_out,), dtype=jnp.float32)
        return {'h': h, 'adj': adj, 'W': W, 'a': a, 'bias': bias}
    _L2_gnn_all = _L2_gnn_setup()
    _L2_gnn_in = {k: v for k, v in _L2_gnn_all.items() if k in ('W', 'a', 'bias', )}
    del _L2_gnn_all

    def _L3_gnn_setup():
        import jax, jax.numpy as jnp
        import numpy as np
        NEG = -9000000000000000.0
        key = jax.random.key(seed)
        k1, k2, k3, k4 = jax.random.split(key, 4)
        B, N, F_in, F_out, MAX_E = (16384, 16, 128, 128, 256)
        inp = jax.random.normal(k1, (B, N, F_in), dtype=jnp.float32)
        adj = jax.random.uniform(k2, (N, N), dtype=jnp.float32)
        limit = 1.414 * np.sqrt(6.0 / (F_in + F_out))
        W = jax.random.uniform(k3, (2, F_in, F_out), dtype=jnp.float32, minval=-limit, maxval=limit)
        e = jnp.ones((1, MAX_E), dtype=jnp.float32)
        stdv = 1.0 / np.sqrt(F_out)
        bias = jax.random.uniform(k4, (F_out,), dtype=jnp.float32, minval=-stdv, maxval=stdv)
        return {'input': inp, 'adj': adj, 'W': W, 'e': e, 'bias': bias}
    _L3_gnn_all = _L3_gnn_setup()
    _L3_gnn_in = {k: v for k, v in _L3_gnn_all.items() if k in ('W', 'e', 'bias', )}
    del _L3_gnn_all

    return {
        "x": x,
        "adj": adj,
        "L0_gnn_others_weight": _L0_gnn_in["others_weight"],
        "L0_gnn_self_weight": _L0_gnn_in["self_weight"],
        "L0_gnn_att_weight": _L0_gnn_in["att_weight"],
        "L1_gnn_Wp": _L1_gnn_in["Wp"],
        "L1_gnn_bp": _L1_gnn_in["bp"],
        "L1_gnn_a_src": _L1_gnn_in["a_src"],
        "L1_gnn_a_dst": _L1_gnn_in["a_dst"],
        "L1_gnn_gat_g": _L1_gnn_in["gat_g"],
        "L1_gnn_gat_b": _L1_gnn_in["gat_b"],
        "L1_gnn_eps": _L1_gnn_in["eps"],
        "L1_gnn_W1": _L1_gnn_in["W1"],
        "L1_gnn_b1": _L1_gnn_in["b1"],
        "L1_gnn_mlp_g": _L1_gnn_in["mlp_g"],
        "L1_gnn_mlp_b": _L1_gnn_in["mlp_b"],
        "L1_gnn_W2": _L1_gnn_in["W2"],
        "L1_gnn_b2": _L1_gnn_in["b2"],
        "L2_gnn_W": _L2_gnn_in["W"],
        "L2_gnn_a": _L2_gnn_in["a"],
        "L2_gnn_bias": _L2_gnn_in["bias"],
        "L3_gnn_W": _L3_gnn_in["W"],
        "L3_gnn_e": _L3_gnn_in["e"],
        "L3_gnn_bias": _L3_gnn_in["bias"],
    }

def reference(x, adj, L0_gnn_others_weight, L0_gnn_self_weight, L0_gnn_att_weight, L1_gnn_Wp, L1_gnn_bp, L1_gnn_a_src, L1_gnn_a_dst, L1_gnn_gat_g, L1_gnn_gat_b, L1_gnn_eps, L1_gnn_W1, L1_gnn_b1, L1_gnn_mlp_g, L1_gnn_mlp_b, L1_gnn_W2, L1_gnn_b2, L2_gnn_W, L2_gnn_a, L2_gnn_bias, L3_gnn_W, L3_gnn_e, L3_gnn_bias):
    import jax
    import jax.numpy as jnp
    def _L0_gnn_ref(x, adj, others_weight, self_weight, att_weight):
        import jax, jax.numpy as jnp
        import numpy as np
        B, N, F_IN, F_OUT = (8, 2048, 128, 128)
        ALPHA = 0.1
        NEG_BIG = -9000000000000000.0

        def _pair_indices(n):
            m = jnp.arange(n)[:, None] * n + jnp.arange(n)[None, :]
            nn = n * n
            k1, k2 = (2 * m, 2 * m + 1)
            idx1 = jnp.where(k1 < nn, k1 // n, k1 % n)
            idx2 = jnp.where(k2 < nn, k2 // n, k2 % n)
            return (idx1, idx2)
        b, n, _ = x.shape
        f_out = others_weight.shape[1]
        h = x @ others_weight
        a1 = att_weight[:f_out, 0]
        a2 = att_weight[f_out:, 0]
        u1 = h @ a1
        u2 = h @ a2
        idx1, idx2 = _pair_indices(n)
        e = u1[:, idx1] + u2[:, idx2]
        e = jnp.where(e >= 0, e, ALPHA * e)
        att = jnp.where(adj > 0, e, NEG_BIG)
        att = jax.nn.softmax(att, axis=1)
        out = jnp.einsum('bik,bkl->bil', att, h)
        out = out + x @ self_weight
        return out

    def _L1_gnn_ref(x, A_final, Wp, bp, a_src, a_dst, gat_g, gat_b, eps, W1, b1, mlp_g, mlp_b, W2, b2):
        import jax, jax.numpy as jnp
        import numpy as np
        B, M, IN, HID, OUT = (8, 2048, 128, 128, 128)
        LN_EPS = 1e-05

        def _layernorm(x, g, b):
            mu = jnp.mean(x, axis=-1, keepdims=True)
            var = jnp.mean((x - mu) ** 2, axis=-1, keepdims=True)
            return (x - mu) * jax.lax.rsqrt(var + LN_EPS) * g + b
        h = jnp.einsum('bmi,ih->bmh', x, Wp) + bp
        s_src = jnp.einsum('bmh,h->bm', h, a_src)
        s_dst = jnp.einsum('bmh,h->bm', h, a_dst)
        scores = s_src[:, :, None] + s_dst[:, None, :]
        scores = jnp.where(scores >= 0, scores, 0.2 * scores)
        fill = jnp.finfo(scores.dtype).min
        scores = jnp.where((A_final <= 0)[None], fill, scores)
        attn = jax.nn.softmax(scores, axis=-1)
        weighted_adj = attn * A_final[None]
        h_gat = jnp.einsum('bmn,bnh->bmh', weighted_adj, h)
        h_gat = jax.nn.relu(_layernorm(h_gat, gat_g, gat_b))
        h_agg = jnp.einsum('mn,bnh->bmh', A_final, h_gat)
        h_gin = (1.0 + eps) * h_gat + h_agg
        z = jnp.einsum('bmh,hk->bmk', h_gin, W1) + b1
        z = jax.nn.relu(_layernorm(z, mlp_g, mlp_b))
        x_gin = jnp.einsum('bmk,ko->bmo', z, W2) + b2
        return jax.nn.relu(x_gin + h_gat)

    def _L2_gnn_ref(h, adj, W, a, bias):
        import jax, jax.numpy as jnp
        import numpy as np
        NEG_INF = -9000000000000000.0
        ALPHA = 0.2
        F_out = W.shape[1]
        Wh = jnp.einsum('bnf,fo->bno', h, W)
        a1 = a[:F_out, 0]
        a2 = a[F_out:, 0]
        f1 = Wh @ a1
        f2 = Wh @ a2
        e = jax.nn.leaky_relu(f1[:, :, None] + f2[:, None, :], negative_slope=ALPHA)
        e = jnp.where(adj[None, :, :] > 0, e, NEG_INF)
        attention = jax.nn.softmax(e, axis=2)
        h_prime = jnp.einsum('bij,bjo->bio', attention, Wh) + bias
        return jax.nn.elu(h_prime)

    def _L3_gnn_ref(input, adj, W, e, bias):
        import jax, jax.numpy as jnp
        import numpy as np
        NEG = -9000000000000000.0
        h0 = jnp.einsum('bnf,fg->bng', input, W[0])
        h1 = jnp.einsum('bnf,fg->bng', input, W[1])
        m = adj > 0
        idx = jnp.cumsum(m.reshape(-1).astype(jnp.int32)) - 1
        vals = e[0][idx].reshape(adj.shape)
        A = jnp.where(m, vals, jnp.float32(NEG))
        A = jax.nn.softmax(A, axis=1)
        M = jnp.eye(adj.shape[0], dtype=A.dtype)
        out = jnp.einsum('ij,bjg->big', A * M, h0) + jnp.einsum('ij,bjg->big', A * (1.0 - M), h1)
        return out + bias[None, None, :]

    h = jnp.maximum(_layernorm(x, axis=-1), 0.0)
    x = x + _L0_gnn_ref(h, adj, L0_gnn_others_weight, L0_gnn_self_weight, L0_gnn_att_weight)
    h = jnp.maximum(_layernorm(x, axis=-1), 0.0)
    x = x + _L1_gnn_ref(h, adj, L1_gnn_Wp, L1_gnn_bp, L1_gnn_a_src, L1_gnn_a_dst, L1_gnn_gat_g, L1_gnn_gat_b, L1_gnn_eps, L1_gnn_W1, L1_gnn_b1, L1_gnn_mlp_g, L1_gnn_mlp_b, L1_gnn_W2, L1_gnn_b2)
    h = jnp.maximum(_layernorm(x, axis=-1), 0.0)
    x = x + _L2_gnn_ref(h, adj, L2_gnn_W, L2_gnn_a, L2_gnn_bias)
    h = jnp.maximum(_layernorm(x, axis=-1), 0.0)
    x = x + _L3_gnn_ref(h, adj, L3_gnn_W, L3_gnn_e, L3_gnn_bias)
    return x


_drawn_inputs = setup_inputs


def setup_inputs(seed=0):
    import zlib

    import numpy as np

    out = dict(_drawn_inputs(seed))
    spreads = {'L1_gnn_bp': (0.0, 0.1),
     'L1_gnn_gat_g': (1.0, 0.2),
     'L1_gnn_gat_b': (0.0, 0.281),
     'L1_gnn_b1': (0.0, 2.0),
     'L1_gnn_mlp_g': (1.0, 0.6),
     'L1_gnn_mlp_b': (0.0, 0.8),
     'L1_gnn_b2': (0.0, 0.1),
     'L2_gnn_bias': (0.0, 0.1),
     'L3_gnn_e': (1.0, 0.6)}
    factors = {'L1_gnn_a_src': 64.0, 'L1_gnn_a_dst': 64.0, 'L3_gnn_bias': 3.209}
    for name, (base, spread) in spreads.items():
        noise = np.random.default_rng([zlib.crc32(name.encode()), seed]).standard_normal(out[name].shape)
        drawn = base * np.exp(spread * noise) if base else spread * noise
        out[name] = jnp.asarray(drawn.astype(out[name].dtype))
    for name, factor in factors.items():
        out[name] = (out[name] * factor).astype(out[name].dtype)
    return out
```

```python
from contextlib import ExitStack

import concourse.bass as bass
from concourse import mybir

P = 128
ALU = mybir.AluOpType
ACT = mybir.ActivationFunctionType
F32 = mybir.dt.float32
F32R = mybir.dt.float32r
I32 = mybir.dt.int32
AX_X = mybir.AxisListType.X
RMAX = bass.bass_isa.ReduceOp.max

NS = 2
G = 2
SLOTS = 4
RING = 2
LN_EPS = 1e-5
NEG = -9000000000000000.0
TINY = 1e-30
HUGE = 1e30

STAGES = [("stat0", 0), ("norm0", 1), ("coef0", 1), ("feat0", 1), ("coefm0", 0), ("coefb0", 1), ("fsplit0", 0),
          ("agg0", 2),
          ("stat1", 0), ("norm1", 1), ("feat1", 2), ("score1", 1), ("att1", G), ("gats1", 0), ("gat1", 0),
          ("gatl1", 0), ("gin1", 1), ("mlpa1", 1), ("mlps1", 0), ("mlpb1", 1), ("mlpc1", 1),
          ("stat2", 0), ("norm2", 1), ("feat2", 2), ("score2", 1), ("lift2", 0), ("att2", G), ("elud2", 0),
          ("elu2", 0), ("stat3", 0), ("norm3", 1), ("feat3", 2), ("agg3", 1)]


def bcast(ap, n):
    return ap.unsqueeze(2).to_broadcast([ap.shape[0], ap.shape[1], n])


def repeat(ap, n):
    return ap.unsqueeze(1).to_broadcast([ap.shape[0], n, ap.shape[1]])


def gnn_kernel(nc, x, adj, Wo_d, Ws_d, att0_d, Wp_d, bp_d, asrc_d, adst_d, gatg_d, gatb_d, eps_d, W1_d, b1_d,
               mlpg_d, mlpb_d, W2_d, b2_d, Wq_d, att2_d, bias2_d, W3_d, e_d, bias3_d, out):
    B, N, F = x.shape
    T = N // P
    TG = T * G
    HALF = T // 2
    WD = F + 2
    ITERS = B // (NS * G)
    NE = e_d.shape[1]
    MB = NE // P
    assert F == P and G == 2 and T == 4 and B % (NS * G) == 0 and TG * F == 1024

    ctx = ExitStack()
    with ctx:
        def sb(name, shape, dt=F32, stack=ctx):
            return stack.enter_context(nc.sbuf_tensor(name, shape, dt))

        def sem(name):
            return ctx.enter_context(nc.semaphore(name))

        ps = [ctx.enter_context(nc.psum_tensor(f"ps{i}", [P, 1024], F32)) for i in range(SLOTS)]

        ident = sb("ident", [P, P])
        ones = sb("ones", [P, P])
        minus_half = sb("minus_half", [P, TG])
        adjn = sb("adjn", [P, T, N], F32R)
        maskT = sb("maskT", [P, T, N], F32R)
        mask0b = sb("mask0b", [P, T, N // 2], F32R)
        empty0 = sb("empty0", [P, T, P], F32R)
        mask2 = sb("mask2", [P, T, N])
        rescue2 = sb("rescue2", [P, N])
        gin_hi = sb("gin_hi", [P, T, N], F32R)
        gin_lo = sb("gin_lo", [P, T, P], F32R)
        a3_hi = sb("a3_hi", [P, T, N], F32R)
        a3_lo = sb("a3_lo", [P, T, N], F32R)
        diag3 = sb("diag3", [P, T])
        Wo, Ws, Wp, W1, W2, Wq = (sb(n, [P, F]) for n in ("Wo", "Ws", "Wp", "W1", "W2", "Wq"))
        W3 = sb("W3", [P, 2, F])
        wcols0 = sb("wcols0", [P, 4])
        feat1w = sb("feat1w", [P, WD])
        feat2w = sb("feat2w", [P, WD])
        src1w = sb("src1w", [P, P])
        src2w = sb("src2w", [P, P])
        const1 = sb("const1", [P, 1])
        pick = sb("pick", [P, P], F32R)
        bias_p = sb("bias_p", [P, G, WD], F32R)
        bias_1 = sb("bias_1", [P, 4, F], F32R)
        bias_2 = sb("bias_2", [P, 4, F], F32R)
        gat_g, gat_b, bias2, bias3 = (sb(n, [P, F]) for n in ("gat_g", "gat_b", "bias2", "bias3"))
        mlp_g, mlp_b = sb("mlp_g", [P, 1]), sb("mlp_b", [P, 1])
        low8 = sb("low8", [P, TG])
        empty8 = sb("empty8", [P, TG])
        full8 = sb("full8", [P, TG])
        share8 = sb("share8", [P, TG])

        loaded = sem("loaded")
        POOL_SETUP = 9
        made = {n: sem("made_" + n) for n in (
            "pool", "adjn", "maskT", "turn", "WT_ps", "WT", "rowtot", "bprep", "wvec", "rank_ps", "rank", "counts",
            "off", "row_of", "offm", "edges_ps", "edge_rows", "at", "cover", "values", "left3", "nmax", "exp3",
            "soft3", "turn3", "a3_hi", "gin_hi", "cast_hi")}
        dve_order = sem("dve_order")
        act_order = sem("act_order")
        pool_order = sem("pool_order")

        ORDER = [(name, s) for name, _ in STAGES for s in range(NS)]
        need = dict(STAGES)
        tiles, total = {}, 0
        rings, used = {}, 0
        for name, s in ORDER:
            tiles[name, s] = [((total + k) % SLOTS, (total + k) // SLOTS) for k in range(need[name])]
            total += need[name]
            if name.startswith("att"):
                rings[name, s] = [((used + b) % RING, (used + b) // RING) for b in range(G)]
                used += G
        assert total % SLOTS == 0 and used % RING == 0
        USES, RUSES = total // SLOTS, used // RING

        full = [sem(f"psum_full{i}") for i in range(SLOTS)]
        taken = [sem(f"psum_taken{i}") for i in range(SLOTS)]
        p_full = [sem(f"matrix_full{i}") for i in range(RING)]
        p_taken = [sem(f"matrix_taken{i}") for i in range(RING)]
        sig = {n: [sem(f"{n}_{s}") for s in range(NS)] for n in (
            "x_loaded", "raw_free", "stored", "var", "rstd", "normed", "cmax", "cmax_all", "cdiff", "cexp",
            "coef", "scaled", "hi", "lo", "dmax", "dmax_all", "ddiff", "dexp", "r_ready", "lifted", "gated",
            "eluexp", "shifted")}

        with ExitStack() as sc:
            adj_raw = sb("adj_raw", [P, T, N], F32, sc)
            upper = sb("upper", [P, T, N], F32R, sc)
            strict = sb("strict", [P, T, N], F32, sc)
            rank = sb("rank", [P, T, N], F32R, sc)
            row_of = sb("row_of", [P, MB, N], F32, sc)
            row_ofT = sb("row_ofT", [P, T, NE], F32R, sc)
            at = sb("at", [P, MB, N], F32, sc)
            e_at = sb("e_at", [P, MB, N], F32, sc)
            v3 = sb("v3", [P, T, N], F32, sc)
            work = sb("work", [P, T, N], F32, sc)
            WoT, WpT, WqT = (sb(n, [P, F], F32, sc) for n in ("WoT", "WpT", "WqT"))
            bprep = sb("bprep", [P, P], F32, sc)
            rowtot_b = sb("rowtot_b", [P, N], F32, sc)
            off_b = sb("off_b", [P, N], F32, sc)
            cntrep = sb("cntrep", [P, T, P], F32, sc)
            att0, asd, att2 = (sb(n, [P, 2], F32, sc) for n in ("att0", "asd", "att2"))
            bpcol, epscol, e255 = (sb(n, [P, 1], F32, sc) for n in ("bpcol", "epscol", "e255"))
            e_col = sb("e_col", [P, MB], F32, sc)
            brow = sb("brow", [P, 3, F], F32, sc)
            bhi = sb("bhi", [P, 3, F], F32R, sc)
            blo = sb("blo", [P, 3, F], F32R, sc)
            m_int = sb("m_int", [P, NE], I32, sc)
            mc_int = sb("mc_int", [P, MB], I32, sc)
            m_row = sb("m_row", [P, NE], F32, sc)
            m_col = sb("m_col", [P, MB], F32, sc)
            cnt_row = sb("cnt_row", [P, T], F32, sc)
            off_col = sb("off_col", [P, T], F32, sc)
            end_col = sb("end_col", [P, T], F32, sc)
            m_loc = sb("m_loc", [P, MB], F32, sc)
            cnt_all = sb("cnt_all", [P, T], F32, sc)
            cnt_low = sb("cnt_low", [P, T], F32, sc)
            empty4 = sb("empty4", [P, T], F32, sc)
            asum = sb("asum", [P, 1], F32, sc)
            epsd = sb("epsd", [P, P], F32, sc)
            diagv = sb("diagv", [P, T, P], F32, sc)
            small = sb("small", [P, 8], F32, sc)
            rmax = sb("rmax", [P, T], F32, sc)
            rsum = sb("rsum", [P, T], F32, sc)
            rinv = sb("rinv", [P, T], F32, sc)
            wv = sb("wv", [P, 8], F32, sc)

            LOADS = [(adj_raw[:], adj.rearrange("(t p) j -> p t j", p=P)),
                     (Wo[:], Wo_d), (Ws[:], Ws_d), (Wp[:], Wp_d), (W1[:], W1_d), (W2[:], W2_d), (Wq[:], Wq_d),
                     (W3[:], W3_d.rearrange("k f g -> f k g")),
                     (att0[:, 0:1], att0_d[0:P, :]), (att0[:, 1:2], att0_d[P:2 * P, :]),
                     (att2[:, 0:1], att2_d[0:P, :]), (att2[:, 1:2], att2_d[P:2 * P, :]),
                     (asd[:, 0:1], asrc_d.rearrange("(p o) -> p o", o=1)),
                     (asd[:, 1:2], adst_d.rearrange("(p o) -> p o", o=1)),
                     (bpcol[:], bp_d.rearrange("(p o) -> p o", o=1)),
                     (mlp_g[:], mlpg_d.rearrange("(p o) -> p o", o=1)),
                     (mlp_b[:], mlpb_d.rearrange("(p o) -> p o", o=1)),
                     (brow[:, 0, :], bp_d.partition_broadcast(P)),
                     (brow[:, 1, :], b1_d.partition_broadcast(P)),
                     (brow[:, 2, :], b2_d.partition_broadcast(P)),
                     (gat_g[:], gatg_d.partition_broadcast(P)), (gat_b[:], gatb_d.partition_broadcast(P)),
                     (bias2[:], bias2_d.partition_broadcast(P)), (bias3[:], bias3_d.partition_broadcast(P)),
                     (epscol[:], eps_d.partition_broadcast(P)),
                     (e255[:], e_d[0, NE - 1:NE].partition_broadcast(P)),
                     *[(e_col[:, m:m + 1], e_d[0, m * P:(m + 1) * P].rearrange("(p o) -> p o", o=1))
                       for m in range(MB)]]

            with nc.Block() as block:
                @block.sync
                def _(sp):
                    for dst, src in LOADS:
                        sp.dma_start(dst, src).then_inc(loaded, 16)
                    for s in taken + p_taken:
                        sp.sem_inc(s, 1)
                    for s in sig["stored"]:
                        sp.sem_inc(s, 16)
                    sp.wait_ge(loaded, 16 * len(LOADS))

                @block.gpsimd
                def _(pool):
                    nc.gpsimd.memset(ident[:], 0.0).then_inc(made["pool"], 1)
                    nc.gpsimd.memset(ones[:], 1.0).then_inc(made["pool"], 1)
                    nc.gpsimd.memset(work[:], 1.0).then_inc(made["pool"], 1)
                    nc.gpsimd.memset(minus_half[:], -0.5).then_inc(made["pool"], 1)
                    pool.wait_ge(made["pool"], 4)
                    nc.gpsimd.affine_select(out=ident[:], in_=ident[:], compare_op=ALU.not_equal, fill=1.0, base=0,
                                            pattern=[[-1, P]], channel_multiplier=1).then_inc(made["pool"], 1)
                    nc.gpsimd.affine_select(out=upper[:], in_=work[:], compare_op=ALU.is_ge, fill=0.0, base=0,
                                            pattern=[[-P, T], [1, N]], channel_multiplier=-1).then_inc(made["pool"], 1)
                    nc.gpsimd.affine_select(out=strict[:], in_=work[:], compare_op=ALU.is_gt, fill=0.0, base=0,
                                            pattern=[[-P, T], [1, N]], channel_multiplier=-1).then_inc(made["pool"], 1)
                    nc.gpsimd.iota(m_int[:], [[1, NE]], base=0, channel_multiplier=0).then_inc(made["pool"], 1)
                    nc.gpsimd.iota(mc_int[:], [[P, MB]], base=0, channel_multiplier=1).then_inc(made["pool"], 1)

                @block.tensor
                def _(pe):
                    T_, MM = nc.tensor.transpose, nc.tensor.matmul
                    pe.wait_ge(made["adjn"], 1)
                    pe.wait_ge(made["pool"], POOL_SETUP)
                    for j in range(T):
                        for i in range(T):
                            o = (j % 2) * N + i * P
                            mm = T_(ps[j // 2][:, o:o + P], adjn[:, i, j * P:(j + 1) * P].bitcast(F32), ident[:])
                    mm.then_inc(made["turn"], 1)
                    pe.wait_ge(loaded, 16 * len(LOADS))
                    for n, w in enumerate((Wo, Wp, Wq)):
                        mm = T_(ps[2][:, n * P:(n + 1) * P], w[:], ident[:])
                    mm.then_inc(made["WT_ps"], 1)
                    pe.wait_ge(made["maskT"], 1)
                    for j in range(T):
                        mm = MM(ps[3][:, 0:N], ones[:], maskT[:, j, :].bitcast(F32), start=(j == 0), stop=(j == T - 1))
                    mm.then_inc(made["rowtot"], 1)
                    pe.wait_ge(made["bprep"], 1)
                    pe.wait_ge(made["WT"], 1)
                    MM(ps[2][:, 512:514], WoT[:], att0[:], start=True, stop=True)
                    MM(ps[2][:, 514:516], WpT[:], asd[:], start=True, stop=True)
                    MM(ps[2][:, 516:518], WqT[:], att2[:], start=True, stop=True)
                    MM(ps[2][:, 518:519], bprep[:], asum[:], start=True, stop=True).then_inc(made["wvec"], 1)
                    for i in range(T):
                        for j in range(T):
                            mm = MM(ps[i // 2][:, (i % 2) * N:(i % 2) * N + N], maskT[:, j, i * P:(i + 1) * P],
                                    upper[:, j, :], start=(j == 0), stop=(j == T - 1))
                    mm.then_inc(made["rank_ps"], 1)
                    pe.wait_ge(made["counts"], 1)
                    for i in range(T):
                        for k in range(T):
                            MM(ps[2][:, 16 + i:17 + i], strict[:, k, i * P:(i + 1) * P], cnt_row[:, k:k + 1],
                               start=(k == 0), stop=(k == T - 1))
                    for k in range(T):
                        mm = MM(ps[3][:, N:2 * N], cntrep[:, k, :], strict[:, k, :], start=(k == 0), stop=(k == T - 1))
                    mm.then_inc(made["off"], 1)
                    pe.wait_ge(made["row_of"], 1)
                    for m in range(MB):
                        for i in range(T):
                            mm = MM(ps[2][:, 32 + m:33 + m], row_ofT[:, i, m * P:(m + 1) * P].bitcast(F32),
                                    off_col[:, i:i + 1], start=(i == 0), stop=(i == T - 1))
                    mm.then_inc(made["offm"], 1)
                    pe.wait_ge(made["rank"], 1)
                    for t, src in enumerate((adjn, rank)):
                        for m in range(MB):
                            for i in range(T):
                                mm = MM(ps[t][:, m * N:(m + 1) * N], row_ofT[:, i, m * P:(m + 1) * P], src[:, i, :],
                                        start=(i == 0), stop=(i == T - 1))
                    mm.then_inc(made["edges_ps"], 1)
                    pe.wait_ge(made["at"], 1)
                    for src, tile0, name in ((at, 2, "cover"), (e_at, 0, "values")):
                        for i in range(T):
                            for m in range(MB):
                                mm = MM(ps[tile0 + i // 2][:, (i % 2) * N:(i % 2) * N + N],
                                        row_of[:, m, i * P:(i + 1) * P], src[:, m, :],
                                        start=(m == 0), stop=(m == MB - 1))
                        mm.then_inc(made[name], 1)
                    pe.wait_ge(made["soft3"], 1)
                    for j in range(T):
                        for i in range(T):
                            o = (j % 2) * N + i * P
                            mm = T_(ps[j // 2][:, o:o + P], v3[:, i, j * P:(j + 1) * P], ident[:])
                    mm.then_inc(made["turn3"], 1)

                @block.scalar
                def _(act):
                    A = nc.scalar.activation
                    act.wait_ge(made["turn"], 1)
                    A(maskT[:, 0:2, :], ps[0][:].rearrange("p (a n) -> p a n", a=2), ACT.Copy)
                    A(maskT[:, 2:4, :], ps[1][:].rearrange("p (a n) -> p a n", a=2), ACT.Copy).then_inc(made["maskT"], 1)
                    act.wait_ge(made["WT_ps"], 1)
                    for n, w in enumerate((WoT, WpT, WqT)):
                        a = A(w[:], ps[2][:, n * P:(n + 1) * P], ACT.Copy)
                    a.then_inc(made["WT"], 1)
                    act.wait_ge(made["maskT"], 1)
                    A(gin_hi[:], maskT[:].bitcast(F32), ACT.Copy).then_inc(made["gin_hi"], 1)
                    act.wait_ge(made["rank_ps"], 1)
                    A(rank[:, 0:2, :], ps[0][:].rearrange("p (a n) -> p a n", a=2), ACT.Copy)
                    A(rank[:, 2:4, :], ps[1][:].rearrange("p (a n) -> p a n", a=2), ACT.Copy).then_inc(made["rank"], 1)
                    act.wait_ge(made["edges_ps"], 1)
                    act.wait_ge(made["row_of"], 1)
                    A(at[:], ps[0][:].rearrange("p (m n) -> p m n", m=MB), ACT.Copy).then_inc(made["edge_rows"], 1)
                    act.wait_ge(made["nmax"], 1)
                    for i in range(T):
                        a = A(work[:, i, :], v3[:, i, :], ACT.Exp, bias=rmax[:, i:i + 1], accum_out=rsum[:, i:i + 1])
                    a.then_inc(made["exp3"], 1)
                    act.wait_ge(made["turn3"], 1)
                    A(a3_hi[:, 0:2, :], ps[0][:].rearrange("p (a n) -> p a n", a=2), ACT.Copy)
                    A(a3_hi[:, 2:4, :], ps[1][:].rearrange("p (a n) -> p a n", a=2), ACT.Copy).then_inc(made["a3_hi"], 1)

                @block.vector
                def _(dve):
                    V = nc.vector
                    order = [0]

                    def link(ins):
                        order[0] += 1
                        ins.then_inc(dve_order, 1)
                        dve.wait_ge(dve_order, order[0])

                    dve.wait_ge(loaded, 16 * len(LOADS))
                    V.tensor_scalar(adjn[:], adj_raw[:], 0.0, None, ALU.is_gt).then_inc(made["adjn"], 1)
                    dve.wait_ge(made["pool"], POOL_SETUP)
                    dve.wait_ge(made["adjn"], 1)
                    V.tensor_copy(m_row[:], m_int[:])
                    V.tensor_copy(m_col[:], mc_int[:])
                    V.tensor_tensor(asum[:], asd[:, 0:1], asd[:, 1:2], ALU.add)
                    V.tensor_scalar(bprep[:], ones[:], bpcol[:, 0:1], None, ALU.mult).then_inc(made["bprep"], 1)
                    link(V.reduce_sum(cnt_row[:], adjn[:].bitcast(F32), AX_X))
                    for k in range(T):
                        a = V.tensor_scalar(cntrep[:, k, :], ones[:], cnt_row[:, k:k + 1], None, ALU.mult)
                    a.then_inc(made["counts"], 1)
                    dve.wait_ge(made["maskT"], 1)
                    mT = maskT[:].bitcast(F32)
                    V.reduce_sum(cnt_low[:], mT[:, :, N // 2:N], AX_X)
                    link(V.reduce_sum(cnt_all[:], mT, AX_X))
                    link(V.tensor_scalar(empty4[:], cnt_all[:], 0.0, None, ALU.is_equal))
                    for k in range(T):
                        V.tensor_scalar(mask0b[:, k, :], mT[:, k, N // 2:N], empty4[:, k:k + 1], None, ALU.max)
                        V.tensor_scalar(empty0[:, k, :], ones[:], empty4[:, k:k + 1], None, ALU.mult)
                    e4, l4 = bcast(empty4[:], G), bcast(cnt_low[:], G)
                    v8 = [t[:].rearrange("p (k b) -> p k b", b=G) for t in (low8, empty8, full8, share8)]
                    V.tensor_copy(v8[0], l4)
                    V.tensor_copy(v8[1], e4)
                    V.tensor_scalar(v8[2], e4, -1.0, 1.0, ALU.mult, ALU.add)
                    V.tensor_scalar(v8[3], e4, 1.0 / N, None, ALU.mult)
                    link(V.tensor_copy(bhi[:], brow[:]))
                    V.tensor_tensor(blo[:], brow[:], bhi[:].bitcast(F32), ALU.subtract)
                    V.memset(pick[:].bitcast(F32), 0.0)
                    V.memset(bias_p[:].bitcast(F32), 0.0)
                    V.memset(bias_1[:].bitcast(F32), 0.0)
                    link(V.memset(bias_2[:].bitcast(F32), 0.0))
                    for p0, src in ((0, bhi), (32, blo)):
                        row = slice(p0, p0 + 1)
                        V.tensor_copy(pick[row, :], ones[row, :])
                        for g in range(G):
                            V.tensor_copy(bias_p[row, g, 0:F], src[row, 0, :].bitcast(F32))
                        for g in range(4):
                            V.tensor_copy(bias_1[row, g, :], src[row, 1, :].bitcast(F32))
                            V.tensor_copy(bias_2[row, g, :], src[row, 2, :].bitcast(F32))
                    link(V.tensor_scalar(small[:, 0:1], epscol[:], 1.0, None, ALU.add))
                    link(V.tensor_scalar(epsd[:], ident[:], small[:, 0:1], None, ALU.mult))
                    for k in range(T):
                        a = V.tensor_tensor(diagv[:, k, :], mT[:, k, k * P:(k + 1) * P], epsd[:], ALU.add)
                    link(a)
                    dve.wait_ge(made["gin_hi"], 1)
                    for k in range(T):
                        a = V.tensor_copy(gin_hi[:, k, k * P:(k + 1) * P], diagv[:, k, :])
                    link(a)
                    for k in range(T):
                        V.tensor_tensor(gin_lo[:, k, :], diagv[:, k, :], gin_hi[:, k, k * P:(k + 1) * P].bitcast(F32),
                                        ALU.subtract)
                    dve.wait_ge(made["rowtot"], 1)
                    V.tensor_copy(rowtot_b[:], ps[3][:, 0:N])
                    link(V.tensor_scalar(rescue2[:], ps[3][:, 0:N], 0.0, None, ALU.is_equal))
                    for k in range(T):
                        a = V.tensor_tensor(mask2[:, k, :], mT[:, k, :], rescue2[:], ALU.max)
                    link(a)
                    V.tensor_scalar(rescue2[:], rescue2[:], HUGE, None, ALU.mult)
                    dve.wait_ge(made["wvec"], 1)
                    V.tensor_copy(const1[:], ps[2][:, 518:519])
                    V.memset(feat1w[:, F + 1:WD], 0.0)
                    V.memset(feat2w[:, F + 1:WD], 0.0)
                    link(V.tensor_copy(wv[:, 0:6], ps[2][:, 512:518]))
                    V.tensor_tensor(wcols0[:, 0:1], wv[:, 0:1], wv[:, 1:2], ALU.add)
                    V.tensor_copy(wcols0[:, 1:3], wv[:, 0:2])
                    V.memset(wcols0[:, 3:4], 0.0)
                    V.tensor_copy(feat1w[:, 0:F], Wp[:])
                    V.tensor_copy(feat1w[:, F:F + 1], wv[:, 3:4])
                    V.tensor_copy(feat2w[:, 0:F], Wq[:])
                    V.tensor_copy(feat2w[:, F:F + 1], wv[:, 5:6])
                    V.tensor_scalar(src1w[:], ones[:], wv[:, 2:3], None, ALU.mult)
                    V.tensor_scalar(src2w[:], ones[:], wv[:, 4:5], None, ALU.mult)
                    dve.wait_ge(made["off"], 1)
                    V.tensor_copy(off_col[:], ps[2][:, 16:16 + T])
                    link(V.tensor_copy(off_b[:], ps[3][:, N:2 * N]))
                    V.tensor_tensor(end_col[:], off_col[:], cnt_row[:], ALU.add)
                    link(V.tensor_tensor(rowtot_b[:], rowtot_b[:], off_b[:], ALU.add))
                    for i in range(T):
                        V.tensor_scalar(v3[:, i, 0:NE], m_row[:], end_col[:, i:i + 1], None, ALU.is_ge)
                    for m in range(MB):
                        a = V.tensor_scalar(at[:, m, :], rowtot_b[:], m_col[:, m:m + 1], None, ALU.is_le)
                    link(a)
                    for i in range(T):
                        V.scalar_tensor_tensor(out=row_ofT[:, i, :], in0=m_row[:], scalar=off_col[:, i:i + 1],
                                               in1=v3[:, i, 0:NE], op0=ALU.is_ge, op1=ALU.subtract)
                    for m in range(MB):
                        a = V.scalar_tensor_tensor(out=row_of[:, m, :], in0=off_b[:], scalar=m_col[:, m:m + 1],
                                                   in1=at[:, m, :], op0=ALU.is_le, op1=ALU.subtract)
                    a.then_inc(made["row_of"], 1)
                    dve.wait_ge(made["offm"], 1)
                    link(V.scalar_tensor_tensor(out=m_loc[:], in0=ps[2][:, 32:32 + MB], scalar=-1.0, in1=m_col[:],
                                                op0=ALU.mult, op1=ALU.add))
                    link(V.tensor_scalar(m_loc[:], m_loc[:], 1.0, None, ALU.add))
                    dve.wait_ge(made["edge_rows"], 1)
                    for m in range(MB):
                        a = V.scalar_tensor_tensor(out=at[:, m, :], in0=ps[1][:, m * N:(m + 1) * N],
                                                   scalar=m_loc[:, m:m + 1], in1=at[:, m, :], op0=ALU.is_equal,
                                                   op1=ALU.mult)
                    link(a)
                    for m in range(MB):
                        a = V.tensor_scalar(e_at[:, m, :], at[:, m, :], e_col[:, m:m + 1], None, ALU.mult)
                    a.then_inc(made["at"], 1)
                    dve.wait_ge(made["cover"], 1)
                    for h in range(2):
                        a = V.tensor_tensor(v3[:, 2 * h:2 * h + 2, :], adjn[:, 2 * h:2 * h + 2, :].bitcast(F32),
                                            ps[2 + h][:].rearrange("p (a n) -> p a n", a=2), ALU.subtract)
                    link(a)
                    dve.wait_ge(made["values"], 1)
                    for i in range(T):
                        a = V.scalar_tensor_tensor(out=v3[:, i, :], in0=v3[:, i, :], scalar=e255[:, 0:1],
                                                   in1=ps[i // 2][:, (i % 2) * N:(i % 2) * N + N], op0=ALU.mult,
                                                   op1=ALU.add)
                    V.tensor_scalar(work[:], adjn[:].bitcast(F32), -1.0, -NEG, ALU.add, ALU.mult)
                    link(V.memset(small[:, 2:3], 0.0))
                    link(V.tensor_tensor(v3[:], v3[:], work[:], ALU.add))
                    link(V.reduce_max(rmax[:], v3[:], AX_X))
                    V.tensor_scalar(rmax[:], rmax[:], -1.0, None, ALU.mult).then_inc(made["nmax"], 1)
                    dve.wait_ge(made["exp3"], 1)
                    link(V.reciprocal(rinv[:], rsum[:]))
                    link(V.tensor_tensor(v3[:], work[:], bcast(rinv[:], N), ALU.mult))
                    for i in range(T):
                        a = V.tensor_tensor(diagv[:, i, :], v3[:, i, i * P:(i + 1) * P], ident[:], ALU.mult)
                    link(a)
                    V.reduce_sum(diag3[:], diagv[:], AX_X)
                    for i in range(T):
                        a = V.tensor_tensor(v3[:, i, i * P:(i + 1) * P], v3[:, i, i * P:(i + 1) * P], diagv[:, i, :],
                                            ALU.subtract)
                    a.then_inc(made["soft3"], 1)
                    dve.wait_ge(made["a3_hi"], 1)
                    for h in range(2):
                        V.tensor_tensor(a3_lo[:, 2 * h:2 * h + 2, :], ps[h][:].rearrange("p (a n) -> p a n", a=2),
                                        a3_hi[:, 2 * h:2 * h + 2, :].bitcast(F32), ALU.subtract)
                    dve.sem_clear(dve_order)

        def per(name, shape, dt=F32):
            return [sb(f"{name}{s}", shape, dt) for s in range(NS)]

        X = per("X", [P, TG, F])
        XL = per("XL", [P, TG, F])
        XN = per("XN", [P, TG, F])
        HT = per("HT", [P, G, N])
        HE = per("HE", [P, TG, WD])
        Y = per("Y", [P, TG, WD])
        VA = per("VA", [P, TG, F])
        SC = per("SC", [P, TG, F])
        HI = per("HI", [P, TG, F], F32R)
        LO = per("LO", [P, TG, F], F32R)
        HIB = per("HIB", [P, TG, F], F32R)
        LOB = per("LOB", [P, TG, F], F32R)
        R = per("R", [P, G, N])
        ST = per("ST", [P, TG, 6])
        US = per("US", [P, TG, 4])
        CD = per("CD", [P, 12])
        CF = per("CF", [P, 2 * TG])
        CE = per("CE", [P, 2 * TG])
        MX = per("MX", [P, 8])
        SM = per("SM", [P, 16, TG])
        PT = [sb(f"PT{r}", [P, T, N]) for r in range(RING)]
        S_SUM, S_DIF, S_Q, S_DD, S_VAR, S_MEAN, S_RSTD, S_INV, S_RS, S_A, S_B, S_Z = range(12)

        LNS = ["norm0", "norm1", "gat1", "mlpb1", "norm2", "norm3"]
        NLN = len(LNS)
        ln_at = {n: k for k, n in enumerate(LNS)}
        NORMED = ["norm0", "norm1", "gat1", "mlpb1", "norm2", "elu2", "norm3"]
        nd_at = {n: k for k, n in enumerate(NORMED)}
        ATT = {"1": 0, "2": 1}
        HIS = {"a0": 0, "b0": 1, "1": 2, "3a": 3, "3b": 4}
        LOS = {"0": 0, "1": 1, "3": 2}

        def count(it, per_group, n):
            return it * per_group + (n + 1)

        def rows_of(ap, it, s, b):
            return ap.rearrange("b (t p) f -> b p t f", p=P)[it * (NS * G) + (s * G + b)]

        with nc.Block() as block:
            @block.sync
            def _(sp):
                def load(it, s):
                    for b in range(G):
                        sp.dma_start(XL[s][:, b::G, :], rows_of(x, it, s, b)).then_inc(sig["x_loaded"][s], 16)

                def store(it, s):
                    slot, k = tiles["agg3", s][0]
                    sp.wait_ge(taken[slot], 1 + count(it, USES, k))
                    for b in range(G):
                        sp.dma_start(rows_of(out, it, s, b), X[s][:, b::G, :]).then_inc(sig["stored"][s], 16)

                for s in range(NS):
                    load(0, s)
                with sp.Fori(0, ITERS - 1) as it:
                    for s in range(NS):
                        sp.wait_ge(sig["raw_free"][s], count(it, 1, 0))
                        load(it + 1, s)
                    for s in range(NS):
                        store(it, s)
                for s in range(NS):
                    store(ITERS - 1, s)
                for s in range(NS):
                    sp.wait_ge(sig["stored"][s], 16 * G * ITERS + 16)

            @block.tensor
            def _(pe):
                T_ = nc.tensor.transpose

                def MM(o, w, m, start, stop):
                    return nc.tensor.matmul(o, w, m, start=start, stop=stop, skip_group_check=True)

                def open_tile(it, name, s, n=0):
                    slot, k = tiles[name, s][n]
                    pe.wait_ge(taken[slot], it * USES + k + 1)
                    return ps[slot], full[slot]

                def turned(it, name, s):
                    slot, k = tiles[name, s][0]
                    pe.wait_ge(taken[slot], 1 + count(it, USES, k))

                def turn_rows(it, name, s):
                    pe.wait_ge(sig["normed"][s], count(it, len(NORMED), nd_at[name]))
                    o, done = open_tile(it, name, s)
                    for b in range(G):
                        for t in range(T):
                            c = b * N + t * P
                            mm = T_(o[:, c:c + P], XN[s][:, t * G + b, :], ident[:])
                    mm.then_inc(done, 1)

                def blk(s, b, t):
                    return HT[s][:, b, t * P:(t + 1) * P]

                def coef0(it, s):
                    turned(it, "norm0", s)
                    o, done = open_tile(it, "coef0", s, 0)
                    for t in range(HALF):
                        for odd in range(2):
                            for b in range(G):
                                c = 4 * ((t * 2 + odd) * G + b)
                                r0 = t * 2 * P + odd
                                mm = MM(o[:, c:c + 4], HT[s][:, b, r0:r0 + 2 * P - 1:2], wcols0[:], True, True)
                    mm.then_inc(done, 1)

                def coefb0(it, s):
                    pe.wait_ge(sig["cexp"][s], count(it, 1, 0))
                    o, done = open_tile(it, "coefb0", s)
                    for k in range(T):
                        for t in range(HALF):
                            c = (t * 2 + k // HALF) * G
                            mm = MM(o[:, k * G:(k + 1) * G], adjn[:, t, k * P:(k + 1) * P].bitcast(F32),
                                    CE[s][:, c:c + G], t == 0, t == HALF - 1)
                    mm.then_inc(done, 1)

                def feat0(it, s):
                    o, done = open_tile(it, "feat0", s)
                    for t in range(T):
                        for b in range(G):
                            c = (t * G + b) * F
                            mm = MM(o[:, c:c + F], blk(s, b, t), Wo[:], True, True)
                    mm.then_inc(done, 1)

                def agg0(it, s):
                    pe.wait_ge(sig["lo"][s], count(it, len(LOS), LOS["0"]))
                    o, done = open_tile(it, "agg0", s, 0)
                    for t in range(HALF):
                        for side in range(2):
                            c = (t * 2 + side) * G * F
                            parts = [(k, m) for k in (2 * side, 2 * side + 1) for m in (HI, LO)]
                            for n, (k, m) in enumerate(parts):
                                mm = MM(o[:, c:c + G * F], maskT[:, k, t * P:(t + 1) * P],
                                        m[s][:, k * G:(k + 1) * G, :], n == 0, n == len(parts) - 1)
                    mm.then_inc(done, 1)
                    o, done = open_tile(it, "agg0", s, 1)
                    for t in range(T):
                        c = t * G * F
                        for b in range(G):
                            MM(o[:, c + b * F:c + (b + 1) * F], blk(s, b, t), Ws[:], b == 0, False)
                        for k in range(T):
                            w = empty0[:, k, :] if t < HALF else mask0b[:, k, (t - HALF) * P:(t - HALF + 1) * P]
                            for m in (HIB, LOB):
                                mm = MM(o[:, c:c + G * F], w, m[s][:, k * G:(k + 1) * G, :], False,
                                        k == T - 1 and m is LOB)
                    mm.then_inc(done, 1)

                def feat(it, name, s, w, bias, before):
                    turned(it, before, s)
                    for h in range(2):
                        o, done = open_tile(it, name, s, h)
                        o4 = o[:].rearrange("p (t b c) -> p t b c", t=2, b=G)
                        for tt in range(2):
                            if bias is not None:
                                MM(o4[:, tt, :, 0:WD], pick[:], bias[:], True, False)
                            for b in range(G):
                                mm = MM(o4[:, tt, b, 0:w.shape[1]], blk(s, b, 2 * h + tt), w,
                                        bias is None, True)
                        mm.then_inc(done, 1)

                def score(it, name, s, w):
                    o, done = open_tile(it, name, s)
                    for b in range(G):
                        mm = MM(o[:, b * N:(b + 1) * N], w[:], HT[s][:, b, :], True, True)
                    mm.then_inc(done, 1)

                def attend(it, name, s):
                    for b in range(G):
                        r, k = rings[name, s][b]
                        pe.wait_ge(p_full[r], count(it, RUSES, k))
                        o, done = open_tile(it, name, s, b)
                        for i in range(T):
                            for j in range(T):
                                mm = MM(o[:, i * 2 * P:i * 2 * P + F + 1], PT[r][:, j, i * P:(i + 1) * P],
                                        HE[s][:, j * G + b, 0:F + 1], j == 0, j == T - 1)
                        mm.then_inc(done, 1)

                def gin1(it, s):
                    pe.wait_ge(sig["lo"][s], count(it, len(LOS), LOS["1"]))
                    o, done = open_tile(it, "gin1", s)
                    for b in range(G):
                        for j in range(T):
                            for m in (HI, LO):
                                MM(o[:, b * N:(b + 1) * N], m[s][:, j * G + b, :], gin_hi[:, j, :],
                                   j == 0 and m is HI, False)
                            c = b * N + j * P
                            mm = MM(o[:, c:c + P], HI[s][:, j * G + b, :], gin_lo[:, j, :], False, j == T - 1)
                    mm.then_inc(done, 1)

                def mlp(it, name, s, w, bias, before):
                    turned(it, before, s)
                    o, done = open_tile(it, name, s)
                    for t in range(T):
                        if t % 2 == 0:
                            MM(o[:, t * G * F:(t + 2) * G * F], pick[:], bias[:], True, False)
                        for b in range(G):
                            c = (t * G + b) * F
                            mm = MM(o[:, c:c + F], blk(s, b, t), w[:], False, True)
                    mm.then_inc(done, 1)

                def agg3(it, s):
                    pe.wait_ge(sig["lo"][s], count(it, len(LOS), LOS["3"]))
                    o, done = open_tile(it, "agg3", s)
                    for t in range(T):
                        c = t * G * F
                        parts = [(k, w, m) for k in range(T) for w, m in ((a3_hi, HI), (a3_hi, LO), (a3_lo, HI))]
                        for n, (k, w, m) in enumerate(parts):
                            mm = MM(o[:, c:c + G * F], w[:, k, t * P:(t + 1) * P], m[s][:, k * G:(k + 1) * G, :],
                                    n == 0, n == len(parts) - 1)
                    mm.then_inc(done, 1)

                run = {
                    "coef0": coef0, "coefb0": coefb0, "feat0": feat0, "agg0": agg0, "gin1": gin1, "agg3": agg3,
                    "norm0": lambda it, s: turn_rows(it, "norm0", s),
                    "norm1": lambda it, s: turn_rows(it, "norm1", s),
                    "norm2": lambda it, s: turn_rows(it, "norm2", s),
                    "norm3": lambda it, s: turn_rows(it, "norm3", s),
                    "mlpb1": lambda it, s: turn_rows(it, "mlpb1", s),
                    "feat1": lambda it, s: feat(it, "feat1", s, feat1w[:], bias_p, "norm1"),
                    "feat2": lambda it, s: feat(it, "feat2", s, feat2w[:], None, "norm2"),
                    "feat3": lambda it, s: feat(it, "feat3", s, W3[:].rearrange("p a f -> p (a f)"), None, "norm3"),
                    "score1": lambda it, s: score(it, "score1", s, src1w),
                    "score2": lambda it, s: score(it, "score2", s, src2w),
                    "att1": lambda it, s: attend(it, "att1", s),
                    "att2": lambda it, s: attend(it, "att2", s),
                    "mlpa1": lambda it, s: mlp(it, "mlpa1", s, W1, bias_1, "gin1"),
                    "mlpc1": lambda it, s: mlp(it, "mlpc1", s, W2, bias_2, "mlpb1"),
                }
                with pe.Fori(0, ITERS) as it:
                    for name, s in ORDER:
                        if name in run:
                            run[name](it, s)

            @block.scalar
            def _(act):
                A = nc.scalar.activation
                order = [0]

                def filled(it, name, s, n=0):
                    slot, k = tiles[name, s][n]
                    act.wait_ge(full[slot], count(it, USES, k))
                    return ps[slot], taken[slot]

                def turn_rows(it, name, s):
                    o, read = filled(it, name, s)
                    v = o[:].rearrange("p (b n) -> p b n", b=G)
                    if name == "mlpb1":
                        A(HT[s][:], v, ACT.Relu, scale=mlp_g[:, 0:1], bias=mlp_b[:, 0:1]).then_inc(read, 1)
                    else:
                        A(HT[s][:], v, ACT.Relu).then_inc(read, 1)

                def coefb0(it, s):
                    act.wait_ge(sig["cdiff"][s], count(it, 1, 0))
                    A(CE[s][:], CF[s][:], ACT.Exp).then_inc(sig["cexp"][s], 1)

                def feat0(it, s):
                    act.wait_ge(sig["scaled"][s], count(it, 1, 0))
                    A(HI[s][:], SC[s][:], ACT.Copy).then_inc(sig["hi"][s], 1)
                    slot, k = tiles["feat0", s][0]
                    act.wait_ge(taken[slot], 1 + count(it, USES, k))
                    A(HIB[s][:], VA[s][:], ACT.Copy).then_inc(sig["hi"][s], 1)

                def feat(it, name, s):
                    for h in range(2):
                        o, read = filled(it, name, s, h)
                        v = o[:].rearrange("p (r c) -> p r c", c=2 * P)
                        A(HE[s][:, 4 * h:4 * h + 4, 0:F + 1], v[:, :, 0:F + 1], ACT.Copy).then_inc(read, 1)

                def score(it, name, s):
                    act.wait_ge(sig["ddiff"][s], count(it, 2, ATT[name[-1]]))
                    A(CE[s][:, 0:TG], CF[s][:, 0:TG], ACT.Exp)
                    A(CE[s][:, TG:2 * TG], CF[s][:, 0:TG], ACT.Exp, scale=0.2).then_inc(sig["dexp"][s], 1)
                    o, read = filled(it, name, s)
                    for b in range(G):
                        a = A(R[s][:, b, :], o[:, b * N:(b + 1) * N], ACT.Relu, scale=0.8, bias=MX[s][:, 4 + b:5 + b])
                    a.then_inc(read, 1)
                    slot, k = tiles[name, s][0]
                    act.wait_ge(taken[slot], 1 + count(it, USES, k))
                    A(R[s][:], R[s][:], ACT.Exp, scale=-1.0).then_inc(sig["r_ready"][s], 1)

                def attend(it, name, s):
                    for b in range(G):
                        o, read = filled(it, name, s, b)
                        r, _ = rings[name, s][b]
                        v = o[:].rearrange("p (t c) -> p t c", c=2 * P)
                        for h in range(2):
                            y = Y[s][:].rearrange("p (t b) c -> p t b c", b=G)[:, 2 * h:2 * h + 2, b, 0:F + 1]
                            A(y, v[:, 2 * h:2 * h + 2, 0:F + 1], ACT.Copy).then_inc((p_taken[r], read)[h], 1)

                def gat1(it, s):
                    act.wait_ge(sig["gated"][s], count(it, 2, 0))
                    A(HI[s][:], VA[s][:], ACT.Relu).then_inc(sig["hi"][s], 1)

                def gin1(it, s):
                    o, read = filled(it, "gin1", s)
                    A(HT[s][:], o[:].rearrange("p (b n) -> p b n", b=G), ACT.Copy).then_inc(read, 1)

                def mlpa1(it, s):
                    o, read = filled(it, "mlpa1", s)
                    A(Y[s][:, :, 0:F], o[:].rearrange("p (r f) -> p r f", f=F), ACT.Copy).then_inc(read, 1)

                def elu2(it, s):
                    act.wait_ge(sig["gated"][s], count(it, 2, 1))
                    A(SC[s][:], VA[s][:], ACT.Exp).then_inc(sig["eluexp"][s], 1)

                def feat3(it, s):
                    for h in range(2):
                        slot, k = tiles["feat3", s][h]
                        act.wait_ge(full[slot], count(it, USES, k))
                        v = ps[slot][:].rearrange("p (r c) -> p r c", c=2 * P)
                        A(HI[s][:, 4 * h:4 * h + 4, :], v[:, :, F:2 * F], ACT.Copy).then_inc(sig["hi"][s], 1)

                run = {
                    "coefb0": coefb0, "fsplit0": feat0, "gat1": gat1, "gin1": gin1, "mlpa1": mlpa1, "elu2": elu2,
                    "feat3": feat3,
                    "norm0": lambda it, s: turn_rows(it, "norm0", s),
                    "norm1": lambda it, s: turn_rows(it, "norm1", s),
                    "norm2": lambda it, s: turn_rows(it, "norm2", s),
                    "norm3": lambda it, s: turn_rows(it, "norm3", s),
                    "mlpb1": lambda it, s: turn_rows(it, "mlpb1", s),
                    "feat1": lambda it, s: feat(it, "feat1", s),
                    "feat2": lambda it, s: feat(it, "feat2", s),
                    "score1": lambda it, s: score(it, "score1", s),
                    "score2": lambda it, s: score(it, "score2", s),
                    "att1": lambda it, s: attend(it, "att1", s),
                    "att2": lambda it, s: attend(it, "att2", s),
                }
                with act.Fori(0, ITERS) as it:
                    for name, s in ORDER:
                        if name in run:
                            run[name](it, s)

            @block.gpsimd
            def _(pool):
                TT = nc.gpsimd.tensor_tensor

                def rstd(it, name, s):
                    pool.wait_ge(sig["var"][s], count(it, NLN, ln_at[name]))
                    TT(SM[s][:, S_RSTD, :], SM[s][:, S_VAR, :], minus_half[:], ALU.pow).then_inc(sig["rstd"][s], 1)

                def all_max(s, done):
                    TT(MX[s][:, 6:8], MX[s][:, 0:2], ones[:, 0:2], ALU.mult).then_inc(pool_order, 1)
                    pool.wait_ge(pool_order, 1)
                    nc.gpsimd.partition_all_reduce(MX[s][:, 2:4], MX[s][:, 6:8], P, RMAX).then_inc(done, 1)
                    pool.sem_clear(pool_order)

                def cmax(it, s):
                    pool.wait_ge(sig["cmax"][s], count(it, 1, 0))
                    all_max(s, sig["cmax_all"][s])

                def dmax(it, name, s):
                    pool.wait_ge(sig["dmax"][s], count(it, 2, ATT[name[-1]]))
                    all_max(s, sig["dmax_all"][s])

                def gat1(it, s):
                    pool.wait_ge(sig["normed"][s], count(it, len(NORMED), nd_at["gat1"]))
                    TT(VA[s][:], VA[s][:], repeat(gat_g[:], TG), ALU.mult).then_inc(pool_order, 1)
                    pool.wait_ge(pool_order, 1)
                    TT(VA[s][:], VA[s][:], repeat(gat_b[:], TG), ALU.add).then_inc(sig["gated"][s], 1)
                    pool.sem_clear(pool_order)

                def lift2(it, s):
                    pool.wait_ge(sig["r_ready"][s], count(it, 2, 1))
                    TT(R[s][:], R[s][:], repeat(rescue2[:], G), ALU.add).then_inc(sig["lifted"][s], 1)

                def norm2(it, s):
                    pool.wait_ge(sig["normed"][s], count(it, len(NORMED), nd_at["norm2"]))
                    TT(X[s][:], X[s][:], repeat(ones[:], TG), ALU.subtract).then_inc(sig["shifted"][s], 1)

                def elu2(it, s):
                    pool.wait_ge(sig["normed"][s], count(it, len(NORMED), nd_at["elu2"]))
                    TT(VA[s][:], VA[s][:], repeat(bias2[:], TG), ALU.add).then_inc(sig["gated"][s], 1)

                def norm3(it, s):
                    pool.wait_ge(sig["normed"][s], count(it, len(NORMED), nd_at["norm3"]))
                    TT(X[s][:], X[s][:], repeat(bias3[:], TG), ALU.add).then_inc(sig["shifted"][s], 1)

                run = {
                    "coef0": cmax, "lift2": lift2, "norm2": norm2, "norm3": norm3, "gat1": gat1, "elu2": elu2,
                    "feat1": lambda it, s: dmax(it, "feat1", s),
                    "feat2": lambda it, s: dmax(it, "feat2", s),
                    "stat0": lambda it, s: rstd(it, "norm0", s),
                    "stat1": lambda it, s: rstd(it, "norm1", s),
                    "stat2": lambda it, s: rstd(it, "norm2", s),
                    "stat3": lambda it, s: rstd(it, "norm3", s),
                    "gats1": lambda it, s: rstd(it, "gat1", s),
                    "mlps1": lambda it, s: rstd(it, "mlpb1", s),
                }
                with pool.Fori(0, ITERS) as it:
                    for name, s in ORDER:
                        if name in run:
                            run[name](it, s)

            @block.vector
            def _(dve):
                V = nc.vector
                order = [0]

                def link(ins):
                    order[0] += 1
                    ins.then_inc(dve_order, 1)
                    dve.wait_ge(dve_order, order[0])

                def filled(it, name, s, n=0):
                    slot, k = tiles[name, s][n]
                    dve.wait_ge(full[slot], count(it, USES, k))
                    return ps[slot], taken[slot]

                def read_by_act(it, name, s, n=0):
                    slot, k = tiles[name, s][n]
                    dve.wait_ge(taken[slot], 1 + count(it, USES, k))

                def stats(it, s, src, sums=None):
                    st, sm = ST[s], SM[s]
                    for n in range(TG):
                        a = V.bn_stats(st[:, n, :], src(n))
                    link(a)
                    V.tensor_tensor(sm[:, S_DIF, :], st[:, :, 1], st[:, :, 4], ALU.subtract)
                    V.tensor_tensor(sm[:, S_SUM, :], st[:, :, 1], st[:, :, 4], ALU.add)
                    if sums is not None:
                        V.tensor_scalar(sm[:, S_INV, :], sums, TINY, None, ALU.max)
                    link(V.tensor_tensor(sm[:, S_Q, :], st[:, :, 2], st[:, :, 5], ALU.add))
                    V.scalar_tensor_tensor(out=sm[:, S_DD, :], in0=sm[:, S_DIF, :], scalar=0.25,
                                           in1=sm[:, S_DIF, :], op0=ALU.mult, op1=ALU.mult)
                    V.tensor_scalar(sm[:, S_MEAN, :], sm[:, S_SUM, :], 0.5, None, ALU.mult)
                    if sums is not None:
                        V.reciprocal(sm[:, S_INV, :], sm[:, S_INV, :])
                    link(V.tensor_scalar(sm[:, S_Q, :], sm[:, S_Q, :], 1.0 / F, None, ALU.mult))
                    link(V.tensor_tensor(sm[:, S_VAR, :], sm[:, S_Q, :], sm[:, S_DD, :], ALU.add))
                    if sums is not None:
                        for _ in range(2):
                            link(V.tensor_tensor(sm[:, S_VAR, :], sm[:, S_VAR, :], sm[:, S_INV, :], ALU.mult))
                    V.tensor_scalar(sm[:, S_VAR, :], sm[:, S_VAR, :], LN_EPS, None, ALU.add).then_inc(
                        sig["var"][s], 1)

                def normalise(it, name, s, src, dst, sums=False):
                    sm = SM[s]
                    dve.wait_ge(sig["rstd"][s], count(it, NLN, ln_at[name]))
                    col = S_RSTD
                    if sums:
                        col = S_RS
                        link(V.tensor_tensor(sm[:, S_RS, :], sm[:, S_RSTD, :], sm[:, S_INV, :], ALU.mult))
                    for n in range(TG):
                        a = V.tensor_scalar(dst[s][:, n, :], src(n), sm[:, S_MEAN, n:n + 1], sm[:, col, n:n + 1],
                                            ALU.subtract, ALU.mult)
                    a.then_inc(sig["normed"][s], 1)

                def stat0(it, s):
                    dve.wait_ge(sig["x_loaded"][s], it * (16 * G) + 16 * G)
                    stats(it, s, lambda n: XL[s][:, n, :])

                def stat(it, s):
                    stats(it, s, lambda n: X[s][:, n, :])

                def coef0(it, s):
                    o, read = filled(it, "coef0", s)
                    V.tensor_copy(US[s][:], o[:, 0:4 * TG].rearrange("p (r c) -> p r c", c=4)).then_inc(read, 1)
                    read_by_act(it, "coef0", s)
                    u4 = US[s][:].rearrange("p (t o b) c -> p t o b c", t=HALF, o=2)
                    V.tensor_copy(CD[s][:, 0:TG], US[s][:, :, 0])
                    link(V.tensor_tensor(CD[s][:, TG:12].rearrange("p (t b) -> p t b", b=G), u4[:, :, 0, :, 1],
                                         u4[:, :, 1, :, 2], ALU.add))
                    link(V.scalar_tensor_tensor(out=CD[s][:], in0=CD[s][:], scalar=0.1, in1=CD[s][:],
                                                op0=ALU.mult, op1=ALU.max))
                    V.reduce_max(MX[s][:, 0:2], CD[s][:, 0:TG].rearrange("p (r b) -> p b r", b=G),
                                 AX_X).then_inc(sig["cmax"][s], 1)

                def coefm0(it, s):
                    dve.wait_ge(sig["cmax_all"][s], count(it, 1, 0))
                    m = MX[s][:, 2:4]
                    d = CD[s][:, TG:12].rearrange("p (t b) -> p t b", b=G)
                    mk = SM[s][:, S_A, 0:4].rearrange("p (t b) -> p t b", b=G)
                    V.tensor_tensor(CF[s][:, 0:TG].rearrange("p (r b) -> p r b", b=G),
                                    CD[s][:, 0:TG].rearrange("p (r b) -> p r b", b=G), repeat(m, 4), ALU.subtract)
                    link(V.tensor_tensor(mk, d, repeat(m, 2), ALU.max))
                    V.tensor_tensor(CF[s][:, 8:12].rearrange("p (t b) -> p t b", b=G), repeat(m, 2), mk, ALU.subtract)
                    V.tensor_tensor(CF[s][:, 12:16].rearrange("p (t b) -> p t b", b=G), d, mk,
                                    ALU.subtract).then_inc(sig["cdiff"][s], 1)

                def coefb0(it, s):
                    o, read = filled(it, "coefb0", s)
                    sm = SM[s]
                    a2, b2 = repeat(CE[s][:, 8:12], 2), repeat(CE[s][:, 12:16], 2)

                    def two(ap):
                        return ap.rearrange("p (h r) -> p h r", h=2)
                    V.tensor_tensor(two(sm[:, S_B, :]), two(low8[:]), b2, ALU.mult)
                    V.tensor_tensor(two(sm[:, S_Z, :]), two(o[:, 0:TG]), a2, ALU.mult).then_inc(read, 1)
                    read_by_act(it, "coefb0", s)
                    link(V.tensor_tensor(sm[:, S_Z, :], sm[:, S_Z, :], sm[:, S_B, :], ALU.add))
                    link(V.tensor_tensor(sm[:, S_Z, :], sm[:, S_Z, :], empty8[:], ALU.add))
                    link(V.tensor_scalar(sm[:, S_Z, :], sm[:, S_Z, :], TINY, None, ALU.max))
                    link(V.reciprocal(sm[:, S_Z, :], sm[:, S_Z, :]))
                    V.tensor_tensor(two(sm[:, S_A, :]), two(sm[:, S_Z, :]), a2, ALU.mult)
                    link(V.tensor_tensor(two(sm[:, S_B, :]), two(sm[:, S_Z, :]), b2, ALU.mult))
                    link(V.tensor_tensor(sm[:, S_B, :], sm[:, S_B, :], full8[:], ALU.mult))
                    link(V.tensor_tensor(sm[:, S_B, :], sm[:, S_B, :], share8[:], ALU.add))

                def feat0(it, s):
                    o, read = filled(it, "feat0", s)
                    v = o[:].rearrange("p (r f) -> p r f", f=F)
                    V.tensor_tensor(SC[s][:], v, bcast(SM[s][:, S_A, :], F), ALU.mult).then_inc(sig["scaled"][s], 1)
                    V.tensor_tensor(VA[s][:], v, bcast(SM[s][:, S_B, :], F), ALU.mult).then_inc(read, 1)
                    dve.wait_ge(sig["hi"][s], count(it, len(HIS), HIS["a0"]))
                    V.tensor_tensor(LO[s][:], SC[s][:], HI[s][:].bitcast(F32), ALU.subtract)
                    dve.wait_ge(sig["hi"][s], count(it, len(HIS), HIS["b0"]))
                    V.tensor_tensor(LOB[s][:], VA[s][:], HIB[s][:].bitcast(F32), ALU.subtract).then_inc(
                        sig["lo"][s], 1)

                def agg0(it, s):
                    og, read_g = filled(it, "agg0", s, 0)
                    V.tensor_tensor(SC[s][:], og[:].rearrange("p (r f) -> p r f", f=F), bcast(CE[s][:, 0:TG], F),
                                    ALU.mult).then_inc(read_g, 1)
                    os_, read_s = filled(it, "agg0", s, 1)
                    dve.wait_ge(sig["stored"][s], it * (16 * G) + 16)
                    V.tensor_tensor(X[s][:], XL[s][:], os_[:].rearrange("p (r f) -> p r f", f=F),
                                    ALU.add).then_inc(read_s, 1)
                    sc = SC[s][:].rearrange("p (t h b) f -> p t h (b f)", t=HALF, h=2)
                    xt = X[s][:, 0:HALF * G, :].rearrange("p (t b) f -> p t (b f)", b=G)
                    read_by_act(it, "agg0", s, 0)
                    read_by_act(it, "agg0", s, 1)
                    link(V.tensor_tensor(xt, xt, sc[:, :, 0, :], ALU.add))
                    V.tensor_tensor(xt, xt, sc[:, :, 1, :], ALU.add).then_inc(sig["raw_free"][s], 1)
                    dve.wait_ge(sig["raw_free"][s], count(it, 1, 0))

                def dmax(it, name, s):
                    read_by_act(it, name, s, 0)
                    read_by_act(it, name, s, 1)
                    V.reduce_max(MX[s][:, 0:2], HE[s][:].rearrange("p (t b) c -> p b t c", b=G)[:, :, :, F],
                                 AX_X).then_inc(sig["dmax"][s], 1)

                def ddiff(it, name, s):
                    dve.wait_ge(sig["dmax_all"][s], count(it, 2, ATT[name[-1]]))
                    V.tensor_tensor(CF[s][:, 0:TG].rearrange("p (t b) -> p t b", b=G),
                                    HE[s][:].rearrange("p (t b) c -> p t b c", b=G)[:, :, :, F],
                                    repeat(MX[s][:, 2:4], T), ALU.subtract)
                    if name[-1] == "1":
                        link(V.tensor_scalar(MX[s][:, 4:6], MX[s][:, 2:4], const1[:, 0:1], 0.8, ALU.add, ALU.mult))
                    else:
                        link(V.tensor_scalar(MX[s][:, 4:6], MX[s][:, 2:4], 0.8, None, ALU.mult))
                    V.memset(HE[s][:, :, F:F + 1], 1.0).then_inc(sig["ddiff"][s], 1)

                def attend(it, name, s):
                    n = ATT[name[-1]]
                    dve.wait_ge(sig["dexp"][s], count(it, 2, n))
                    if n == 0:
                        dve.wait_ge(sig["r_ready"][s], count(it, 2, n))
                    else:
                        dve.wait_ge(sig["lifted"][s], count(it, 1, 0))
                    mask = (maskT[:].bitcast(F32), mask2[:])[n]
                    for b in range(G):
                        r, k = rings[name, s][b]
                        dve.wait_ge(p_taken[r], it * RUSES + k + 1)
                        for j in range(T):
                            c = j * G + b
                            a = V.tensor_scalar(PT[r][:, j, :], R[s][:, b, :], CE[s][:, TG + c:TG + c + 1],
                                                CE[s][:, c:c + 1], ALU.mult, ALU.max)
                        link(a)
                        V.tensor_tensor(PT[r][:], PT[r][:], mask, ALU.min).then_inc(p_full[r], 1)

                def gats1(it, s):
                    for b in range(G):
                        read_by_act(it, "att1", s, b)
                    stats(it, s, lambda n: Y[s][:, n, 0:F], Y[s][:, :, F])

                def gat1(it, s):
                    normalise(it, "gat1", s, lambda n: Y[s][:, n, 0:F], VA, True)

                def gatl1(it, s):
                    dve.wait_ge(sig["hi"][s], count(it, len(HIS), HIS["1"]))
                    V.scalar_tensor_tensor(out=LO[s][:], in0=VA[s][:], scalar=0.0, in1=HI[s][:].bitcast(F32),
                                           op0=ALU.max, op1=ALU.subtract).then_inc(sig["lo"][s], 1)

                def mlps1(it, s):
                    read_by_act(it, "mlpa1", s)
                    stats(it, s, lambda n: Y[s][:, n, 0:F])

                def mlpc1(it, s):
                    o, read = filled(it, "mlpc1", s)
                    V.scalar_tensor_tensor(out=SC[s][:], in0=VA[s][:], scalar=0.0,
                                           in1=o[:].rearrange("p (r f) -> p r f", f=F), op0=ALU.max,
                                           op1=ALU.add).then_inc(read, 1)
                    read_by_act(it, "mlpc1", s)
                    link(V.scalar_tensor_tensor(out=X[s][:], in0=SC[s][:], scalar=0.0, in1=X[s][:], op0=ALU.max,
                                                op1=ALU.add))

                def elud2(it, s):
                    for b in range(G):
                        read_by_act(it, "att2", s, b)
                    link(V.tensor_scalar(SM[s][:, S_INV, :], Y[s][:, :, F], TINY, None, ALU.max))
                    link(V.reciprocal(SM[s][:, S_INV, :], SM[s][:, S_INV, :]))
                    for n in range(TG):
                        a = V.tensor_scalar(VA[s][:, n, :], Y[s][:, n, 0:F], SM[s][:, S_INV, n:n + 1], None, ALU.mult)
                    a.then_inc(sig["normed"][s], 1)

                def elu2(it, s):
                    dve.wait_ge(sig["eluexp"][s], count(it, 1, 0))
                    dve.wait_ge(sig["shifted"][s], count(it, 2, 0))
                    link(V.scalar_tensor_tensor(out=SC[s][:], in0=SC[s][:], scalar=1.0, in1=X[s][:], op0=ALU.min,
                                                op1=ALU.add))
                    link(V.scalar_tensor_tensor(out=X[s][:], in0=VA[s][:], scalar=0.0, in1=SC[s][:], op0=ALU.max,
                                                op1=ALU.add))

                def feat3(it, s):
                    dve.wait_ge(sig["shifted"][s], count(it, 2, 1))
                    for h in range(2):
                        slot, k = tiles["feat3", s][h]
                        dve.wait_ge(sig["hi"][s], count(it, len(HIS), HIS["3a"] + h))
                        v = ps[slot][:].rearrange("p (r c) -> p r c", c=2 * P)
                        a = V.tensor_tensor(LO[s][:, 4 * h:4 * h + 4, :], v[:, :, F:2 * F],
                                            HI[s][:, 4 * h:4 * h + 4, :].bitcast(F32), ALU.subtract)
                        if h == 1:
                            a.then_inc(sig["lo"][s], 1)
                        for tt in range(2):
                            t = 2 * h + tt
                            xt = X[s][:, t * G:(t + 1) * G, :]
                            a = V.scalar_tensor_tensor(out=xt, in0=v[:, tt * G:(tt + 1) * G, 0:F],
                                                       scalar=diag3[:, t:t + 1], in1=xt, op0=ALU.mult, op1=ALU.add)
                        a.then_inc(taken[slot], 1)

                def agg3(it, s):
                    for h in range(2):
                        read_by_act(it, "feat3", s, h)
                    o, read = filled(it, "agg3", s)
                    V.tensor_tensor(X[s][:], X[s][:], o[:].rearrange("p (r f) -> p r f", f=F),
                                    ALU.add).then_inc(read, 1)

                def from_x(s):
                    return lambda n: X[s][:, n, :]

                run = {
                    "stat0": stat0, "stat1": stat, "stat2": stat, "stat3": stat, "coef0": coef0, "coefm0": coefm0,
                    "coefb0": coefb0, "fsplit0": feat0, "agg0": agg0, "gats1": gats1, "gat1": gat1, "gatl1": gatl1,
                    "mlps1": mlps1, "mlpc1": mlpc1, "elud2": elud2, "elu2": elu2, "feat3": feat3, "agg3": agg3,
                    "norm0": lambda it, s: normalise(it, "norm0", s, lambda n: XL[s][:, n, :], XN),
                    "norm1": lambda it, s: normalise(it, "norm1", s, from_x(s), XN),
                    "norm2": lambda it, s: normalise(it, "norm2", s, from_x(s), XN),
                    "norm3": lambda it, s: normalise(it, "norm3", s, from_x(s), XN),
                    "mlpb1": lambda it, s: normalise(it, "mlpb1", s, lambda n: Y[s][:, n, 0:F], XN),
                    "feat1": lambda it, s: dmax(it, "feat1", s),
                    "feat2": lambda it, s: dmax(it, "feat2", s),
                    "score1": lambda it, s: ddiff(it, "score1", s),
                    "score2": lambda it, s: ddiff(it, "score2", s),
                    "att1": lambda it, s: attend(it, "att1", s),
                    "att2": lambda it, s: attend(it, "att2", s),
                }
                with dve.Fori(0, ITERS) as it:
                    order[0] = 0
                    for name, s in ORDER:
                        if name in run:
                            run[name](it, s)
                    dve.sem_clear(dve_order)


_INS = ["x", "adj", "L0_gnn_others_weight", "L0_gnn_self_weight", "L0_gnn_att_weight", "L1_gnn_Wp", "L1_gnn_bp",
        "L1_gnn_a_src", "L1_gnn_a_dst", "L1_gnn_gat_g", "L1_gnn_gat_b", "L1_gnn_eps", "L1_gnn_W1", "L1_gnn_b1",
        "L1_gnn_mlp_g", "L1_gnn_mlp_b", "L1_gnn_W2", "L1_gnn_b2", "L2_gnn_W", "L2_gnn_a", "L2_gnn_bias",
        "L3_gnn_W", "L3_gnn_e", "L3_gnn_bias"]
_OUTS = [((32, 512, 128), "float32")]


def kernel(**inputs):
    import numpy as _np
    import concourse.bacc as _bacc
    from concourse import mybir as _mybir
    from concourse.bass_utils import run_bass_kernel_spmd as _run

    nc = _bacc.Bacc("TRN2", target_bir_lowering=False, num_devices=1)
    arrays, args = {}, []
    for name in _INS:
        a = _np.ascontiguousarray(inputs[name])
        arrays[f"in_{name}_dram"] = a
        args.append(nc.dram_tensor(f"in_{name}_dram", a.shape, _mybir.dt.from_np(a.dtype), kind="ExternalInput").ap())
    for i, (shape, dtype) in enumerate(_OUTS):
        dt = _mybir.dt.from_np(_np.dtype(dtype))
        args.append(nc.dram_tensor(f"out_{i}_dram", shape, dt, kind="ExternalOutput").ap())
    gnn_kernel(nc, *args)
    r = _run(nc, [arrays], core_ids=[0])
    got = tuple(r.results[0][f"out_{i}_dram"] for i in range(len(_OUTS)))
    return got[0]
```

```python
from contextlib import ExitStack

import concourse.bass as bass
from concourse import mybir

P = 128
ALU = mybir.AluOpType
ACT = mybir.ActivationFunctionType
F32 = mybir.dt.float32
F32R = mybir.dt.float32r
I32 = mybir.dt.int32
AX_X = mybir.AxisListType.X
RMAX = bass.bass_isa.ReduceOp.max

NS = 3
G = 2
SLOTS = 4
RING = 2
LN_EPS = 1e-5
NEG = -9000000000000000.0
TINY = 1e-30
HUGE = 1e30

WINDOW = 70.05
PLAN = [
    ("load", 0, {"sp": -23.2}),
    ("stat0", 0, {"dve": 0, "pool": 2.53}),
    ("norm0", 1, {"dve": 10.86, "pe": 13.74, "act": 15.62}),
    ("coef0", 1, {"pe": 16.7, "dve": 17.33, "pool": 18.06}),
    ("feat0", 1, {"pe": 21.04}),
    ("coefm0", 0, {"dve": 19.53}),
    ("coefb0", 1, {"act": 20.16, "pe": 20.54, "dve": 26.53}),
    ("split0", 0, {"dve": 28.78, "act": 31.57}),
    ("low0", 0, {"dve": 33.6, "pool": 33.6}),
    ("agg0", 1, {"pe": 36.04, "dve": 39.5}),
    ("self0", 1, {"pe": 37.74, "dve": 44.07}),
    ("stat1", 0, {"dve": 46.72, "pool": 49.25}),
    ("norm1", 1, {"dve": 51.52, "pe": 53.05, "act": 54.93}),
    ("feat1", 2, {"pe": 59.91, "act": 62.5, "dve": 64.79, "pool": 64.8}),
    ("score1", 0, {"dve": 65.9, "act": 66.53}),
    ("turn1", 1, {"dve": 66.91, "pe": 67.57, "act": 67.9}),
    ("spread1", 1, {"pe": 68.28, "act": 69.36}),
    ("att1a", 1, {"act": 70.31, "dve": 72.74, "pe": 75.69}),
    ("att1b", 1, {"act": 73.56, "dve": 75.99, "pe": 79.64}),
    ("collect1a", 0, {"act": 80.38}),
    ("collect1b", 0, {"act": 83.72}),
    ("gats1", 0, {"dve": 84.45, "pool": 88.81}),
    ("gain1", 0, {"dve": 87.98}),
    ("gat1", 0, {"dve": 94.2, "act": 97.09}),
    ("gatl1", 0, {"dve": 97.68}),
    ("gin1", 1, {"pe": 100.89, "act": 106.22}),
    ("mlpa1", 1, {"pe": 113.99, "act": 116.27}),
    ("mlps1", 0, {"dve": 119.17, "pool": 121.7}),
    ("mlpb1", 1, {"dve": 123.53, "pe": 124.85, "act": 126.73}),
    ("mlpc1", 1, {"pe": 127.81, "dve": 130.09}),
    ("stat2", 0, {"dve": 132.44, "pool": 135.82}),
    ("norm2", 1, {"dve": 139, "pe": 140.23, "act": 142.66, "pool": 144.33}),
    ("feat2", 2, {"pe": 143.74, "act": 145.91, "dve": 148.44, "pool": 148.72}),
    ("score2", 0, {"dve": 149.55, "act": 150.18}),
    ("turn2", 1, {"dve": 150.56, "pe": 153.64, "act": 154.37}),
    ("spread2", 1, {"pe": 155.59, "act": 156.67}),
    ("att2a", 1, {"act": 157.62, "dve": 160.13, "pe": 163.04}),
    ("att2b", 1, {"act": 160.51, "dve": 164.23, "pe": 166.99}),
    ("collect2a", 0, {"act": 167.12}),
    ("collect2b", 0, {"act": 171.07}),
    ("elud2", 0, {"dve": 171.8}),
    ("elu2", 0, {"act": 173.68, "dve": 174.9}),
    ("stat3", 0, {"dve": 177.2, "pool": 179.73}),
    ("norm3", 1, {"dve": 181.56, "pool": 182.79, "pe": 186.19, "act": 188.07}),
    ("feat3", 2, {"pe": 189.15, "act": 193.28, "dve": 194.68}),
    ("agg3", 1, {"pe": 202.47, "dve": 207.8}),
    ("store", 0, {"sp": 209.18}),
]


def bcast(ap, n):
    return ap.unsqueeze(2).to_broadcast([ap.shape[0], ap.shape[1], n])


def repeat(ap, n):
    return ap.unsqueeze(1).to_broadcast([ap.shape[0], n, ap.shape[1]])


def gnn_kernel(nc, x, adj, Wo_d, Ws_d, att0_d, Wp_d, bp_d, asrc_d, adst_d, gatg_d, gatb_d, eps_d, W1_d, b1_d,
               mlpg_d, mlpb_d, W2_d, b2_d, Wq_d, att2_d, bias2_d, W3_d, e_d, bias3_d, out):
    B, N, F = x.shape
    T = N // P
    TG = T * G
    HALF = T // 2
    WD = F + 2
    GROUPS = B // G
    NE = e_d.shape[1]
    MB = NE // P
    assert F == P and G == 2 and T == 4 and B % G == 0 and TG * F == 1024

    ctx = ExitStack()
    with ctx:
        def sb(name, shape, dt=F32, stack=ctx):
            return stack.enter_context(nc.sbuf_tensor(name, shape, dt))

        def sem(name):
            return ctx.enter_context(nc.semaphore(name))

        ps = [ctx.enter_context(nc.psum_tensor(f"ps{i}", [P, 1024], F32)) for i in range(SLOTS)]

        ident = sb("ident", [P, P])
        ones = sb("ones", [P, P])
        minus_half = sb("minus_half", [P, TG])
        adj_top = sb("adj_top", [P, HALF, N])
        maskT = sb("maskT", [P, T, N], F32R)
        mask0b = sb("mask0b", [P, T, N // 2], F32R)
        empty0 = sb("empty0", [P, T, P], F32R)
        mask2 = sb("mask2", [P, T, N])
        rescue8 = sb("rescue8", [P, TG])
        both8 = sb("both8", [P, TG, P], F32R)
        gin_hi = sb("gin_hi", [P, T, N], F32R)
        gin_lo = sb("gin_lo", [P, T, P], F32R)
        a3_hi = sb("a3_hi", [P, T, N], F32R)
        a3_lo = sb("a3_lo", [P, T, N], F32R)
        diag3 = sb("diag3", [P, T])
        Wo, Ws, W1, W2 = (sb(n, [P, F]) for n in ("Wo", "Ws", "W1", "W2"))
        W3 = sb("W3", [P, 2, F])
        wcols0 = sb("wcols0", [P, 4])
        feat1w = sb("feat1w", [P, WD])
        feat2w = sb("feat2w", [P, WD])
        const1 = sb("const1", [P, 1])
        pick = sb("pick", [P, P], F32R)
        bias_p = sb("bias_p", [P, WD], F32R)
        bias_1 = sb("bias_1", [P, F], F32R)
        bias_2 = sb("bias_2", [P, F], F32R)
        gat_g, gat_b, bias2, bias3 = (sb(n, [P, F]) for n in ("gat_g", "gat_b", "bias2", "bias3"))
        mlp_g, mlp_b = sb("mlp_g", [P, 1]), sb("mlp_b", [P, 1])
        low8 = sb("low8", [P, TG])
        empty8 = sb("empty8", [P, TG])
        full8 = sb("full8", [P, TG])
        share8 = sb("share8", [P, TG])

        loaded = sem("loaded")
        POOL_SETUP = 9
        made = {n: sem("made_" + n) for n in (
            "pool", "adjn", "maskT", "turn", "WT_ps", "WT", "rowtot", "bprep", "wvec", "rank_ps", "rank", "counts",
            "off", "row_of", "offm", "edges_ps", "edge_rows", "at", "cover", "values", "left3", "nmax", "exp3",
            "soft3", "turn3", "a3_hi", "gin_hi", "cast_hi")}
        dve_order = sem("dve_order")
        act_order = sem("act_order")
        pool_order = sem("pool_order")

        order = {e: sorted((when[e] % WINDOW, int(when[e] // WINDOW), name) for name, _, when in PLAN if e in when)
                 for e in ("pe", "act", "pool", "dve", "sp")}
        parts = {(name, e): int(when[e] // WINDOW) for name, _, when in PLAN for e in when}
        tiles_of = {name: n for name, n, _ in PLAN}
        LOOP_FIRST = max(parts.values())
        LOOPS = (GROUPS - 1 - LOOP_FIRST) // NS
        LAST = GROUPS + LOOP_FIRST

        tile_at, mat_at = {}, {}
        tiles = mats = 0
        for _, _, name in order["pe"]:
            tile_at[name] = tiles
            tiles += tiles_of[name]
        for _, _, name in order["act"]:
            if name.startswith("att"):
                mat_at[name] = mats
                mats += 1
        assert tiles % SLOTS == 0 and mats % RING == 0

        class Step:

            def __init__(self, name, w, part, it):
                self.name, self.w, self.part, self.it = name, w, part, it
                self.s = (w - part) % NS
                self.g = self.linear(1, (w - part) // NS)
                self.group = w - part if it is None else None

            def linear(self, per_loop, n):
                return n if self.it is None else self.it * per_loop + n

            def all_groups(self, per_group, n):
                return self.linear(NS * per_group, (self.w - self.part) * per_group + n)

            def ring(self, used, n, size):
                return n % size, self.linear(NS * used // size, n // size)

            def tile(self, name, n=0):
                w = self.w - self.part + parts[name, "pe"]
                return self.ring(tiles, w * tiles + tile_at[name] + n, SLOTS)

            def matrix(self, name):
                w = self.w - self.part + parts[name, "act"]
                return self.ring(mats, w * mats + mat_at[name], RING)

        def walk(core, e, run, skip=None, end_pass=None):
            def window(w, it=None):
                for _, part, name in order[e]:
                    u = Step(name, w, part, it)
                    if it is not None or 0 <= w - part < GROUPS:
                        run[name](u, u.s)
                    elif skip is not None and w >= 0:
                        skip(u)

            for w in range(-1, LOOP_FIRST):
                window(w)
            if end_pass is not None:
                end_pass()
            with core.Fori(0, LOOPS) as it:
                for w in range(LOOP_FIRST, LOOP_FIRST + NS):
                    window(w, it)
                if end_pass is not None:
                    end_pass()
            for w in range(LOOP_FIRST + NS * LOOPS, LAST):
                window(w)


        def count(it, per_group, n):
            return it * per_group + (n + 1)

        full = [sem(f"psum_full{i}") for i in range(SLOTS)]
        taken = [sem(f"psum_taken{i}") for i in range(SLOTS)]
        p_full = [sem(f"matrix_full{i}") for i in range(RING)]
        p_taken = [sem(f"matrix_taken{i}") for i in range(RING)]
        sig = {n: [sem(f"{n}_{s}") for s in range(NS)] for n in (
            "result", "stored", "var", "rstd", "normed", "cmax", "cmax_all", "cdiff", "cexp",
            "scaled", "hi", "lo", "lo_below", "dmax", "dmax_all", "ddiff", "dexp", "r_split", "raised", "gated",
            "eluexp", "shifted")}
        x_loaded = sem("x_loaded")
        raw_free = sem("raw_free")

        RT = [sb(f"RT{s}", [P, P], F32R) for s in range(NS)]

        with ExitStack() as sc:
            adj_raw = sb("adj_raw", [P, T, N], F32, sc)
            adjn = sb("adjn", [P, T, N], F32R, sc)
            upper = sb("upper", [P, T, N], F32R, sc)
            strict = sb("strict", [P, T, N], F32, sc)
            rank = sb("rank", [P, T, N], F32R, sc)
            row_of = sb("row_of", [P, MB, N], F32, sc)
            row_ofT = sb("row_ofT", [P, T, NE], F32R, sc)
            at = sb("at", [P, MB, N], F32, sc)
            e_at = sb("e_at", [P, MB, N], F32, sc)
            v3 = sb("v3", [P, T, N], F32, sc)
            work = sb("work", [P, T, N], F32, sc)
            WoT, WpT, WqT = (sb(n, [P, F], F32, sc) for n in ("WoT", "WpT", "WqT"))
            bprep = sb("bprep", [P, P], F32, sc)
            rowtot_b = sb("rowtot_b", [P, N], F32, sc)
            norow = sb("norow", [P, N], F32, sc)
            two8 = sb("two8", [P, TG], F32, sc)
            off_b = sb("off_b", [P, N], F32, sc)
            cntrep = sb("cntrep", [P, T, P], F32, sc)
            att0, asd, att2 = (sb(n, [P, 2], F32, sc) for n in ("att0", "asd", "att2"))
            bpcol, epscol, e255 = (sb(n, [P, 1], F32, sc) for n in ("bpcol", "epscol", "e255"))
            e_col = sb("e_col", [P, MB], F32, sc)
            brow = sb("brow", [P, 3, F], F32, sc)
            bhi = sb("bhi", [P, 3, F], F32R, sc)
            blo = sb("blo", [P, 3, F], F32R, sc)
            m_int = sb("m_int", [P, NE], I32, sc)
            mc_int = sb("mc_int", [P, MB], I32, sc)
            m_row = sb("m_row", [P, NE], F32, sc)
            m_col = sb("m_col", [P, MB], F32, sc)
            cnt_row = sb("cnt_row", [P, T], F32, sc)
            off_col = sb("off_col", [P, T], F32, sc)
            end_col = sb("end_col", [P, T], F32, sc)
            m_loc = sb("m_loc", [P, MB], F32, sc)
            cnt_all = sb("cnt_all", [P, T], F32, sc)
            cnt_low = sb("cnt_low", [P, T], F32, sc)
            empty4 = sb("empty4", [P, T], F32, sc)
            asum = sb("asum", [P, 1], F32, sc)
            epsd = sb("epsd", [P, P], F32, sc)
            diagv = sb("diagv", [P, T, P], F32, sc)
            small = sb("small", [P, 8], F32, sc)
            rmax = sb("rmax", [P, T], F32, sc)
            rsum = sb("rsum", [P, T], F32, sc)
            rinv = sb("rinv", [P, T], F32, sc)
            wv = sb("wv", [P, 8], F32, sc)

            LOADS = [(adj_raw[:], adj.rearrange("(t p) j -> p t j", p=P)),
                     (Wo[:], Wo_d), (Ws[:], Ws_d), (feat1w[:, 0:F], Wp_d), (W1[:], W1_d), (W2[:], W2_d), (feat2w[:, 0:F], Wq_d),
                     (W3[:], W3_d.rearrange("k f g -> f k g")),
                     (att0[:, 0:1], att0_d[0:P, :]), (att0[:, 1:2], att0_d[P:2 * P, :]),
                     (att2[:, 0:1], att2_d[0:P, :]), (att2[:, 1:2], att2_d[P:2 * P, :]),
                     (asd[:, 0:1], asrc_d.rearrange("(p o) -> p o", o=1)),
                     (asd[:, 1:2], adst_d.rearrange("(p o) -> p o", o=1)),
                     (bpcol[:], bp_d.rearrange("(p o) -> p o", o=1)),
                     (mlp_g[:], mlpg_d.rearrange("(p o) -> p o", o=1)),
                     (mlp_b[:], mlpb_d.rearrange("(p o) -> p o", o=1)),
                     (brow[:, 0, :], bp_d.partition_broadcast(P)),
                     (brow[:, 1, :], b1_d.partition_broadcast(P)),
                     (brow[:, 2, :], b2_d.partition_broadcast(P)),
                     (gat_g[:], gatg_d.partition_broadcast(P)), (gat_b[:], gatb_d.partition_broadcast(P)),
                     (bias2[:], bias2_d.partition_broadcast(P)), (bias3[:], bias3_d.partition_broadcast(P)),
                     (epscol[:], eps_d.partition_broadcast(P)),
                     (e255[:], e_d[0, NE - 1:NE].partition_broadcast(P)),
                     *[(e_col[:, m:m + 1], e_d[0, m * P:(m + 1) * P].rearrange("(p o) -> p o", o=1))
                       for m in range(MB)]]

            with nc.Block() as block:
                @block.sync
                def _(sp):
                    for dst, src in LOADS:
                        sp.dma_start(dst, src).then_inc(loaded, 16)
                    for s in taken + p_taken:
                        sp.sem_inc(s, 1)
                    for s in sig["stored"]:
                        sp.sem_inc(s, 16)
                    sp.wait_ge(loaded, 16 * len(LOADS))

                @block.gpsimd
                def _(pool):
                    nc.gpsimd.memset(ident[:], 0.0).then_inc(made["pool"], 1)
                    nc.gpsimd.memset(ones[:], 1.0).then_inc(made["pool"], 1)
                    nc.gpsimd.memset(work[:], 1.0).then_inc(made["pool"], 1)
                    nc.gpsimd.memset(minus_half[:], -0.5).then_inc(made["pool"], 1)
                    pool.wait_ge(made["pool"], 4)
                    nc.gpsimd.affine_select(out=ident[:], in_=ident[:], compare_op=ALU.not_equal, fill=1.0, base=0,
                                            pattern=[[-1, P]], channel_multiplier=1).then_inc(made["pool"], 1)
                    nc.gpsimd.affine_select(out=upper[:], in_=work[:], compare_op=ALU.is_ge, fill=0.0, base=0,
                                            pattern=[[-P, T], [1, N]], channel_multiplier=-1).then_inc(made["pool"], 1)
                    nc.gpsimd.affine_select(out=strict[:], in_=work[:], compare_op=ALU.is_gt, fill=0.0, base=0,
                                            pattern=[[-P, T], [1, N]], channel_multiplier=-1).then_inc(made["pool"], 1)
                    nc.gpsimd.iota(m_int[:], [[1, NE]], base=0, channel_multiplier=0).then_inc(made["pool"], 1)
                    nc.gpsimd.iota(mc_int[:], [[P, MB]], base=0, channel_multiplier=1).then_inc(made["pool"], 1)

                @block.tensor
                def _(pe):
                    T_, MM = nc.tensor.transpose, nc.tensor.matmul
                    pe.wait_ge(made["adjn"], 1)
                    pe.wait_ge(made["pool"], POOL_SETUP)
                    for j in range(T):
                        for i in range(T):
                            o = (j % 2) * N + i * P
                            mm = T_(ps[j // 2][:, o:o + P], adjn[:, i, j * P:(j + 1) * P].bitcast(F32), ident[:])
                    mm.then_inc(made["turn"], 1)
                    pe.wait_ge(loaded, 16 * len(LOADS))
                    for n, w in enumerate((Wo, feat1w, feat2w)):
                        mm = T_(ps[2][:, n * P:(n + 1) * P], w[:, 0:F], ident[:])
                    mm.then_inc(made["WT_ps"], 1)
                    pe.wait_ge(made["maskT"], 1)
                    for j in range(T):
                        mm = MM(ps[3][:, 0:N], ones[:], maskT[:, j, :].bitcast(F32), start=(j == 0), stop=(j == T - 1))
                    mm.then_inc(made["rowtot"], 1)
                    pe.wait_ge(made["bprep"], 1)
                    pe.wait_ge(made["WT"], 1)
                    MM(ps[2][:, 512:514], WoT[:], att0[:], start=True, stop=True)
                    MM(ps[2][:, 514:516], WpT[:], asd[:], start=True, stop=True)
                    MM(ps[2][:, 516:518], WqT[:], att2[:], start=True, stop=True)
                    MM(ps[2][:, 518:519], bprep[:], asum[:], start=True, stop=True).then_inc(made["wvec"], 1)
                    for i in range(T):
                        for j in range(T):
                            mm = MM(ps[i // 2][:, (i % 2) * N:(i % 2) * N + N], maskT[:, j, i * P:(i + 1) * P],
                                    upper[:, j, :], start=(j == 0), stop=(j == T - 1))
                    mm.then_inc(made["rank_ps"], 1)
                    pe.wait_ge(made["counts"], 1)
                    for i in range(T):
                        for k in range(T):
                            MM(ps[2][:, 16 + i:17 + i], strict[:, k, i * P:(i + 1) * P], cnt_row[:, k:k + 1],
                               start=(k == 0), stop=(k == T - 1))
                    for k in range(T):
                        mm = MM(ps[3][:, N:2 * N], cntrep[:, k, :], strict[:, k, :], start=(k == 0), stop=(k == T - 1))
                    mm.then_inc(made["off"], 1)
                    pe.wait_ge(made["row_of"], 1)
                    for m in range(MB):
                        for i in range(T):
                            mm = MM(ps[2][:, 32 + m:33 + m], row_ofT[:, i, m * P:(m + 1) * P].bitcast(F32),
                                    off_col[:, i:i + 1], start=(i == 0), stop=(i == T - 1))
                    mm.then_inc(made["offm"], 1)
                    pe.wait_ge(made["rank"], 1)
                    for t, src in enumerate((adjn, rank)):
                        for m in range(MB):
                            for i in range(T):
                                mm = MM(ps[t][:, m * N:(m + 1) * N], row_ofT[:, i, m * P:(m + 1) * P], src[:, i, :],
                                        start=(i == 0), stop=(i == T - 1))
                    mm.then_inc(made["edges_ps"], 1)
                    pe.wait_ge(made["at"], 1)
                    for src, tile0, name in ((at, 2, "cover"), (e_at, 0, "values")):
                        for i in range(T):
                            for m in range(MB):
                                mm = MM(ps[tile0 + i // 2][:, (i % 2) * N:(i % 2) * N + N],
                                        row_of[:, m, i * P:(i + 1) * P], src[:, m, :],
                                        start=(m == 0), stop=(m == MB - 1))
                        mm.then_inc(made[name], 1)
                    pe.wait_ge(made["soft3"], 1)
                    for j in range(T):
                        for i in range(T):
                            o = (j % 2) * N + i * P
                            mm = T_(ps[j // 2][:, o:o + P], v3[:, i, j * P:(j + 1) * P], ident[:])
                    mm.then_inc(made["turn3"], 1)

                @block.scalar
                def _(act):
                    A = nc.scalar.activation
                    act.wait_ge(made["turn"], 1)
                    A(maskT[:, 0:2, :], ps[0][:].rearrange("p (a n) -> p a n", a=2), ACT.Copy)
                    A(maskT[:, 2:4, :], ps[1][:].rearrange("p (a n) -> p a n", a=2), ACT.Copy).then_inc(made["maskT"], 1)
                    act.wait_ge(made["WT_ps"], 1)
                    for n, w in enumerate((WoT, WpT, WqT)):
                        a = A(w[:], ps[2][:, n * P:(n + 1) * P], ACT.Copy)
                    a.then_inc(made["WT"], 1)
                    act.wait_ge(made["maskT"], 1)
                    A(gin_hi[:], maskT[:].bitcast(F32), ACT.Copy).then_inc(made["gin_hi"], 1)
                    act.wait_ge(made["rank_ps"], 1)
                    A(rank[:, 0:2, :], ps[0][:].rearrange("p (a n) -> p a n", a=2), ACT.Copy)
                    A(rank[:, 2:4, :], ps[1][:].rearrange("p (a n) -> p a n", a=2), ACT.Copy).then_inc(made["rank"], 1)
                    act.wait_ge(made["edges_ps"], 1)
                    act.wait_ge(made["row_of"], 1)
                    A(at[:], ps[0][:].rearrange("p (m n) -> p m n", m=MB), ACT.Copy).then_inc(made["edge_rows"], 1)
                    act.wait_ge(made["nmax"], 1)
                    for i in range(T):
                        a = A(work[:, i, :], v3[:, i, :], ACT.Exp, bias=rmax[:, i:i + 1], accum_out=rsum[:, i:i + 1])
                    a.then_inc(made["exp3"], 1)
                    act.wait_ge(made["turn3"], 1)
                    A(a3_hi[:, 0:2, :], ps[0][:].rearrange("p (a n) -> p a n", a=2), ACT.Copy)
                    A(a3_hi[:, 2:4, :], ps[1][:].rearrange("p (a n) -> p a n", a=2), ACT.Copy).then_inc(made["a3_hi"], 1)

                @block.vector
                def _(dve):
                    V = nc.vector
                    order = [0]

                    def link(ins):
                        order[0] += 1
                        ins.then_inc(dve_order, 1)
                        dve.wait_ge(dve_order, order[0])

                    dve.wait_ge(loaded, 16 * len(LOADS))
                    V.tensor_scalar(adjn[:], adj_raw[:], 0.0, None, ALU.is_gt).then_inc(made["adjn"], 1)
                    dve.wait_ge(made["pool"], POOL_SETUP)
                    dve.wait_ge(made["adjn"], 1)
                    V.tensor_copy(adj_top[:], adjn[:, 0:HALF, :].bitcast(F32))
                    V.tensor_copy(m_row[:], m_int[:])
                    V.tensor_copy(m_col[:], mc_int[:])
                    V.tensor_tensor(asum[:], asd[:, 0:1], asd[:, 1:2], ALU.add)
                    V.tensor_scalar(bprep[:], ones[:], bpcol[:, 0:1], None, ALU.mult).then_inc(made["bprep"], 1)
                    link(V.reduce_sum(cnt_row[:], adjn[:].bitcast(F32), AX_X))
                    for k in range(T):
                        a = V.tensor_scalar(cntrep[:, k, :], ones[:], cnt_row[:, k:k + 1], None, ALU.mult)
                    a.then_inc(made["counts"], 1)
                    dve.wait_ge(made["maskT"], 1)
                    mT = maskT[:].bitcast(F32)
                    V.reduce_sum(cnt_low[:], mT[:, :, N // 2:N], AX_X)
                    link(V.reduce_sum(cnt_all[:], mT, AX_X))
                    link(V.tensor_scalar(empty4[:], cnt_all[:], 0.0, None, ALU.is_equal))
                    for k in range(T):
                        V.tensor_scalar(mask0b[:, k, :], mT[:, k, N // 2:N], empty4[:, k:k + 1], None, ALU.max)
                        V.tensor_scalar(empty0[:, k, :], ones[:], empty4[:, k:k + 1], None, ALU.mult)
                    e4, l4 = bcast(empty4[:], G), bcast(cnt_low[:], G)
                    v8 = [t[:].rearrange("p (k b) -> p k b", b=G) for t in (low8, empty8, full8, share8)]
                    V.tensor_copy(v8[0], l4)
                    V.tensor_copy(v8[1], e4)
                    V.tensor_scalar(v8[2], e4, -1.0, 1.0, ALU.mult, ALU.add)
                    V.tensor_scalar(v8[3], e4, 1.0 / N, None, ALU.mult)
                    link(V.tensor_copy(bhi[:], brow[:]))
                    V.tensor_tensor(blo[:], brow[:], bhi[:].bitcast(F32), ALU.subtract)
                    V.memset(pick[:].bitcast(F32), 0.0)
                    V.memset(bias_p[:].bitcast(F32), 0.0)
                    V.memset(bias_1[:].bitcast(F32), 0.0)
                    link(V.memset(bias_2[:].bitcast(F32), 0.0))
                    for p0, src in ((0, bhi), (32, blo)):
                        row = slice(p0, p0 + 1)
                        V.tensor_copy(pick[row, :], ones[row, :])
                        V.tensor_copy(bias_p[row, 0:F], src[row, 0, :].bitcast(F32))
                        V.tensor_copy(bias_1[row, :], src[row, 1, :].bitcast(F32))
                        V.tensor_copy(bias_2[row, :], src[row, 2, :].bitcast(F32))
                    link(V.tensor_scalar(small[:, 0:1], epscol[:], 1.0, None, ALU.add))
                    link(V.tensor_scalar(epsd[:], ident[:], small[:, 0:1], None, ALU.mult))
                    for k in range(T):
                        a = V.tensor_tensor(diagv[:, k, :], mT[:, k, k * P:(k + 1) * P], epsd[:], ALU.add)
                    link(a)
                    dve.wait_ge(made["gin_hi"], 1)
                    for k in range(T):
                        a = V.tensor_copy(gin_hi[:, k, k * P:(k + 1) * P], diagv[:, k, :])
                    link(a)
                    for k in range(T):
                        V.tensor_tensor(gin_lo[:, k, :], diagv[:, k, :], gin_hi[:, k, k * P:(k + 1) * P].bitcast(F32),
                                        ALU.subtract)
                    dve.wait_ge(made["rowtot"], 1)
                    V.tensor_copy(rowtot_b[:], ps[3][:, 0:N])
                    link(V.tensor_scalar(norow[:], ps[3][:, 0:N], 0.0, None, ALU.is_equal))
                    for k in range(T):
                        V.tensor_tensor(mask2[:, k, :], mT[:, k, :], norow[:], ALU.max)
                    V.tensor_scalar(rescue8[:].rearrange("p (t b) -> p t b", b=G), bcast(cnt_row[:], G), 0.0, HUGE,
                                    ALU.is_equal, ALU.mult)
                    link(V.tensor_tensor(two8[:], ident[:, 0:TG], ident[:, TG:2 * TG], ALU.add))
                    for n in range(TG):
                        V.tensor_scalar(both8[:, n, :], ones[:], two8[:, n:n + 1], None, ALU.mult)
                    for s in range(NS):
                        V.memset(RT[s][:].bitcast(F32), 0.0)
                    dve.wait_ge(made["wvec"], 1)
                    V.tensor_copy(const1[:], ps[2][:, 518:519])
                    link(V.tensor_copy(wv[:, 0:6], ps[2][:, 512:518]))
                    V.tensor_tensor(wcols0[:, 0:1], wv[:, 0:1], wv[:, 1:2], ALU.add)
                    V.tensor_copy(wcols0[:, 1:3], wv[:, 0:2])
                    V.memset(wcols0[:, 3:4], 0.0)
                    V.tensor_copy(feat1w[:, F:F + 1], wv[:, 3:4])
                    V.tensor_copy(feat1w[:, F + 1:F + 2], wv[:, 2:3])
                    V.tensor_copy(feat2w[:, F:F + 1], wv[:, 5:6])
                    V.tensor_copy(feat2w[:, F + 1:F + 2], wv[:, 4:5])
                    dve.wait_ge(made["off"], 1)
                    V.tensor_copy(off_col[:], ps[2][:, 16:16 + T])
                    link(V.tensor_copy(off_b[:], ps[3][:, N:2 * N]))
                    V.tensor_tensor(end_col[:], off_col[:], cnt_row[:], ALU.add)
                    link(V.tensor_tensor(rowtot_b[:], rowtot_b[:], off_b[:], ALU.add))
                    for i in range(T):
                        V.tensor_scalar(v3[:, i, 0:NE], m_row[:], end_col[:, i:i + 1], None, ALU.is_ge)
                    for m in range(MB):
                        a = V.tensor_scalar(at[:, m, :], rowtot_b[:], m_col[:, m:m + 1], None, ALU.is_le)
                    link(a)
                    for i in range(T):
                        V.scalar_tensor_tensor(out=row_ofT[:, i, :], in0=m_row[:], scalar=off_col[:, i:i + 1],
                                               in1=v3[:, i, 0:NE], op0=ALU.is_ge, op1=ALU.subtract)
                    for m in range(MB):
                        a = V.scalar_tensor_tensor(out=row_of[:, m, :], in0=off_b[:], scalar=m_col[:, m:m + 1],
                                                   in1=at[:, m, :], op0=ALU.is_le, op1=ALU.subtract)
                    a.then_inc(made["row_of"], 1)
                    dve.wait_ge(made["offm"], 1)
                    link(V.scalar_tensor_tensor(out=m_loc[:], in0=ps[2][:, 32:32 + MB], scalar=-1.0, in1=m_col[:],
                                                op0=ALU.mult, op1=ALU.add))
                    link(V.tensor_scalar(m_loc[:], m_loc[:], 1.0, None, ALU.add))
                    dve.wait_ge(made["edge_rows"], 1)
                    for m in range(MB):
                        a = V.scalar_tensor_tensor(out=at[:, m, :], in0=ps[1][:, m * N:(m + 1) * N],
                                                   scalar=m_loc[:, m:m + 1], in1=at[:, m, :], op0=ALU.is_equal,
                                                   op1=ALU.mult)
                    link(a)
                    for m in range(MB):
                        a = V.tensor_scalar(e_at[:, m, :], at[:, m, :], e_col[:, m:m + 1], None, ALU.mult)
                    a.then_inc(made["at"], 1)
                    dve.wait_ge(made["cover"], 1)
                    for h in range(2):
                        a = V.tensor_tensor(v3[:, 2 * h:2 * h + 2, :], adjn[:, 2 * h:2 * h + 2, :].bitcast(F32),
                                            ps[2 + h][:].rearrange("p (a n) -> p a n", a=2), ALU.subtract)
                    link(a)
                    dve.wait_ge(made["values"], 1)
                    for i in range(T):
                        a = V.scalar_tensor_tensor(out=v3[:, i, :], in0=v3[:, i, :], scalar=e255[:, 0:1],
                                                   in1=ps[i // 2][:, (i % 2) * N:(i % 2) * N + N], op0=ALU.mult,
                                                   op1=ALU.add)
                    V.tensor_scalar(work[:], adjn[:].bitcast(F32), -1.0, -NEG, ALU.add, ALU.mult)
                    link(V.memset(small[:, 2:3], 0.0))
                    link(V.tensor_tensor(v3[:], v3[:], work[:], ALU.add))
                    link(V.reduce_max(rmax[:], v3[:], AX_X))
                    V.tensor_scalar(rmax[:], rmax[:], -1.0, None, ALU.mult).then_inc(made["nmax"], 1)
                    dve.wait_ge(made["exp3"], 1)
                    link(V.reciprocal(rinv[:], rsum[:]))
                    link(V.tensor_tensor(v3[:], work[:], bcast(rinv[:], N), ALU.mult))
                    for i in range(T):
                        a = V.tensor_tensor(diagv[:, i, :], v3[:, i, i * P:(i + 1) * P], ident[:], ALU.mult)
                    link(a)
                    V.reduce_sum(diag3[:], diagv[:], AX_X)
                    for i in range(T):
                        a = V.tensor_tensor(v3[:, i, i * P:(i + 1) * P], v3[:, i, i * P:(i + 1) * P], diagv[:, i, :],
                                            ALU.subtract)
                    a.then_inc(made["soft3"], 1)
                    dve.wait_ge(made["a3_hi"], 1)
                    for h in range(2):
                        V.tensor_tensor(a3_lo[:, 2 * h:2 * h + 2, :], ps[h][:].rearrange("p (a n) -> p a n", a=2),
                                        a3_hi[:, 2 * h:2 * h + 2, :].bitcast(F32), ALU.subtract)
                    dve.sem_clear(dve_order)

        def per(name, shape, dt=F32):
            return [sb(f"{name}{s}", shape, dt) for s in range(NS)]

        X = per("X", [P, TG, F])
        Y = per("Y", [P, TG, WD])
        HT = per("HT", [P, G, N])
        HE = per("HE", [P, TG, WD])
        VA = per("VA", [P, TG, F])
        SC = per("SC", [P, TG, F])
        HI = per("HI", [P, TG, F], F32R)
        LO = per("LO", [P, TG, F], F32R)

        def R(s):
            return SC[s][:].rearrange("p (b t) f -> p b (t f)", b=G)

        XL = sb("XL", [P, TG, F])
        HIB = sb("HIB", [P, TG, F], F32R)
        LOB = sb("LOB", [P, TG, F], F32R)
        ST = per("ST", [P, TG, 6])
        US = per("US", [P, TG, 4])
        CD = per("CD", [P, 12])
        CF = per("CF", [P, 3 * TG])
        CE = per("CE", [P, 3 * TG])
        NF = per("NF", [P, TG])
        R2 = per("R2", [P, 2 * TG], F32R)
        MX = per("MX", [P, 8])
        SM = per("SM", [P, 16, TG])
        PT = [sb(f"PT{r}", [P, T, N]) for r in range(RING)]
        S_SUM, S_DIF, S_Q, S_DD, S_VAR, S_MEAN, S_RSTD, S_INV, S_RS, S_A, S_B, S_Z = range(12)

        LNS = ["norm0", "norm1", "gat1", "mlpb1", "norm2", "norm3"]
        NLN = len(LNS)
        ln_at = {n: k for k, n in enumerate(LNS)}
        NORMED = ["norm0", "norm1", "mlpb1", "norm2", "norm3"]
        nd_at = {n: k for k, n in enumerate(NORMED)}
        ATT = {"1": 0, "2": 1}
        HIS = {"a0": 0, "b0": 1, "1": 2, "3a": 3, "3b": 4}
        LOS = {"0": 0, "1": 1, "3": 2}

        def rows_of(ap, u, b):
            return ap.rearrange("b (t p) f -> b p t f", p=P)[u.all_groups(G, b)]

        with nc.Block() as block:
            @block.sync
            def _(sp):
                def load(u, s):
                    if u.group is None or u.group > 0:
                        sp.wait_ge(raw_free, u.all_groups(1, 0))
                    for b in range(G):
                        sp.dma_start(XL[:, b::G, :], rows_of(x, u, b)).then_inc(x_loaded, 16)

                def store(u, s):
                    sp.wait_ge(sig["result"][s], count(u.g, 1, 0))
                    for b in range(G):
                        sp.dma_start(rows_of(out, u, b), X[s][:, b::G, :]).then_inc(sig["stored"][s], 16)

                walk(sp, "sp", {"load": load, "store": store})
                for s in range(NS):
                    sp.wait_ge(sig["stored"][s], 16 * G * ((GROUPS - s + NS - 1) // NS) + 16)

            @block.tensor
            def _(pe):
                T_ = nc.tensor.transpose

                def MM(o, w, m, start, stop):
                    return nc.tensor.matmul(o, w, m, start=start, stop=stop, skip_group_check=True)

                def open_tile(u, name, s, n=0):
                    slot, k = u.tile(name, n)
                    pe.wait_ge(taken[slot], k + 1)
                    return ps[slot], full[slot]

                def turned(u, name, s):
                    slot, k = u.tile(name, 0)
                    pe.wait_ge(taken[slot], k + 2)

                def turn_rows(u, name, s):
                    pe.wait_ge(sig["normed"][s], count(u.g, len(NORMED), nd_at[name]))
                    o, done = open_tile(u, name, s)
                    for b in range(G):
                        for t in range(T):
                            c = b * N + t * P
                            mm = T_(o[:, c:c + P], Y[s][:, t * G + b, 0:F], ident[:])
                    mm.then_inc(done, 1)

                def blk(s, b, t):
                    return HT[s][:, b, t * P:(t + 1) * P]

                def coef0(u, s):
                    turned(u, "norm0", s)
                    o, done = open_tile(u, "coef0", s, 0)
                    for t in range(HALF):
                        for odd in range(2):
                            for b in range(G):
                                c = 4 * ((t * 2 + odd) * G + b)
                                r0 = t * 2 * P + odd
                                mm = MM(o[:, c:c + 4], HT[s][:, b, r0:r0 + 2 * P - 1:2], wcols0[:], True, True)
                    mm.then_inc(done, 1)

                def coefb0(u, s):
                    pe.wait_ge(sig["cexp"][s], count(u.g, 1, 0))
                    o, done = open_tile(u, "coefb0", s)
                    for k in range(T):
                        for t in range(HALF):
                            c = (t * 2 + k // HALF) * G
                            mm = MM(o[:, k * G:(k + 1) * G], adj_top[:, t, k * P:(k + 1) * P],
                                    CE[s][:, c:c + G], t == 0, t == HALF - 1)
                    mm.then_inc(done, 1)

                def feat0(u, s):
                    o, done = open_tile(u, "feat0", s)
                    for t in range(T):
                        for b in range(G):
                            c = (t * G + b) * F
                            mm = MM(o[:, c:c + F], blk(s, b, t), Wo[:], True, True)
                    mm.then_inc(done, 1)

                def agg0(u, s):
                    pe.wait_ge(sig["lo"][s], count(u.g, len(LOS), LOS["0"]))
                    o, done = open_tile(u, "agg0", s, 0)
                    for t in range(HALF):
                        for side in range(2):
                            c = (t * 2 + side) * G * F
                            parts = [(k, m) for k in (2 * side, 2 * side + 1) for m in (HI, LO)]
                            for n, (k, m) in enumerate(parts):
                                mm = MM(o[:, c:c + G * F], maskT[:, k, t * P:(t + 1) * P],
                                        m[s][:, k * G:(k + 1) * G, :], n == 0, n == len(parts) - 1)
                    mm.then_inc(done, 1)

                def self0(u, s):
                    pe.wait_ge(sig["lo_below"][s], count(u.g, 1, 0))
                    o, done = open_tile(u, "self0", s)
                    for t in range(T):
                        c = t * G * F
                        for b in range(G):
                            MM(o[:, c + b * F:c + (b + 1) * F], blk(s, b, t), Ws[:], b == 0, False)
                        for k in range(T):
                            w = empty0[:, k, :] if t < HALF else mask0b[:, k, (t - HALF) * P:(t - HALF + 1) * P]
                            for m in (HIB, LOB):
                                mm = MM(o[:, c:c + G * F], w, m[:, k * G:(k + 1) * G, :], False,
                                        k == T - 1 and m is LOB)
                    mm.then_inc(done, 1)

                def feat(u, name, s, w, bias, before):
                    turned(u, before, s)
                    for h in range(2):
                        o, done = open_tile(u, name, s, h)
                        o4 = o[:].rearrange("p (t b c) -> p t b c", t=2, b=G)
                        for tt in range(2):
                            if bias is not None:
                                MM(o4[:, tt, :, 0:WD], pick[:], repeat(bias[:], G), True, False)
                            for b in range(G):
                                mm = MM(o4[:, tt, b, 0:w.shape[1]], blk(s, b, 2 * h + tt), w,
                                        bias is None, True)
                        mm.then_inc(done, 1)

                def turn_r(u, name, s):
                    pe.wait_ge(sig["r_split"][s], count(u.g, 2, ATT[name[-1]]))
                    o, done = open_tile(u, name, s, 0)
                    T_(o[0:2 * TG, 0:P], R2[s][:].bitcast(F32), ident[:]).then_inc(done, 1)

                def spread(u, name, s):
                    turned(u, "turn" + name[-1], s)
                    o, done = open_tile(u, name, s)
                    for t in range(T):
                        for b in range(G):
                            c = b * N + t * P
                            mm = MM(o[:, c:c + P], both8[:, t * G + b, :], RT[s][:], True, True)
                    mm.then_inc(done, 1)

                def attend(u, name, s, b):
                    r, k = u.matrix(name)
                    pe.wait_ge(p_full[r], k + 1)
                    o, done = open_tile(u, name, s)
                    for i in range(T):
                        for j in range(T):
                            mm = MM(o[:, i * 2 * P:i * 2 * P + F + 1], PT[r][:, j, i * P:(i + 1) * P],
                                    HE[s][:, j * G + b, 0:F + 1], j == 0, j == T - 1)
                    mm.then_inc(done, 1)

                def gin1(u, s):
                    pe.wait_ge(sig["lo"][s], count(u.g, len(LOS), LOS["1"]))
                    o, done = open_tile(u, "gin1", s)
                    for b in range(G):
                        for j in range(T):
                            for m in (HI, LO):
                                MM(o[:, b * N:(b + 1) * N], m[s][:, j * G + b, :], gin_hi[:, j, :],
                                   j == 0 and m is HI, False)
                            c = b * N + j * P
                            mm = MM(o[:, c:c + P], HI[s][:, j * G + b, :], gin_lo[:, j, :], False, j == T - 1)
                    mm.then_inc(done, 1)

                def mlp(u, name, s, w, bias, before):
                    turned(u, before, s)
                    o, done = open_tile(u, name, s)
                    for t in range(T):
                        if t % 2 == 0:
                            MM(o[:, t * G * F:(t + 2) * G * F], pick[:], repeat(bias[:], 2 * G), True, False)
                        for b in range(G):
                            c = (t * G + b) * F
                            mm = MM(o[:, c:c + F], blk(s, b, t), w[:], False, True)
                    mm.then_inc(done, 1)

                def agg3(u, s):
                    pe.wait_ge(sig["lo"][s], count(u.g, len(LOS), LOS["3"]))
                    o, done = open_tile(u, "agg3", s)
                    for t in range(T):
                        c = t * G * F
                        parts = [(k, w, m) for k in range(T) for w, m in ((a3_hi, HI), (a3_hi, LO), (a3_lo, HI))]
                        for n, (k, w, m) in enumerate(parts):
                            mm = MM(o[:, c:c + G * F], w[:, k, t * P:(t + 1) * P], m[s][:, k * G:(k + 1) * G, :],
                                    n == 0, n == len(parts) - 1)
                    mm.then_inc(done, 1)

                run = {
                    "coef0": coef0, "coefb0": coefb0, "feat0": feat0, "agg0": agg0, "self0": self0, "gin1": gin1, "agg3": agg3,
                    "norm0": lambda u, s: turn_rows(u, "norm0", s),
                    "norm1": lambda u, s: turn_rows(u, "norm1", s),
                    "norm2": lambda u, s: turn_rows(u, "norm2", s),
                    "norm3": lambda u, s: turn_rows(u, "norm3", s),
                    "mlpb1": lambda u, s: turn_rows(u, "mlpb1", s),
                    "feat1": lambda u, s: feat(u, "feat1", s, feat1w[:], bias_p, "norm1"),
                    "feat2": lambda u, s: feat(u, "feat2", s, feat2w[:], None, "norm2"),
                    "feat3": lambda u, s: feat(u, "feat3", s, W3[:].rearrange("p a f -> p (a f)"), None, "norm3"),
                    "turn1": lambda u, s: turn_r(u, "turn1", s),
                    "turn2": lambda u, s: turn_r(u, "turn2", s),
                    "spread1": lambda u, s: spread(u, "spread1", s),
                    "spread2": lambda u, s: spread(u, "spread2", s),
                    "att1a": lambda u, s: attend(u, "att1a", s, 0),
                    "att1b": lambda u, s: attend(u, "att1b", s, 1),
                    "att2a": lambda u, s: attend(u, "att2a", s, 0),
                    "att2b": lambda u, s: attend(u, "att2b", s, 1),
                    "mlpa1": lambda u, s: mlp(u, "mlpa1", s, W1, bias_1, "gin1"),
                    "mlpc1": lambda u, s: mlp(u, "mlpc1", s, W2, bias_2, "mlpb1"),
                }
                def pass_tiles(u):
                    for n in range(tiles_of[u.name]):
                        slot, k = u.tile(u.name, n)
                        pe.wait_ge(taken[slot], k + 1)
                        pe.sem_inc(full[slot], 1)
                        pe.sem_inc(taken[slot], 1)

                walk(pe, "pe", run, pass_tiles)

            @block.scalar
            def _(act):
                A = nc.scalar.activation
                order = [0]

                def filled(u, name, s, n=0):
                    slot, k = u.tile(name, n)
                    act.wait_ge(full[slot], k + 1)
                    return ps[slot], taken[slot]

                def turn_rows(u, name, s):
                    o, read = filled(u, name, s)
                    v = o[:].rearrange("p (b n) -> p b n", b=G)
                    if name == "mlpb1":
                        A(HT[s][:], v, ACT.Relu, scale=mlp_g[:, 0:1], bias=mlp_b[:, 0:1]).then_inc(read, 1)
                    else:
                        A(HT[s][:], v, ACT.Relu).then_inc(read, 1)

                def coefb0(u, s):
                    act.wait_ge(sig["cdiff"][s], count(u.g, 1, 0))
                    A(CE[s][:, 0:2 * TG], CF[s][:, 0:2 * TG], ACT.Exp).then_inc(sig["cexp"][s], 1)

                def split0(u, s):
                    act.wait_ge(sig["scaled"][s], count(u.g, 1, 0))
                    A(HI[s][:], SC[s][:], ACT.Copy).then_inc(sig["hi"][s], 1)
                    slot, k = u.tile("feat0", 0)
                    act.wait_ge(taken[slot], k + 2)
                    A(HIB[:], VA[s][:], ACT.Copy).then_inc(sig["hi"][s], 1)

                def feat(u, name, s):
                    for h in range(2):
                        o, read = filled(u, name, s, h)
                        v = o[:].rearrange("p (r c) -> p r c", c=2 * P)
                        A(HE[s][:, 4 * h:4 * h + 4, :], v[:, :, 0:WD], ACT.Copy).then_inc(read, 1)

                def score(u, name, s):
                    act.wait_ge(sig["ddiff"][s], count(u.g, 2, ATT[name[-1]]))
                    A(CE[s][:], CF[s][:], ACT.Exp).then_inc(sig["dexp"][s], 1)

                def turn_r(u, name, s):
                    o, read = filled(u, name, s)
                    A(RT[s][0:2 * TG, :], o[0:2 * TG, 0:P], ACT.Copy).then_inc(read, 1)

                def spread(u, name, s):
                    o, read = filled(u, name, s)
                    A(R(s), o[:].rearrange("p (b n) -> p b n", b=G), ACT.Copy).then_inc(read, 1)

                def attend(u, name, s, b):
                    slot, k = u.tile("spread" + name[3])
                    act.wait_ge(taken[slot], k + 2)
                    act.wait_ge(sig["r_split"][s], count(u.g, 2, ATT[name[3]]))
                    r, k = u.matrix(name)
                    act.wait_ge(p_taken[r], k + 1)
                    for j in range(T):
                        c = j * G + b
                        a = A(PT[r][:, j, :], R(s)[:, b, :], ACT.Relu, scale=CE[s][:, TG + c:TG + c + 1],
                              bias=NF[s][:, c:c + 1])
                    a.then_inc(sig["raised"][s], 1)

                def collect(u, name, s, b):
                    att = name.replace("collect", "att")
                    slot, k = u.tile(att)
                    act.wait_ge(full[slot], k + 1)
                    r, k = u.matrix(att)
                    v = ps[slot][:].rearrange("p (t c) -> p t c", c=2 * P)
                    for h in range(2):
                        y = Y[s][:].rearrange("p (t b) c -> p t b c", b=G)[:, 2 * h:2 * h + 2, b, 0:F + 1]
                        A(y, v[:, 2 * h:2 * h + 2, 0:F + 1], ACT.Copy).then_inc((p_taken[r], taken[slot])[h], 1)

                def gat1(u, s):
                    act.wait_ge(sig["gated"][s], count(u.g, 2, 0))
                    A(HI[s][:], VA[s][:], ACT.Relu).then_inc(sig["hi"][s], 1)

                def gin1(u, s):
                    o, read = filled(u, "gin1", s)
                    A(HT[s][:], o[:].rearrange("p (b n) -> p b n", b=G), ACT.Copy).then_inc(read, 1)

                def mlpa1(u, s):
                    o, read = filled(u, "mlpa1", s)
                    A(Y[s][:, :, 0:F], o[:].rearrange("p (r f) -> p r f", f=F), ACT.Copy).then_inc(read, 1)

                def elu2(u, s):
                    act.wait_ge(sig["gated"][s], count(u.g, 2, 1))
                    A(SC[s][:], VA[s][:], ACT.Exp).then_inc(sig["eluexp"][s], 1)

                def feat3(u, s):
                    for h in range(2):
                        slot, k = u.tile("feat3", h)
                        act.wait_ge(full[slot], k + 1)
                        v = ps[slot][:].rearrange("p (r c) -> p r c", c=2 * P)
                        A(HI[s][:, 4 * h:4 * h + 4, :], v[:, :, F:2 * F], ACT.Copy).then_inc(sig["hi"][s], 1)

                run = {
                    "coefb0": coefb0, "split0": split0, "gat1": gat1, "gin1": gin1, "mlpa1": mlpa1, "elu2": elu2,
                    "feat3": feat3,
                    "norm0": lambda u, s: turn_rows(u, "norm0", s),
                    "norm1": lambda u, s: turn_rows(u, "norm1", s),
                    "norm2": lambda u, s: turn_rows(u, "norm2", s),
                    "norm3": lambda u, s: turn_rows(u, "norm3", s),
                    "mlpb1": lambda u, s: turn_rows(u, "mlpb1", s),
                    "feat1": lambda u, s: feat(u, "feat1", s),
                    "feat2": lambda u, s: feat(u, "feat2", s),
                    "score1": lambda u, s: score(u, "score1", s),
                    "score2": lambda u, s: score(u, "score2", s),
                    "turn1": lambda u, s: turn_r(u, "turn1", s),
                    "turn2": lambda u, s: turn_r(u, "turn2", s),
                    "spread1": lambda u, s: spread(u, "spread1", s),
                    "spread2": lambda u, s: spread(u, "spread2", s),
                    "att1a": lambda u, s: attend(u, "att1a", s, 0),
                    "att1b": lambda u, s: attend(u, "att1b", s, 1),
                    "att2a": lambda u, s: attend(u, "att2a", s, 0),
                    "att2b": lambda u, s: attend(u, "att2b", s, 1),
                    "collect1a": lambda u, s: collect(u, "collect1a", s, 0),
                    "collect1b": lambda u, s: collect(u, "collect1b", s, 1),
                    "collect2a": lambda u, s: collect(u, "collect2a", s, 0),
                    "collect2b": lambda u, s: collect(u, "collect2b", s, 1),
                }
                def pass_matrices(u):
                    if u.name in mat_at:
                        r, k = u.matrix(u.name)
                        act.wait_ge(p_taken[r], k + 1)
                        act.sem_inc(p_full[r], 1)
                        act.sem_inc(p_taken[r], 1)

                walk(act, "act", run, pass_matrices)

            @block.gpsimd
            def _(pool):
                TT = nc.gpsimd.tensor_tensor

                def rstd(u, name, s):
                    pool.wait_ge(sig["var"][s], count(u.g, NLN, ln_at[name]))
                    TT(SM[s][:, S_RSTD, :], SM[s][:, S_VAR, :], minus_half[:], ALU.pow).then_inc(sig["rstd"][s], 1)

                def all_max(s, done):
                    TT(MX[s][:, 6:8], MX[s][:, 0:2], ones[:, 0:2], ALU.mult).then_inc(pool_order, 1)
                    pool.wait_ge(pool_order, 1)
                    nc.gpsimd.partition_all_reduce(MX[s][:, 2:4], MX[s][:, 6:8], P, RMAX).then_inc(done, 1)
                    pool.sem_clear(pool_order)

                def cmax(u, s):
                    pool.wait_ge(sig["cmax"][s], count(u.g, 1, 0))
                    all_max(s, sig["cmax_all"][s])

                def dmax(u, name, s):
                    pool.wait_ge(sig["dmax"][s], count(u.g, 2, ATT[name[-1]]))
                    all_max(s, sig["dmax_all"][s])

                def low0(u, s):
                    pool.wait_ge(sig["hi"][s], count(u.g, len(HIS), HIS["b0"]))
                    TT(LOB[:], VA[s][:], HIB[:].bitcast(F32), ALU.subtract).then_inc(sig["lo_below"][s], 1)

                def norm2(u, s):
                    pool.wait_ge(sig["normed"][s], count(u.g, len(NORMED), nd_at["norm2"]))
                    TT(X[s][:], X[s][:], repeat(ones[:], TG), ALU.subtract).then_inc(sig["shifted"][s], 1)

                def norm3(u, s):
                    pool.wait_ge(sig["normed"][s], count(u.g, len(NORMED), nd_at["norm3"]))
                    TT(X[s][:], X[s][:], repeat(bias3[:], TG), ALU.add).then_inc(sig["shifted"][s], 1)

                run = {
                    "coef0": cmax, "low0": low0, "norm2": norm2, "norm3": norm3,
                    "feat1": lambda u, s: dmax(u, "feat1", s),
                    "feat2": lambda u, s: dmax(u, "feat2", s),
                    "stat0": lambda u, s: rstd(u, "norm0", s),
                    "stat1": lambda u, s: rstd(u, "norm1", s),
                    "stat2": lambda u, s: rstd(u, "norm2", s),
                    "stat3": lambda u, s: rstd(u, "norm3", s),
                    "gats1": lambda u, s: rstd(u, "gat1", s),
                    "mlps1": lambda u, s: rstd(u, "mlpb1", s),
                }
                walk(pool, "pool", run)

            @block.vector
            def _(dve):
                V = nc.vector
                order = [0]

                def link(ins):
                    order[0] += 1
                    ins.then_inc(dve_order, 1)
                    dve.wait_ge(dve_order, order[0])

                def filled(u, name, s, n=0):
                    slot, k = u.tile(name, n)
                    dve.wait_ge(full[slot], k + 1)
                    return ps[slot], taken[slot]

                def read_by_act(u, name, s, n=0):
                    slot, k = u.tile(name, n)
                    dve.wait_ge(taken[slot], k + 2)

                def stats(u, s, src, sums=None):
                    st, sm = ST[s], SM[s]
                    for n in range(TG):
                        a = V.bn_stats(st[:, n, :], src(n))
                    link(a)
                    V.tensor_tensor(sm[:, S_DIF, :], st[:, :, 1], st[:, :, 4], ALU.subtract)
                    V.tensor_tensor(sm[:, S_SUM, :], st[:, :, 1], st[:, :, 4], ALU.add)
                    if sums is not None:
                        V.tensor_scalar(sm[:, S_INV, :], sums, TINY, None, ALU.max)
                    link(V.tensor_tensor(sm[:, S_Q, :], st[:, :, 2], st[:, :, 5], ALU.add))
                    V.scalar_tensor_tensor(out=sm[:, S_DD, :], in0=sm[:, S_DIF, :], scalar=0.25,
                                           in1=sm[:, S_DIF, :], op0=ALU.mult, op1=ALU.mult)
                    V.tensor_scalar(sm[:, S_MEAN, :], sm[:, S_SUM, :], 0.5, None, ALU.mult)
                    if sums is not None:
                        V.reciprocal(sm[:, S_INV, :], sm[:, S_INV, :])
                    link(V.tensor_scalar(sm[:, S_Q, :], sm[:, S_Q, :], 1.0 / F, None, ALU.mult))
                    link(V.tensor_tensor(sm[:, S_VAR, :], sm[:, S_Q, :], sm[:, S_DD, :], ALU.add))
                    if sums is not None:
                        for _ in range(2):
                            link(V.tensor_tensor(sm[:, S_VAR, :], sm[:, S_VAR, :], sm[:, S_INV, :], ALU.mult))
                    V.tensor_scalar(sm[:, S_VAR, :], sm[:, S_VAR, :], LN_EPS, None, ALU.add).then_inc(
                        sig["var"][s], 1)

                def normalise(u, name, s, src):
                    sm = SM[s]
                    dve.wait_ge(sig["rstd"][s], count(u.g, NLN, ln_at[name]))
                    for n in range(TG):
                        a = V.tensor_scalar(Y[s][:, n, 0:F], src(n), sm[:, S_MEAN, n:n + 1],
                                            sm[:, S_RSTD, n:n + 1], ALU.subtract, ALU.mult)
                    a.then_inc(sig["normed"][s], 1)

                def stat0(u, s):
                    dve.wait_ge(x_loaded, u.all_groups(16 * G, 16 * G))
                    stats(u, s, lambda n: XL[:, n, :])

                def stat(u, s):
                    stats(u, s, lambda n: X[s][:, n, :])

                def coef0(u, s):
                    o, read = filled(u, "coef0", s)
                    V.tensor_copy(US[s][:], o[:, 0:4 * TG].rearrange("p (r c) -> p r c", c=4)).then_inc(read, 1)
                    read_by_act(u, "coef0", s)
                    u4 = US[s][:].rearrange("p (t o b) c -> p t o b c", t=HALF, o=2)
                    V.tensor_copy(CD[s][:, 0:TG], US[s][:, :, 0])
                    link(V.tensor_tensor(CD[s][:, TG:12].rearrange("p (t b) -> p t b", b=G), u4[:, :, 0, :, 1],
                                         u4[:, :, 1, :, 2], ALU.add))
                    link(V.scalar_tensor_tensor(out=CD[s][:], in0=CD[s][:], scalar=0.1, in1=CD[s][:],
                                                op0=ALU.mult, op1=ALU.max))
                    V.reduce_max(MX[s][:, 0:2], CD[s][:, 0:TG].rearrange("p (r b) -> p b r", b=G),
                                 AX_X).then_inc(sig["cmax"][s], 1)

                def coefm0(u, s):
                    dve.wait_ge(sig["cmax_all"][s], count(u.g, 1, 0))
                    m = MX[s][:, 2:4]
                    d = CD[s][:, TG:12].rearrange("p (t b) -> p t b", b=G)
                    mk = SM[s][:, S_A, 0:4].rearrange("p (t b) -> p t b", b=G)
                    V.tensor_tensor(CF[s][:, 0:TG].rearrange("p (r b) -> p r b", b=G),
                                    CD[s][:, 0:TG].rearrange("p (r b) -> p r b", b=G), repeat(m, 4), ALU.subtract)
                    link(V.tensor_tensor(mk, d, repeat(m, 2), ALU.max))
                    V.tensor_tensor(CF[s][:, 8:12].rearrange("p (t b) -> p t b", b=G), repeat(m, 2), mk, ALU.subtract)
                    V.tensor_tensor(CF[s][:, 12:16].rearrange("p (t b) -> p t b", b=G), d, mk,
                                    ALU.subtract).then_inc(sig["cdiff"][s], 1)

                def coefb0(u, s):
                    o, read = filled(u, "coefb0", s)
                    sm = SM[s]
                    a2, b2 = repeat(CE[s][:, 8:12], 2), repeat(CE[s][:, 12:16], 2)

                    def two(ap):
                        return ap.rearrange("p (h r) -> p h r", h=2)
                    V.tensor_tensor(two(sm[:, S_B, :]), two(low8[:]), b2, ALU.mult)
                    V.tensor_tensor(two(sm[:, S_Z, :]), two(o[:, 0:TG]), a2, ALU.mult).then_inc(read, 1)
                    read_by_act(u, "coefb0", s)
                    link(V.tensor_tensor(sm[:, S_Z, :], sm[:, S_Z, :], sm[:, S_B, :], ALU.add))
                    link(V.tensor_tensor(sm[:, S_Z, :], sm[:, S_Z, :], empty8[:], ALU.add))
                    link(V.tensor_scalar(sm[:, S_Z, :], sm[:, S_Z, :], TINY, None, ALU.max))
                    link(V.reciprocal(sm[:, S_Z, :], sm[:, S_Z, :]))
                    V.tensor_tensor(two(sm[:, S_A, :]), two(sm[:, S_Z, :]), a2, ALU.mult)
                    link(V.tensor_tensor(two(sm[:, S_B, :]), two(sm[:, S_Z, :]), b2, ALU.mult))
                    link(V.tensor_tensor(sm[:, S_B, :], sm[:, S_B, :], full8[:], ALU.mult))
                    link(V.tensor_tensor(sm[:, S_B, :], sm[:, S_B, :], share8[:], ALU.add))

                def split0(u, s):
                    o, read = filled(u, "feat0", s)
                    v = o[:].rearrange("p (r f) -> p r f", f=F)
                    V.tensor_tensor(SC[s][:], v, bcast(SM[s][:, S_A, :], F), ALU.mult).then_inc(sig["scaled"][s], 1)
                    V.tensor_tensor(VA[s][:], v, bcast(SM[s][:, S_B, :], F), ALU.mult).then_inc(read, 1)

                def low0(u, s):
                    dve.wait_ge(sig["hi"][s], count(u.g, len(HIS), HIS["a0"]))
                    V.tensor_tensor(LO[s][:], SC[s][:], HI[s][:].bitcast(F32), ALU.subtract).then_inc(
                        sig["lo"][s], 1)

                def agg0(u, s):
                    og, read_g = filled(u, "agg0", s)
                    V.tensor_tensor(SC[s][:], og[:].rearrange("p (r f) -> p r f", f=F), bcast(CE[s][:, 0:TG], F),
                                    ALU.mult).then_inc(read_g, 1)

                def self0(u, s):
                    os_, read_s = filled(u, "self0", s)
                    dve.wait_ge(sig["stored"][s], u.g * (16 * G) + 16)
                    V.tensor_tensor(X[s][:], XL[:], os_[:].rearrange("p (r f) -> p r f", f=F),
                                    ALU.add).then_inc(read_s, 1)
                    sc = SC[s][:].rearrange("p (t h b) f -> p t h (b f)", t=HALF, h=2)
                    xt = X[s][:, 0:HALF * G, :].rearrange("p (t b) f -> p t (b f)", b=G)
                    read_by_act(u, "agg0", s)
                    read_by_act(u, "self0", s)
                    link(V.tensor_tensor(xt, xt, sc[:, :, 0, :], ALU.add))
                    V.tensor_tensor(xt, xt, sc[:, :, 1, :], ALU.add).then_inc(raw_free, 1)
                    dve.wait_ge(raw_free, u.all_groups(1, 1))

                def dmax(u, name, s):
                    read_by_act(u, name, s, 0)
                    read_by_act(u, name, s, 1)
                    V.reduce_max(MX[s][:, 0:2], HE[s][:].rearrange("p (t b) c -> p b t c", b=G)[:, :, :, F],
                                 AX_X).then_inc(sig["dmax"][s], 1)

                def ddiff(u, name, s):
                    dve.wait_ge(sig["dmax_all"][s], count(u.g, 2, ATT[name[-1]]))
                    he = HE[s][:].rearrange("p (t b) c -> p t b c", b=G)
                    cf = CF[s][:].rearrange("p (k t b) -> p k t b", k=3, b=G)
                    top = repeat(MX[s][:, 2:4], T)
                    V.tensor_tensor(cf[:, 0], he[:, :, :, F], top, ALU.subtract)
                    link(V.tensor_tensor(cf[:, 2], he[:, :, :, F + 1], top, ALU.add))
                    const = const1[:, 0:1] if name[-1] == "1" else 0.0
                    V.tensor_scalar(cf[:, 1], cf[:, 0], 0.2, None, ALU.mult)
                    link(V.tensor_scalar(cf[:, 2], cf[:, 2], const, -0.8, ALU.add, ALU.mult))
                    V.tensor_scalar(cf[:, 2], cf[:, 2], 0.0, None, ALU.min)
                    V.memset(HE[s][:, :, F:F + 1], 1.0).then_inc(sig["ddiff"][s], 1)

                def turn_r(u, name, s):
                    n = ATT[name[-1]]
                    dve.wait_ge(sig["dexp"][s], count(u.g, 2, n))
                    rr = CE[s][:, 2 * TG:3 * TG]
                    V.tensor_scalar(NF[s][:], CE[s][:, 0:TG], -1.0, None, ALU.mult)
                    if n == 1:
                        link(V.tensor_tensor(rr, rr, rescue8[:], ALU.add))
                    link(V.tensor_copy(R2[s][:, 0:TG], rr))
                    V.tensor_tensor(R2[s][:, TG:2 * TG], rr, R2[s][:, 0:TG].bitcast(F32), ALU.subtract).then_inc(
                        sig["r_split"][s], 1)

                def attend(u, name, s, b):
                    n = ATT[name[3]]
                    mask = (maskT[:].bitcast(F32), mask2[:])[n]
                    dve.wait_ge(sig["raised"][s], count(u.g, 2 * G, n * G + b))
                    r, k = u.matrix(name)
                    for j in range(T):
                        c = j * G + b
                        a = V.scalar_tensor_tensor(out=PT[r][:, j, :], in0=PT[r][:, j, :],
                                                   scalar=CE[s][:, c:c + 1], in1=mask[:, j, :], op0=ALU.add,
                                                   op1=ALU.min)
                    a.then_inc(p_full[r], 1)

                def gats1(u, s):
                    for b in range(G):
                        read_by_act(u, "att1" + "ab"[b], s)
                    stats(u, s, lambda n: Y[s][:, n, 0:F], Y[s][:, :, F])

                def gain1(u, s):
                    for n in range(TG):
                        a = V.scalar_tensor_tensor(out=VA[s][:, n, :], in0=Y[s][:, n, 0:F],
                                                   scalar=SM[s][:, S_MEAN, n:n + 1], in1=gat_g[:],
                                                   op0=ALU.subtract, op1=ALU.mult)
                    link(a)

                def gat1(u, s):
                    dve.wait_ge(sig["rstd"][s], count(u.g, NLN, ln_at["gat1"]))
                    link(V.tensor_tensor(SM[s][:, S_RS, :], SM[s][:, S_RSTD, :], SM[s][:, S_INV, :], ALU.mult))
                    for n in range(TG):
                        a = V.scalar_tensor_tensor(out=VA[s][:, n, :], in0=VA[s][:, n, :],
                                                   scalar=SM[s][:, S_RS, n:n + 1], in1=gat_b[:],
                                                   op0=ALU.mult, op1=ALU.add)
                    a.then_inc(sig["gated"][s], 1)

                def gatl1(u, s):
                    dve.wait_ge(sig["hi"][s], count(u.g, len(HIS), HIS["1"]))
                    V.scalar_tensor_tensor(out=LO[s][:], in0=VA[s][:], scalar=0.0, in1=HI[s][:].bitcast(F32),
                                           op0=ALU.max, op1=ALU.subtract).then_inc(sig["lo"][s], 1)

                def mlps1(u, s):
                    read_by_act(u, "mlpa1", s)
                    stats(u, s, lambda n: Y[s][:, n, 0:F])

                def mlpc1(u, s):
                    o, read = filled(u, "mlpc1", s)
                    V.scalar_tensor_tensor(out=SC[s][:], in0=VA[s][:], scalar=0.0,
                                           in1=o[:].rearrange("p (r f) -> p r f", f=F), op0=ALU.max,
                                           op1=ALU.add).then_inc(read, 1)
                    read_by_act(u, "mlpc1", s)
                    link(V.scalar_tensor_tensor(out=X[s][:], in0=SC[s][:], scalar=0.0, in1=X[s][:], op0=ALU.max,
                                                op1=ALU.add))

                def elud2(u, s):
                    for b in range(G):
                        read_by_act(u, "att2" + "ab"[b], s)
                    link(V.tensor_scalar(SM[s][:, S_INV, :], Y[s][:, :, F], TINY, None, ALU.max))
                    link(V.reciprocal(SM[s][:, S_INV, :], SM[s][:, S_INV, :]))
                    for n in range(TG):
                        a = V.scalar_tensor_tensor(out=VA[s][:, n, :], in0=Y[s][:, n, 0:F],
                                                   scalar=SM[s][:, S_INV, n:n + 1], in1=bias2[:], op0=ALU.mult,
                                                   op1=ALU.add)
                    a.then_inc(sig["gated"][s], 1)

                def elu2(u, s):
                    dve.wait_ge(sig["eluexp"][s], count(u.g, 1, 0))
                    dve.wait_ge(sig["shifted"][s], count(u.g, 2, 0))
                    link(V.scalar_tensor_tensor(out=SC[s][:], in0=SC[s][:], scalar=1.0, in1=X[s][:], op0=ALU.min,
                                                op1=ALU.add))
                    link(V.scalar_tensor_tensor(out=X[s][:], in0=VA[s][:], scalar=0.0, in1=SC[s][:], op0=ALU.max,
                                                op1=ALU.add))

                def feat3(u, s):
                    dve.wait_ge(sig["shifted"][s], count(u.g, 2, 1))
                    for h in range(2):
                        slot, k = u.tile("feat3", h)
                        dve.wait_ge(sig["hi"][s], count(u.g, len(HIS), HIS["3a"] + h))
                        v = ps[slot][:].rearrange("p (r c) -> p r c", c=2 * P)
                        a = V.tensor_tensor(LO[s][:, 4 * h:4 * h + 4, :], v[:, :, F:2 * F],
                                            HI[s][:, 4 * h:4 * h + 4, :].bitcast(F32), ALU.subtract)
                        if h == 1:
                            a.then_inc(sig["lo"][s], 1)
                        for tt in range(2):
                            t = 2 * h + tt
                            xt = X[s][:, t * G:(t + 1) * G, :]
                            a = V.scalar_tensor_tensor(out=xt, in0=v[:, tt * G:(tt + 1) * G, 0:F],
                                                       scalar=diag3[:, t:t + 1], in1=xt, op0=ALU.mult, op1=ALU.add)
                        a.then_inc(taken[slot], 1)

                def agg3(u, s):
                    for h in range(2):
                        read_by_act(u, "feat3", s, h)
                    o, read = filled(u, "agg3", s)
                    V.tensor_tensor(X[s][:], X[s][:], o[:].rearrange("p (r f) -> p r f", f=F),
                                    ALU.add).then_inc(read, 1)
                    read_by_act(u, "agg3", s)
                    dve.sem_inc(sig["result"][s], 1)

                def from_x(s):
                    return lambda n: X[s][:, n, :]

                run = {
                    "stat0": stat0, "stat1": stat, "stat2": stat, "stat3": stat, "coef0": coef0, "coefm0": coefm0,
                    "coefb0": coefb0, "split0": split0, "low0": low0, "agg0": agg0, "self0": self0, "gats1": gats1, "gain1": gain1, "gat1": gat1, "gatl1": gatl1,
                    "mlps1": mlps1, "mlpc1": mlpc1, "elud2": elud2, "elu2": elu2, "feat3": feat3, "agg3": agg3,
                    "norm0": lambda u, s: normalise(u, "norm0", s, lambda n: XL[:, n, :]),
                    "norm1": lambda u, s: normalise(u, "norm1", s, from_x(s)),
                    "norm2": lambda u, s: normalise(u, "norm2", s, from_x(s)),
                    "norm3": lambda u, s: normalise(u, "norm3", s, from_x(s)),
                    "mlpb1": lambda u, s: normalise(u, "mlpb1", s, lambda n: Y[s][:, n, 0:F]),
                    "feat1": lambda u, s: dmax(u, "feat1", s),
                    "feat2": lambda u, s: dmax(u, "feat2", s),
                    "score1": lambda u, s: ddiff(u, "score1", s),
                    "score2": lambda u, s: ddiff(u, "score2", s),
                    "turn1": lambda u, s: turn_r(u, "turn1", s),
                    "turn2": lambda u, s: turn_r(u, "turn2", s),
                    "att1a": lambda u, s: attend(u, "att1a", s, 0),
                    "att1b": lambda u, s: attend(u, "att1b", s, 1),
                    "att2a": lambda u, s: attend(u, "att2a", s, 0),
                    "att2b": lambda u, s: attend(u, "att2b", s, 1),
                }
                def end_pass():
                    order[0] = 0
                    dve.sem_clear(dve_order)

                walk(dve, "dve", run, end_pass=end_pass)


_INS = ["x", "adj", "L0_gnn_others_weight", "L0_gnn_self_weight", "L0_gnn_att_weight", "L1_gnn_Wp", "L1_gnn_bp",
        "L1_gnn_a_src", "L1_gnn_a_dst", "L1_gnn_gat_g", "L1_gnn_gat_b", "L1_gnn_eps", "L1_gnn_W1", "L1_gnn_b1",
        "L1_gnn_mlp_g", "L1_gnn_mlp_b", "L1_gnn_W2", "L1_gnn_b2", "L2_gnn_W", "L2_gnn_a", "L2_gnn_bias",
        "L3_gnn_W", "L3_gnn_e", "L3_gnn_bias"]
_OUTS = [((32, 512, 128), "float32")]


def kernel(**inputs):
    import numpy as _np
    import concourse.bacc as _bacc
    from concourse import mybir as _mybir
    from concourse.bass_utils import run_bass_kernel_spmd as _run

    nc = _bacc.Bacc("TRN2", target_bir_lowering=False, num_devices=1)
    arrays, args = {}, []
    for name in _INS:
        a = _np.ascontiguousarray(inputs[name])
        arrays[f"in_{name}_dram"] = a
        args.append(nc.dram_tensor(f"in_{name}_dram", a.shape, _mybir.dt.from_np(a.dtype), kind="ExternalInput").ap())
    for i, (shape, dtype) in enumerate(_OUTS):
        dt = _mybir.dt.from_np(_np.dtype(dtype))
        args.append(nc.dram_tensor(f"out_{i}_dram", shape, dt, kind="ExternalOutput").ap())
    gnn_kernel(nc, *args)
    r = _run(nc, [arrays], core_ids=[0])
    got = tuple(r.results[0][f"out_{i}_dram"] for i in range(len(_OUTS)))
    return got[0]
```

```python
from contextlib import ExitStack

import concourse.bass as bass
from concourse import mybir

P = 128
ALU = mybir.AluOpType
ACT = mybir.ActivationFunctionType
F32 = mybir.dt.float32
F32R = mybir.dt.float32r
I32 = mybir.dt.int32
AX_X = mybir.AxisListType.X
RMAX = bass.bass_isa.ReduceOp.max

NS = 4
G = 2
SLOTS = 4
RING = 2
LN_EPS = 1e-5
NEG = -9000000000000000.0
TINY = 1e-30
HUGE = 1e30

WINDOW = 61.72
PLAN = [
    ("load", 0, {"sp": -10.67}),
    ("stat0", 0, {"dve": 0, "pool": 2.65}),
    ("scale0", 0, {"act": 5.29}),
    ("norm0", 1, {"pe": 10.24, "act": 11.31}),
    ("coef0", 1, {"pe": 12.54, "dve": 14.34, "pool": 15.29}),
    ("feat0", 1, {"pe": 20.19}),
    ("coefm0", 0, {"dve": 21.19}),
    ("coefb0", 1, {"act": 22.06, "pe": 22.49, "dve": 25.44}),
    ("split0", 0, {"dve": 27.14, "act": 28.49}),
    ("low0", 0, {"pool": 34.04}),
    ("agg0", 1, {"pe": 39.24, "dve": 42.62}),
    ("self0", 1, {"pe": 42.89, "dve": 48.42}),
    ("stat1", 0, {"dve": 50.92, "pool": 53.57}),
    ("norm1", 1, {"dve": 54.57, "pool": 55.87, "pe": 59.18, "act": 60.33}),
    ("feat1", 2, {"pe": 66.21, "act": 70.11, "dve": 71.26, "pool": 72.22}),
    ("score1", 0, {"dve": 72.36, "act": 73.98}),
    ("turn1", 1, {"dve": 73.99, "pe": 76.29, "act": 76.66}),
    ("spread1", 1, {"pe": 78.18, "act": 79.98}),
    ("att1a", 1, {"act": 80.93, "dve": 84.51, "pe": 87.55}),
    ("att1b", 1, {"act": 85.61, "dve": 93.66, "pe": 96.59}),
    ("collect1a", 0, {"act": 92.11}),
    ("collect1b", 0, {"act": 100.29}),
    ("gats1", 0, {"dve": 101.04, "pool": 104.49}),
    ("gat1", 0, {"dve": 106.34, "pool": 108.69, "act": 113.54}),
    ("gatl1", 0, {"dve": 115.14}),
    ("gin1", 1, {"pe": 116.64, "act": 121.1}),
    ("mlpa1", 1, {"pe": 122.33, "act": 125.85}),
    ("mlps1", 0, {"dve": 128.65, "pool": 133.93}),
    ("mlpb1", 1, {"dve": 131.05, "pool": 135.63, "pe": 138.16, "act": 140.1}),
    ("mlpc1", 1, {"pe": 141.5, "dve": 145.08, "act": 146.38, "pool": 147.48}),
    ("stat2", 0, {"dve": 152.88, "pool": 155.53}),
    ("scale2", 0, {"act": 158.4}),
    ("shift2", 0, {"pool": 162.08}),
    ("norm2", 1, {"pe": 161.81, "act": 162.88}),
    ("feat2", 2, {"pe": 164.48, "act": 166.53, "dve": 167.68, "pool": 167.93}),
    ("score2", 0, {"dve": 170.26, "act": 171.11}),
    ("turn2", 1, {"dve": 171.41, "pe": 176.73, "act": 177.08}),
    ("spread2", 1, {"pe": 177.56, "act": 178.56}),
    ("att2a", 1, {"act": 179.51, "dve": 182.51, "pe": 186.15}),
    ("att2b", 1, {"act": 184.72, "dve": 187.72, "pe": 191.9}),
    ("collect2a", 0, {"act": 189.85}),
    ("collect2b", 0, {"act": 195.6}),
    ("elud2", 0, {"dve": 196.5}),
    ("elu2", 0, {"act": 199.15, "dve": 200.3}),
    ("stat3", 0, {"dve": 202.7, "pool": 205.35}),
    ("norm3", 1, {"dve": 205.2, "pool": 207.05, "pe": 209.25, "act": 211.9}),
    ("shift3", 0, {"pool": 211.5}),
    ("feat3", 2, {"pe": 215.32, "act": 219.12, "dve": 220.27}),
    ("agg3", 1, {"pe": 233.25, "dve": 240.88}),
    ("store", 0, {"sp": 242.18}),
]


def bcast(ap, n):
    return ap.unsqueeze(2).to_broadcast([ap.shape[0], ap.shape[1], n])


def wide(ap):
    return ap.to_broadcast([ap.shape[0], P])


def repeat(ap, n):
    return ap.unsqueeze(1).to_broadcast([ap.shape[0], n, ap.shape[1]])


def gnn_kernel(nc, x, adj, Wo_d, Ws_d, att0_d, Wp_d, bp_d, asrc_d, adst_d, gatg_d, gatb_d, eps_d, W1_d, b1_d,
               mlpg_d, mlpb_d, W2_d, b2_d, Wq_d, att2_d, bias2_d, W3_d, e_d, bias3_d, out):
    B, N, F = x.shape
    T = N // P
    TG = T * G
    HALF = T // 2
    WD = F + 2
    GROUPS = B // G
    NE = e_d.shape[1]
    MB = NE // P
    assert F == P and G == 2 and T == 4 and B % G == 0 and TG * F == 1024

    ctx = ExitStack()
    with ctx:
        def sb(name, shape, dt=F32, stack=ctx):
            return stack.enter_context(nc.sbuf_tensor(name, shape, dt))

        def sem(name):
            return ctx.enter_context(nc.semaphore(name))

        ps = [ctx.enter_context(nc.psum_tensor(f"ps{i}", [P, 1024], F32)) for i in range(SLOTS)]

        ident = sb("ident", [P, P])
        ones = sb("ones", [P, P])
        minus_half = sb("minus_half", [P, TG])
        adj_top = sb("adj_top", [P, HALF, N])
        maskT = sb("maskT", [P, T, N], F32R)
        mask0b = sb("mask0b", [P, T, N // 2], F32R)
        empty0 = sb("empty0", [P, T], F32R)
        mask2 = sb("mask2", [P, T, N])
        rescue8 = sb("rescue8", [P, TG])
        both8 = sb("both8", [P, TG], F32R)
        gin_hi = sb("gin_hi", [P, T, N], F32R)
        gin_lo = sb("gin_lo", [P, T, P], F32R)
        a3_hi = sb("a3_hi", [P, T, N], F32R)
        a3_lo = sb("a3_lo", [P, T, N], F32R)
        diag3 = sb("diag3", [P, T])
        Wo, Ws, W1, W2 = (sb(n, [P, F]) for n in ("Wo", "Ws", "W1", "W2"))
        W3 = sb("W3", [P, 2, F])
        wcols0 = sb("wcols0", [P, 4])
        feat1w = sb("feat1w", [P, WD])
        feat2w = sb("feat2w", [P, WD])
        const1 = sb("const1", [P, 1])
        pick = sb("pick", [P, P], F32R)
        bias_p = sb("bias_p", [P, WD], F32R)
        bias_1 = sb("bias_1", [P, F], F32R)
        bias_2 = sb("bias_2", [P, F], F32R)
        gat_g, gat_b, bias2, bias3 = (sb(n, [P, F]) for n in ("gat_g", "gat_b", "bias2", "bias3"))
        mlp_g, mlp_b = sb("mlp_g", [P, 1]), sb("mlp_b", [P, 1])
        XL = sb("XL", [P, TG, F])
        low8 = sb("low8", [P, TG])
        empty8 = sb("empty8", [P, TG])
        full8 = sb("full8", [P, TG])
        share8 = sb("share8", [P, TG])

        loaded = sem("loaded")
        adj_loaded = sem("adj_loaded")
        POOL_SETUP = 10
        made = {n: sem("made_" + n) for n in (
            "pool", "adjn", "maskT", "turn", "WT_ps", "WT", "rowtot", "bprep", "wvec", "rank_ps", "rank", "counts",
            "off", "row_of", "offm", "edges_ps", "edge_rows", "at", "cover", "values", "left3", "nmax", "exp3",
            "soft3", "turn3", "a3_hi", "gin_hi", "cast_hi")}
        dve_order = sem("dve_order")
        act_order = sem("act_order")
        pool_order = sem("pool_order")

        order = {e: sorted((when[e] % WINDOW, int(when[e] // WINDOW), name) for name, _, when in PLAN if e in when)
                 for e in ("pe", "act", "pool", "dve", "sp")}
        parts = {(name, e): int(when[e] // WINDOW) for name, _, when in PLAN for e in when}
        tiles_of = {name: n for name, n, _ in PLAN}
        LOOP_FIRST = max(parts.values())
        LOOPS = (GROUPS - 1 - LOOP_FIRST) // NS
        LAST = GROUPS + LOOP_FIRST

        tile_at, mat_at = {}, {}
        tiles = mats = 0
        for _, _, name in order["pe"]:
            tile_at[name] = tiles
            tiles += tiles_of[name]
        for _, _, name in order["act"]:
            if name.startswith("att"):
                mat_at[name] = mats
                mats += 1
        assert tiles % SLOTS == 0 and mats % RING == 0

        class Step:

            def __init__(self, name, w, part, it):
                self.name, self.w, self.part, self.it = name, w, part, it
                self.s = (w - part) % NS
                self.g = self.linear(1, (w - part) // NS)
                self.group = w - part if it is None else None

            def linear(self, per_loop, n):
                return n if self.it is None else self.it * per_loop + n

            def all_groups(self, per_group, n):
                return self.linear(NS * per_group, (self.w - self.part) * per_group + n)

            def ring(self, used, n, size):
                return n % size, self.linear(NS * used // size, n // size)

            def tile(self, name, n=0):
                w = self.w - self.part + parts[name, "pe"]
                return self.ring(tiles, w * tiles + tile_at[name] + n, SLOTS)

            def matrix(self, name):
                w = self.w - self.part + parts[name, "act"]
                return self.ring(mats, w * mats + mat_at[name], RING)

        def walk(core, e, run, skip=None, end_pass=None):
            def window(w, it=None):
                for _, part, name in order[e]:
                    u = Step(name, w, part, it)
                    if it is not None or 0 <= w - part < GROUPS:
                        run[name](u, u.s)
                    elif skip is not None and w >= 0:
                        skip(u)

            for w in range(-1, LOOP_FIRST):
                window(w)
            if end_pass is not None:
                end_pass()
            with core.Fori(0, LOOPS) as it:
                for w in range(LOOP_FIRST, LOOP_FIRST + NS):
                    window(w, it)
                if end_pass is not None:
                    end_pass()
            for w in range(LOOP_FIRST + NS * LOOPS, LAST):
                window(w)


        def count(it, per_group, n):
            return it * per_group + (n + 1)

        full = [sem(f"psum_full{i}") for i in range(SLOTS)]
        taken = [sem(f"psum_taken{i}") for i in range(SLOTS)]
        p_full = [sem(f"matrix_full{i}") for i in range(RING)]
        p_taken = [sem(f"matrix_taken{i}") for i in range(RING)]
        sig = {n: [sem(f"{n}_{s}") for s in range(NS)] for n in (
            "result", "stored", "var", "rstd", "normed", "cmax", "cmax_all", "cdiff", "cexp",
            "scaled", "hi", "lo", "lo_below", "dmax", "dmax_all", "ddiff", "dexp", "r_split", "raised", "gated",
            "eluexp", "shifted", "centred", "mlp_relu", "x_added")}
        x_loaded = sem("x_loaded")
        raw_free = sem("raw_free")

        RT = [sb(f"RT{s}", [P, P], F32R) for s in range(NS)]

        with ExitStack() as sc:
            adj_raw = sb("adj_raw", [P, T, N], F32, sc)
            adjn = sb("adjn", [P, T, N], F32R, sc)
            upper = sb("upper", [P, T, N], F32R, sc)
            ones_r = sb("ones_r", [P, P], F32R, sc)
            strict = sb("strict", [P, T, N], F32R, sc)
            rank = sb("rank", [P, T, N], F32R, sc)
            row_of = sb("row_of", [P, MB, N], F32R, sc)
            row_ofT = sb("row_ofT", [P, T, NE], F32R, sc)
            at = sb("at", [P, MB, N], F32R, sc)
            e_at_hi = sb("e_at_hi", [P, MB, N], F32R, sc)
            e_at_lo = sb("e_at_lo", [P, MB, N], F32R, sc)
            v3 = sb("v3", [P, T, N], F32, sc)
            work = sb("work", [P, T, N], F32, sc)
            WoT, WpT, WqT = (sb(n, [P, F], F32, sc) for n in ("WoT", "WpT", "WqT"))
            bprep = sb("bprep", [P, P], F32, sc)
            rowtot_b = sb("rowtot_b", [P, N], F32, sc)
            norow = sb("norow", [P, N], F32, sc)
            off_b = sb("off_b", [P, N], F32, sc)
            cntrep = sb("cntrep", [P, T, P], F32R, sc)
            att0, asd, att2 = (sb(n, [P, 2], F32, sc) for n in ("att0", "asd", "att2"))
            bpcol, epscol, e255 = (sb(n, [P, 1], F32, sc) for n in ("bpcol", "epscol", "e255"))
            e_col = sb("e_col", [P, MB], F32, sc)
            e_hi = sb("e_hi", [P, MB], F32R, sc)
            e_lo = sb("e_lo", [P, MB], F32R, sc)
            brow = sb("brow", [P, 3, F], F32, sc)
            bhi = sb("bhi", [P, 3, F], F32R, sc)
            blo = sb("blo", [P, 3, F], F32R, sc)
            m_int = sb("m_int", [P, NE], I32, sc)
            mc_int = sb("mc_int", [P, MB], I32, sc)
            m_row = sb("m_row", [P, NE], F32, sc)
            m_col = sb("m_col", [P, MB], F32, sc)
            cnt_row = sb("cnt_row", [P, T], F32, sc)
            off_col = sb("off_col", [P, T], F32, sc)
            end_col = sb("end_col", [P, T], F32, sc)
            m_loc = sb("m_loc", [P, MB], F32, sc)
            cnt_all = sb("cnt_all", [P, T], F32, sc)
            cnt_low = sb("cnt_low", [P, T], F32, sc)
            empty4 = sb("empty4", [P, T], F32, sc)
            asum = sb("asum", [P, 1], F32, sc)
            epsd = sb("epsd", [P, P], F32, sc)
            diagv = sb("diagv", [P, T, P], F32, sc)
            small = sb("small", [P, 8], F32, sc)
            rmax = sb("rmax", [P, T], F32, sc)
            rsum = sb("rsum", [P, T], F32, sc)
            rinv = sb("rinv", [P, T], F32, sc)
            wv = sb("wv", [P, 8], F32, sc)

            LOADS = [(Wo[:], Wo_d), (Ws[:], Ws_d), (feat1w[:, 0:F], Wp_d), (W1[:], W1_d), (W2[:], W2_d), (feat2w[:, 0:F], Wq_d),
                     (W3[:], W3_d.rearrange("k f g -> f k g")),
                     (att0[:, 0:1], att0_d[0:P, :]), (att0[:, 1:2], att0_d[P:2 * P, :]),
                     (att2[:, 0:1], att2_d[0:P, :]), (att2[:, 1:2], att2_d[P:2 * P, :]),
                     (asd[:, 0:1], asrc_d.rearrange("(p o) -> p o", o=1)),
                     (asd[:, 1:2], adst_d.rearrange("(p o) -> p o", o=1)),
                     (bpcol[:], bp_d.rearrange("(p o) -> p o", o=1)),
                     (mlp_g[:], mlpg_d.rearrange("(p o) -> p o", o=1)),
                     (mlp_b[:], mlpb_d.rearrange("(p o) -> p o", o=1)),
                     (brow[:, 0, :], bp_d.partition_broadcast(P)),
                     (brow[:, 1, :], b1_d.partition_broadcast(P)),
                     (brow[:, 2, :], b2_d.partition_broadcast(P)),
                     (gat_g[:], gatg_d.partition_broadcast(P)), (gat_b[:], gatb_d.partition_broadcast(P)),
                     (bias2[:], bias2_d.partition_broadcast(P)), (bias3[:], bias3_d.partition_broadcast(P)),
                     (epscol[:], eps_d.partition_broadcast(P)),
                     (e255[:], e_d[0, NE - 1:NE].partition_broadcast(P)),
                     *[(e_col[:, m:m + 1], e_d[0, m * P:(m + 1) * P].rearrange("(p o) -> p o", o=1))
                       for m in range(MB)]]

            with nc.Block() as block:
                @block.sync
                def _(sp):
                    for t in range(T):
                        sp.dma_start(adj_raw[:, t, :], adj[t * P:(t + 1) * P, :]).then_inc(adj_loaded, 16)
                    for dst, src in LOADS:
                        sp.dma_start(dst, src).then_inc(loaded, 16)
                    for b in range(G):
                        sp.dma_start(XL[:, b::G, :], x.rearrange("b (t p) f -> b p t f", p=P)[b]).then_inc(x_loaded, 16)
                    for s in taken + p_taken:
                        sp.sem_inc(s, 1)
                    for s in sig["stored"]:
                        sp.sem_inc(s, 16)
                    sp.wait_ge(loaded, 16 * len(LOADS))

                @block.gpsimd
                def _(pool):
                    nc.gpsimd.memset(ident[:], 0.0).then_inc(made["pool"], 1)
                    nc.gpsimd.memset(ones[:], 1.0).then_inc(made["pool"], 1)
                    nc.gpsimd.memset(work[:], 1.0).then_inc(made["pool"], 1)
                    nc.gpsimd.memset(minus_half[:], -0.5).then_inc(made["pool"], 1)
                    nc.gpsimd.memset(ones_r[:].bitcast(F32), 1.0).then_inc(made["pool"], 1)
                    pool.wait_ge(made["pool"], 5)
                    nc.gpsimd.affine_select(out=ident[:], in_=ident[:], compare_op=ALU.not_equal, fill=1.0, base=0,
                                            pattern=[[-1, P]], channel_multiplier=1).then_inc(made["pool"], 1)
                    nc.gpsimd.affine_select(out=upper[:], in_=work[:], compare_op=ALU.is_ge, fill=0.0, base=0,
                                            pattern=[[-P, T], [1, N]], channel_multiplier=-1).then_inc(made["pool"], 1)
                    nc.gpsimd.affine_select(out=strict[:], in_=work[:], compare_op=ALU.is_gt, fill=0.0, base=0,
                                            pattern=[[-P, T], [1, N]], channel_multiplier=-1).then_inc(made["pool"], 1)
                    nc.gpsimd.iota(m_int[:], [[1, NE]], base=0, channel_multiplier=0).then_inc(made["pool"], 1)
                    nc.gpsimd.iota(mc_int[:], [[P, MB]], base=0, channel_multiplier=1).then_inc(made["pool"], 1)

                @block.tensor
                def _(pe):
                    T_, MM = nc.tensor.transpose, nc.tensor.matmul
                    pe.wait_ge(made["adjn"], 1)
                    pe.wait_ge(made["pool"], POOL_SETUP)
                    for j in range(T):
                        for i in range(T):
                            o = (j % 2) * N + i * P
                            mm = T_(ps[j // 2][:, o:o + P], adjn[:, i, j * P:(j + 1) * P].bitcast(F32), ident[:])
                    mm.then_inc(made["turn"], 1)
                    pe.wait_ge(made["maskT"], 1)
                    for j in range(T):
                        mm = MM(ps[3][:, 0:N], ones_r[:], maskT[:, j, :], start=(j == 0), stop=(j == T - 1))
                    mm.then_inc(made["rowtot"], 1)
                    for i in range(T):
                        for j in range(T):
                            mm = MM(ps[i // 2][:, (i % 2) * N:(i % 2) * N + N], maskT[:, j, i * P:(i + 1) * P],
                                    upper[:, j, :], start=(j == 0), stop=(j == T - 1))
                    mm.then_inc(made["rank_ps"], 1)
                    pe.wait_ge(made["counts"], 1)
                    for i in range(T):
                        for k in range(T):
                            MM(ps[2][:, 16 + i:17 + i], strict[:, k, i * P:(i + 1) * P].bitcast(F32), cnt_row[:, k:k + 1],
                               start=(k == 0), stop=(k == T - 1))
                    for k in range(T):
                        mm = MM(ps[3][:, N:2 * N], cntrep[:, k, :], strict[:, k, :], start=(k == 0), stop=(k == T - 1))
                    mm.then_inc(made["off"], 1)
                    pe.wait_ge(loaded, 16 * len(LOADS))
                    for n, w in enumerate((Wo, feat1w, feat2w)):
                        mm = T_(ps[2][:, N + n * P:N + (n + 1) * P], w[:, 0:F], ident[:])
                    mm.then_inc(made["WT_ps"], 1)
                    pe.wait_ge(made["bprep"], 1)
                    pe.wait_ge(made["WT"], 1)
                    MM(ps[2][:, 896:898], WoT[:], att0[:], start=True, stop=True)
                    MM(ps[2][:, 898:900], WpT[:], asd[:], start=True, stop=True)
                    MM(ps[2][:, 900:902], WqT[:], att2[:], start=True, stop=True)
                    MM(ps[2][:, 902:903], bprep[:], asum[:], start=True, stop=True).then_inc(made["wvec"], 1)
                    pe.wait_ge(made["row_of"], 1)
                    for m in range(MB):
                        for i in range(T):
                            mm = MM(ps[2][:, 32 + m:33 + m], row_ofT[:, i, m * P:(m + 1) * P].bitcast(F32),
                                    off_col[:, i:i + 1], start=(i == 0), stop=(i == T - 1))
                    mm.then_inc(made["offm"], 1)
                    pe.wait_ge(made["rank"], 1)
                    for t, src in enumerate((adjn, rank)):
                        for m in range(MB):
                            for i in range(T):
                                mm = MM(ps[t][:, m * N:(m + 1) * N], row_ofT[:, i, m * P:(m + 1) * P], src[:, i, :],
                                        start=(i == 0), stop=(i == T - 1))
                    mm.then_inc(made["edges_ps"], 1)
                    pe.wait_ge(made["at"], 1)
                    for srcs, tile0, name in (((at,), 2, "cover"), ((e_at_hi, e_at_lo), 0, "values")):
                        if name == "values":
                            pe.wait_ge(made["at"], 2)
                        for i in range(T):
                            terms = [(m, src) for m in range(MB) for src in srcs]
                            for n, (m, src) in enumerate(terms):
                                mm = MM(ps[tile0 + i // 2][:, (i % 2) * N:(i % 2) * N + N],
                                        row_of[:, m, i * P:(i + 1) * P], src[:, m, :],
                                        start=(n == 0), stop=(n == len(terms) - 1))
                        mm.then_inc(made[name], 1)
                    pe.wait_ge(made["soft3"], 1)
                    for j in range(T):
                        for i in range(T):
                            o = (j % 2) * N + i * P
                            mm = T_(ps[j // 2][:, o:o + P], v3[:, i, j * P:(j + 1) * P], ident[:])
                    mm.then_inc(made["turn3"], 1)

                @block.scalar
                def _(act):
                    A = nc.scalar.activation
                    act.wait_ge(made["turn"], 1)
                    A(maskT[:, 0:2, :], ps[0][:].rearrange("p (a n) -> p a n", a=2), ACT.Copy)
                    A(maskT[:, 2:4, :], ps[1][:].rearrange("p (a n) -> p a n", a=2), ACT.Copy).then_inc(made["maskT"], 1)
                    act.wait_ge(made["maskT"], 1)
                    A(gin_hi[:], maskT[:].bitcast(F32), ACT.Copy).then_inc(made["gin_hi"], 1)
                    act.wait_ge(made["rank_ps"], 1)
                    A(rank[:, 0:2, :], ps[0][:].rearrange("p (a n) -> p a n", a=2), ACT.Copy)
                    A(rank[:, 2:4, :], ps[1][:].rearrange("p (a n) -> p a n", a=2), ACT.Copy).then_inc(made["rank"], 1)
                    act.wait_ge(made["WT_ps"], 1)
                    for n, w in enumerate((WoT, WpT, WqT)):
                        a = A(w[:], ps[2][:, N + n * P:N + (n + 1) * P], ACT.Copy)
                    a.then_inc(made["WT"], 1)
                    act.wait_ge(made["edges_ps"], 1)
                    act.wait_ge(made["row_of"], 1)
                    A(at[:], ps[0][:].rearrange("p (m n) -> p m n", m=MB), ACT.Copy).then_inc(made["edge_rows"], 1)
                    act.wait_ge(made["nmax"], 1)
                    for i in range(T):
                        a = A(work[:, i, :], v3[:, i, :], ACT.Exp, bias=rmax[:, i:i + 1], accum_out=rsum[:, i:i + 1])
                    a.then_inc(made["exp3"], 1)
                    act.wait_ge(made["turn3"], 1)
                    A(a3_hi[:, 0:2, :], ps[0][:].rearrange("p (a n) -> p a n", a=2), ACT.Copy)
                    A(a3_hi[:, 2:4, :], ps[1][:].rearrange("p (a n) -> p a n", a=2), ACT.Copy).then_inc(made["a3_hi"], 1)

                @block.vector
                def _(dve):
                    V = nc.vector
                    order = [0]

                    def link(ins):
                        order[0] += 1
                        ins.then_inc(dve_order, 1)
                        dve.wait_ge(dve_order, order[0])

                    dve.wait_ge(adj_loaded, 16 * T)
                    V.tensor_scalar(adjn[:], adj_raw[:], 0.0, None, ALU.is_gt).then_inc(made["adjn"], 1)
                    dve.wait_ge(made["pool"], POOL_SETUP)
                    dve.wait_ge(made["adjn"], 1)
                    V.tensor_copy(adj_top[:], adjn[:, 0:HALF, :].bitcast(F32))
                    V.tensor_copy(m_row[:], m_int[:])
                    V.tensor_copy(m_col[:], mc_int[:])
                    link(V.reduce_sum(cnt_row[:], adjn[:].bitcast(F32), AX_X))
                    for k in range(T):
                        a = V.tensor_scalar(cntrep[:, k, :], ones[:], cnt_row[:, k:k + 1], None, ALU.mult)
                    a.then_inc(made["counts"], 1)
                    dve.wait_ge(made["maskT"], 1)
                    mT = maskT[:].bitcast(F32)
                    V.reduce_sum(cnt_low[:], mT[:, :, N // 2:N], AX_X)
                    link(V.reduce_sum(cnt_all[:], mT, AX_X))
                    link(V.tensor_scalar(empty4[:], cnt_all[:], 0.0, None, ALU.is_equal))
                    for k in range(T):
                        V.tensor_scalar(mask0b[:, k, :], mT[:, k, N // 2:N], empty4[:, k:k + 1], None, ALU.max)
                    V.tensor_copy(empty0[:], empty4[:])
                    e4, l4 = bcast(empty4[:], G), bcast(cnt_low[:], G)
                    v8 = [t[:].rearrange("p (k b) -> p k b", b=G) for t in (low8, empty8, full8, share8)]
                    V.tensor_copy(v8[0], l4)
                    V.tensor_copy(v8[1], e4)
                    V.tensor_scalar(v8[2], e4, -1.0, 1.0, ALU.mult, ALU.add)
                    V.tensor_scalar(v8[3], e4, 1.0 / N, None, ALU.mult)
                    dve.wait_ge(loaded, 16 * len(LOADS))
                    V.tensor_tensor(asum[:], asd[:, 0:1], asd[:, 1:2], ALU.add)
                    V.tensor_scalar(bprep[:], ones[:], bpcol[:, 0:1], None, ALU.mult).then_inc(made["bprep"], 1)
                    V.tensor_copy(e_hi[:], e_col[:])
                    link(V.tensor_copy(bhi[:], brow[:]))
                    V.tensor_tensor(e_lo[:], e_col[:], e_hi[:].bitcast(F32), ALU.subtract)
                    V.tensor_tensor(blo[:], brow[:], bhi[:].bitcast(F32), ALU.subtract)
                    V.memset(pick[:].bitcast(F32), 0.0)
                    V.memset(bias_p[:].bitcast(F32), 0.0)
                    V.memset(bias_1[:].bitcast(F32), 0.0)
                    link(V.memset(bias_2[:].bitcast(F32), 0.0))
                    for p0, src in ((0, bhi), (32, blo)):
                        row = slice(p0, p0 + 1)
                        V.tensor_copy(pick[row, :], ones[row, :])
                        V.tensor_copy(bias_p[row, 0:F], src[row, 0, :].bitcast(F32))
                        V.tensor_copy(bias_1[row, :], src[row, 1, :].bitcast(F32))
                        V.tensor_copy(bias_2[row, :], src[row, 2, :].bitcast(F32))
                    link(V.tensor_scalar(small[:, 0:1], epscol[:], 1.0, None, ALU.add))
                    link(V.tensor_scalar(epsd[:], ident[:], small[:, 0:1], None, ALU.mult))
                    for k in range(T):
                        a = V.tensor_tensor(diagv[:, k, :], mT[:, k, k * P:(k + 1) * P], epsd[:], ALU.add)
                    link(a)
                    dve.wait_ge(made["gin_hi"], 1)
                    for k in range(T):
                        a = V.tensor_copy(gin_hi[:, k, k * P:(k + 1) * P], diagv[:, k, :])
                    link(a)
                    for k in range(T):
                        V.tensor_tensor(gin_lo[:, k, :], diagv[:, k, :], gin_hi[:, k, k * P:(k + 1) * P].bitcast(F32),
                                        ALU.subtract)
                    dve.wait_ge(made["rowtot"], 1)
                    V.tensor_copy(rowtot_b[:], ps[3][:, 0:N])
                    link(V.tensor_scalar(norow[:], ps[3][:, 0:N], 0.0, None, ALU.is_equal))
                    for k in range(T):
                        V.tensor_tensor(mask2[:, k, :], mT[:, k, :], norow[:], ALU.max)
                    V.tensor_scalar(rescue8[:].rearrange("p (t b) -> p t b", b=G), bcast(cnt_row[:], G), 0.0, HUGE,
                                    ALU.is_equal, ALU.mult)
                    V.tensor_tensor(both8[:], ident[:, 0:TG], ident[:, TG:2 * TG], ALU.add)
                    for s in range(NS):
                        V.memset(RT[s][:].bitcast(F32), 0.0)
                    dve.wait_ge(made["off"], 1)
                    V.tensor_copy(off_col[:], ps[2][:, 16:16 + T])
                    link(V.tensor_copy(off_b[:], ps[3][:, N:2 * N]))
                    V.tensor_tensor(end_col[:], off_col[:], cnt_row[:], ALU.add)
                    link(V.tensor_tensor(rowtot_b[:], rowtot_b[:], off_b[:], ALU.add))
                    for i in range(T):
                        V.tensor_scalar(v3[:, i, 0:NE], m_row[:], end_col[:, i:i + 1], None, ALU.is_ge)
                    for m in range(MB):
                        a = V.tensor_scalar(at[:, m, :], rowtot_b[:], m_col[:, m:m + 1], None, ALU.is_le)
                    link(a)
                    for i in range(T):
                        V.scalar_tensor_tensor(out=row_ofT[:, i, :], in0=m_row[:], scalar=off_col[:, i:i + 1],
                                               in1=v3[:, i, 0:NE], op0=ALU.is_ge, op1=ALU.subtract)
                    for m in range(MB):
                        a = V.scalar_tensor_tensor(out=row_of[:, m, :], in0=off_b[:], scalar=m_col[:, m:m + 1],
                                                   in1=at[:, m, :].bitcast(F32), op0=ALU.is_le,
                                                   op1=ALU.subtract)
                    a.then_inc(made["row_of"], 1)
                    dve.wait_ge(made["wvec"], 1)
                    V.tensor_copy(const1[:], ps[2][:, 902:903])
                    link(V.tensor_copy(wv[:, 0:6], ps[2][:, 896:902]))
                    V.tensor_tensor(wcols0[:, 0:1], wv[:, 0:1], wv[:, 1:2], ALU.add)
                    V.tensor_copy(wcols0[:, 1:3], wv[:, 0:2])
                    V.memset(wcols0[:, 3:4], 0.0)
                    V.tensor_copy(feat1w[:, F:F + 1], wv[:, 3:4])
                    V.tensor_copy(feat1w[:, F + 1:F + 2], wv[:, 2:3])
                    V.tensor_copy(feat2w[:, F:F + 1], wv[:, 5:6])
                    V.tensor_copy(feat2w[:, F + 1:F + 2], wv[:, 4:5])
                    dve.wait_ge(made["offm"], 1)
                    link(V.scalar_tensor_tensor(out=m_loc[:], in0=ps[2][:, 32:32 + MB], scalar=-1.0, in1=m_col[:],
                                                op0=ALU.mult, op1=ALU.add))
                    link(V.tensor_scalar(m_loc[:], m_loc[:], 1.0, None, ALU.add))
                    dve.wait_ge(made["edge_rows"], 1)
                    for m in range(MB):
                        a = V.scalar_tensor_tensor(out=at[:, m, :], in0=ps[1][:, m * N:(m + 1) * N],
                                                   scalar=m_loc[:, m:m + 1], in1=at[:, m, :].bitcast(F32),
                                                   op0=ALU.is_equal, op1=ALU.mult)
                    a.then_inc(made["at"], 1)
                    dve.wait_ge(made["at"], 1)
                    for m in range(MB):
                        for dst, src in ((e_at_hi, e_hi), (e_at_lo, e_lo)):
                            a = V.tensor_scalar(dst[:, m, :], at[:, m, :].bitcast(F32),
                                                src[:, m:m + 1].bitcast(F32), None, ALU.mult)
                    a.then_inc(made["at"], 1)
                    dve.wait_ge(made["cover"], 1)
                    for h in range(2):
                        a = V.tensor_tensor(v3[:, 2 * h:2 * h + 2, :], adjn[:, 2 * h:2 * h + 2, :].bitcast(F32),
                                            ps[2 + h][:].rearrange("p (a n) -> p a n", a=2), ALU.subtract)
                    link(a)
                    dve.wait_ge(made["values"], 1)
                    for i in range(T):
                        a = V.scalar_tensor_tensor(out=v3[:, i, :], in0=v3[:, i, :], scalar=e255[:, 0:1],
                                                   in1=ps[i // 2][:, (i % 2) * N:(i % 2) * N + N], op0=ALU.mult,
                                                   op1=ALU.add)
                    V.tensor_scalar(work[:], adjn[:].bitcast(F32), -1.0, -NEG, ALU.add, ALU.mult)
                    link(V.memset(small[:, 2:3], 0.0))
                    link(V.tensor_tensor(v3[:], v3[:], work[:], ALU.add))
                    link(V.reduce_max(rmax[:], v3[:], AX_X))
                    V.tensor_scalar(rmax[:], rmax[:], -1.0, None, ALU.mult).then_inc(made["nmax"], 1)
                    dve.wait_ge(made["exp3"], 1)
                    link(V.reciprocal(rinv[:], rsum[:]))
                    link(V.tensor_tensor(v3[:], work[:], bcast(rinv[:], N), ALU.mult))
                    for i in range(T):
                        a = V.tensor_tensor(diagv[:, i, :], v3[:, i, i * P:(i + 1) * P], ident[:], ALU.mult)
                    link(a)
                    V.reduce_sum(diag3[:], diagv[:], AX_X)
                    for i in range(T):
                        a = V.tensor_tensor(v3[:, i, i * P:(i + 1) * P], v3[:, i, i * P:(i + 1) * P], diagv[:, i, :],
                                            ALU.subtract)
                    a.then_inc(made["soft3"], 1)
                    dve.wait_ge(made["a3_hi"], 1)
                    for h in range(2):
                        V.tensor_tensor(a3_lo[:, 2 * h:2 * h + 2, :], ps[h][:].rearrange("p (a n) -> p a n", a=2),
                                        a3_hi[:, 2 * h:2 * h + 2, :].bitcast(F32), ALU.subtract)
                    dve.sem_clear(dve_order)

        def per(name, shape, dt=F32):
            return [sb(f"{name}{s}", shape, dt) for s in range(NS)]

        X = per("X", [P, TG, F])
        Y = per("Y", [P, TG, WD])
        HT = per("HT", [P, G, N])
        HE = per("HE", [P, TG, WD])
        SC = per("SC", [P, TG, F])
        HI = per("HI", [P, TG, F], F32R)
        LO = per("LO", [P, TG, F], F32R)
        VA = [he[:, :, 0:F] for he in HE]

        def R(s):
            return SC[s][:].rearrange("p (b t) f -> p b (t f)", b=G)

        HIB = sb("HIB", [P, TG, F], F32R)
        LOB = sb("LOB", [P, TG, F], F32R)
        ST = per("ST", [P, TG, 6])
        US = per("US", [P, TG, 4])
        CD = per("CD", [P, 12])
        CF = per("CF", [P, 3 * TG])
        CE = per("CE", [P, 3 * TG])
        NF = per("NF", [P, TG])
        R2 = per("R2", [P, 2 * TG], F32R)
        MX = per("MX", [P, 8])
        SM = per("SM", [P, 16, TG])
        PT = [sb(f"PT{r}", [P, T, N]) for r in range(RING)]
        S_SUM, S_DIF, S_Q, S_DD, S_VAR, S_MEAN, S_RSTD, S_INV, S_RS, S_A, S_B, S_Z, S_SHIFT = range(13)

        LNS = ["norm0", "norm1", "gat1", "mlpb1", "norm2", "norm3"]
        NLN = len(LNS)
        ln_at = {n: k for k, n in enumerate(LNS)}
        NORMED = ["norm0", "norm1", "gat1", "mlpb1", "norm2", "norm3"]
        nd_at = {n: k for k, n in enumerate(NORMED)}
        ATT = {"1": 0, "2": 1}
        HIS = {"a0": 0, "b0": 1, "1": 2, "3a": 3, "3b": 4}
        LOS = {"0": 0, "1": 1, "3": 2}

        def rows_of(ap, u, b):
            return ap.rearrange("b (t p) f -> b p t f", p=P)[u.all_groups(G, b)]

        with nc.Block() as block:
            @block.sync
            def _(sp):
                def load(u, s):
                    if u.group == 0:
                        return
                    sp.wait_ge(raw_free, u.all_groups(1, 0))
                    for b in range(G):
                        sp.dma_start(XL[:, b::G, :], rows_of(x, u, b)).then_inc(x_loaded, 16)

                def store(u, s):
                    sp.wait_ge(sig["result"][s], count(u.g, 1, 0))
                    for b in range(G):
                        sp.dma_start(rows_of(out, u, b), X[s][:, b::G, :]).then_inc(sig["stored"][s], 16)

                walk(sp, "sp", {"load": load, "store": store})
                for s in range(NS):
                    sp.wait_ge(sig["stored"][s], 16 * G * ((GROUPS - s + NS - 1) // NS) + 16)

            @block.tensor
            def _(pe):
                T_ = nc.tensor.transpose

                def MM(o, w, m, start, stop):
                    return nc.tensor.matmul(o, w, m, start=start, stop=stop, skip_group_check=True)

                def open_tile(u, name, s, n=0):
                    slot, k = u.tile(name, n)
                    pe.wait_ge(taken[slot], k + 1)
                    return ps[slot], full[slot]

                def turned(u, name, s):
                    slot, k = u.tile(name, 0)
                    pe.wait_ge(taken[slot], k + 2)

                def turn_rows(u, name, s):
                    pe.wait_ge(sig["normed"][s], count(u.g, len(NORMED), nd_at[name]))
                    o, done = open_tile(u, name, s)
                    for b in range(G):
                        for t in range(T):
                            c = b * N + t * P
                            mm = T_(o[:, c:c + P], Y[s][:, t * G + b, 0:F], ident[:])
                    mm.then_inc(done, 1)

                def blk(s, b, t):
                    return HT[s][:, b, t * P:(t + 1) * P]

                def coef0(u, s):
                    turned(u, "norm0", s)
                    o, done = open_tile(u, "coef0", s, 0)
                    for t in range(HALF):
                        for odd in range(2):
                            for b in range(G):
                                c = 4 * ((t * 2 + odd) * G + b)
                                r0 = t * 2 * P + odd
                                mm = MM(o[:, c:c + 4], HT[s][:, b, r0:r0 + 2 * P - 1:2], wcols0[:], True, True)
                    mm.then_inc(done, 1)

                def coefb0(u, s):
                    pe.wait_ge(sig["cexp"][s], count(u.g, 1, 0))
                    o, done = open_tile(u, "coefb0", s)
                    for k in range(T):
                        for t in range(HALF):
                            c = (t * 2 + k // HALF) * G
                            mm = MM(o[:, k * G:(k + 1) * G], adj_top[:, t, k * P:(k + 1) * P],
                                    CE[s][:, c:c + G], t == 0, t == HALF - 1)
                    mm.then_inc(done, 1)

                def feat0(u, s):
                    o, done = open_tile(u, "feat0", s)
                    for t in range(T):
                        for b in range(G):
                            c = (t * G + b) * F
                            mm = MM(o[:, c:c + F], blk(s, b, t), Wo[:], True, True)
                    mm.then_inc(done, 1)

                def agg0(u, s):
                    pe.wait_ge(sig["lo"][s], count(u.g, len(LOS), LOS["0"]))
                    o, done = open_tile(u, "agg0", s, 0)
                    for t in range(HALF):
                        for side in range(2):
                            c = (t * 2 + side) * G * F
                            parts = [(k, m) for k in (2 * side, 2 * side + 1) for m in (HI, LO)]
                            for n, (k, m) in enumerate(parts):
                                mm = MM(o[:, c:c + G * F], maskT[:, k, t * P:(t + 1) * P],
                                        m[s][:, k * G:(k + 1) * G, :], n == 0, n == len(parts) - 1)
                    mm.then_inc(done, 1)

                def self0(u, s):
                    pe.wait_ge(sig["lo_below"][s], count(u.g, 1, 0))
                    o, done = open_tile(u, "self0", s)
                    for t in range(T):
                        c = t * G * F
                        for b in range(G):
                            MM(o[:, c + b * F:c + (b + 1) * F], blk(s, b, t), Ws[:], b == 0, False)
                        for k in range(T):
                            w = wide(empty0[:, k:k + 1]) if t < HALF else mask0b[:, k, (t - HALF) * P:(t - HALF + 1) * P]
                            for m in (HIB, LOB):
                                mm = MM(o[:, c:c + G * F], w, m[:, k * G:(k + 1) * G, :], False,
                                        k == T - 1 and m is LOB)
                    mm.then_inc(done, 1)

                def feat(u, name, s, w, bias, before):
                    turned(u, before, s)
                    for h in range(2):
                        o, done = open_tile(u, name, s, h)
                        o4 = o[:].rearrange("p (t b c) -> p t b c", t=2, b=G)
                        for tt in range(2):
                            if bias is not None:
                                MM(o4[:, tt, :, 0:WD], pick[:], repeat(bias[:], G), True, False)
                            for b in range(G):
                                mm = MM(o4[:, tt, b, 0:w.shape[1]], blk(s, b, 2 * h + tt), w,
                                        bias is None, True)
                        mm.then_inc(done, 1)

                def turn_r(u, name, s):
                    pe.wait_ge(sig["r_split"][s], count(u.g, 2, ATT[name[-1]]))
                    o, done = open_tile(u, name, s, 0)
                    T_(o[0:2 * TG, 0:P], R2[s][:].bitcast(F32), ident[:]).then_inc(done, 1)

                def spread(u, name, s):
                    turned(u, "turn" + name[-1], s)
                    o, done = open_tile(u, name, s)
                    for t in range(T):
                        for b in range(G):
                            c = b * N + t * P
                            mm = MM(o[:, c:c + P], wide(both8[:, t * G + b:t * G + b + 1]), RT[s][:], True, True)
                    mm.then_inc(done, 1)

                def attend(u, name, s, b):
                    r, k = u.matrix(name)
                    pe.wait_ge(p_full[r], k + 1)
                    o, done = open_tile(u, name, s)
                    for i in range(T):
                        for j in range(T):
                            mm = MM(o[:, i * 2 * P:i * 2 * P + F + 1], PT[r][:, j, i * P:(i + 1) * P],
                                    HE[s][:, j * G + b, 0:F + 1], j == 0, j == T - 1)
                    mm.then_inc(done, 1)

                def gin1(u, s):
                    pe.wait_ge(sig["lo"][s], count(u.g, len(LOS), LOS["1"]))
                    o, done = open_tile(u, "gin1", s)
                    for b in range(G):
                        for j in range(T):
                            for m in (HI, LO):
                                MM(o[:, b * N:(b + 1) * N], m[s][:, j * G + b, :], gin_hi[:, j, :],
                                   j == 0 and m is HI, False)
                            c = b * N + j * P
                            mm = MM(o[:, c:c + P], HI[s][:, j * G + b, :], gin_lo[:, j, :], False, j == T - 1)
                    mm.then_inc(done, 1)

                def mlp(u, name, s, w, bias, before):
                    turned(u, before, s)
                    o, done = open_tile(u, name, s)
                    for t in range(T):
                        if t % 2 == 0:
                            MM(o[:, t * G * F:(t + 2) * G * F], pick[:], repeat(bias[:], 2 * G), True, False)
                        for b in range(G):
                            c = (t * G + b) * F
                            mm = MM(o[:, c:c + F], blk(s, b, t), w[:], False, True)
                    mm.then_inc(done, 1)

                def agg3(u, s):
                    pe.wait_ge(sig["lo"][s], count(u.g, len(LOS), LOS["3"]))
                    o, done = open_tile(u, "agg3", s)
                    for t in range(T):
                        c = t * G * F
                        parts = [(k, w, m) for k in range(T) for w, m in ((a3_hi, HI), (a3_hi, LO), (a3_lo, HI))]
                        for n, (k, w, m) in enumerate(parts):
                            mm = MM(o[:, c:c + G * F], w[:, k, t * P:(t + 1) * P], m[s][:, k * G:(k + 1) * G, :],
                                    n == 0, n == len(parts) - 1)
                    mm.then_inc(done, 1)

                run = {
                    "coef0": coef0, "coefb0": coefb0, "feat0": feat0, "agg0": agg0, "self0": self0, "gin1": gin1, "agg3": agg3,
                    "norm0": lambda u, s: turn_rows(u, "norm0", s),
                    "norm1": lambda u, s: turn_rows(u, "norm1", s),
                    "norm2": lambda u, s: turn_rows(u, "norm2", s),
                    "norm3": lambda u, s: turn_rows(u, "norm3", s),
                    "mlpb1": lambda u, s: turn_rows(u, "mlpb1", s),
                    "feat1": lambda u, s: feat(u, "feat1", s, feat1w[:], bias_p, "norm1"),
                    "feat2": lambda u, s: feat(u, "feat2", s, feat2w[:], None, "norm2"),
                    "feat3": lambda u, s: feat(u, "feat3", s, W3[:].rearrange("p a f -> p (a f)"), None, "norm3"),
                    "turn1": lambda u, s: turn_r(u, "turn1", s),
                    "turn2": lambda u, s: turn_r(u, "turn2", s),
                    "spread1": lambda u, s: spread(u, "spread1", s),
                    "spread2": lambda u, s: spread(u, "spread2", s),
                    "att1a": lambda u, s: attend(u, "att1a", s, 0),
                    "att1b": lambda u, s: attend(u, "att1b", s, 1),
                    "att2a": lambda u, s: attend(u, "att2a", s, 0),
                    "att2b": lambda u, s: attend(u, "att2b", s, 1),
                    "mlpa1": lambda u, s: mlp(u, "mlpa1", s, W1, bias_1, "gin1"),
                    "mlpc1": lambda u, s: mlp(u, "mlpc1", s, W2, bias_2, "mlpb1"),
                }
                def pass_tiles(u):
                    for n in range(tiles_of[u.name]):
                        slot, k = u.tile(u.name, n)
                        pe.wait_ge(taken[slot], k + 1)
                        pe.sem_inc(full[slot], 1)
                        pe.sem_inc(taken[slot], 1)

                walk(pe, "pe", run, pass_tiles)

            @block.scalar
            def _(act):
                A = nc.scalar.activation

                def filled(u, name, s, n=0):
                    slot, k = u.tile(name, n)
                    act.wait_ge(full[slot], k + 1)
                    return ps[slot], taken[slot]

                def turn_rows(u, name, s):
                    o, read = filled(u, name, s)
                    v = o[:].rearrange("p (b n) -> p b n", b=G)
                    if name == "mlpb1":
                        A(HT[s][:], v, ACT.Relu, scale=mlp_g[:, 0:1], bias=mlp_b[:, 0:1]).then_inc(read, 1)
                    else:
                        A(HT[s][:], v, ACT.Relu).then_inc(read, 1)

                def normalise(u, name, s, src):
                    act.wait_ge(sig["rstd"][s], count(u.g, NLN, ln_at[name]))
                    for n in range(TG):
                        a = A(Y[s][:, n, 0:F], src[:, n, :], ACT.Relu, scale=SM[s][:, S_RSTD, n:n + 1],
                              bias=SM[s][:, S_SHIFT, n:n + 1])
                    a.then_inc(sig["normed"][s], 1)

                def mlpc1(u, s):
                    slot, k = u.tile("mlpc1")
                    act.wait_ge(taken[slot], k + 2)
                    A(VA[s], SC[s][:], ACT.Relu).then_inc(sig["mlp_relu"][s], 1)

                def coefb0(u, s):
                    act.wait_ge(sig["cdiff"][s], count(u.g, 1, 0))
                    A(CE[s][:, 0:2 * TG], CF[s][:, 0:2 * TG], ACT.Exp).then_inc(sig["cexp"][s], 1)

                def split0(u, s):
                    act.wait_ge(sig["scaled"][s], count(u.g, 1, 0))
                    A(HI[s][:], SC[s][:], ACT.Copy).then_inc(sig["hi"][s], 1)
                    slot, k = u.tile("feat0", 0)
                    act.wait_ge(taken[slot], k + 2)
                    A(HIB[:], VA[s], ACT.Copy).then_inc(sig["hi"][s], 1)

                def feat(u, name, s):
                    for h in range(2):
                        o, read = filled(u, name, s, h)
                        v = o[:].rearrange("p (r c) -> p r c", c=2 * P)
                        A(HE[s][:, 4 * h:4 * h + 4, :], v[:, :, 0:WD], ACT.Copy).then_inc(read, 1)

                def score(u, name, s):
                    act.wait_ge(sig["ddiff"][s], count(u.g, 2, ATT[name[-1]]))
                    A(CE[s][:], CF[s][:], ACT.Exp).then_inc(sig["dexp"][s], 1)

                def turn_r(u, name, s):
                    o, read = filled(u, name, s)
                    A(RT[s][0:2 * TG, :], o[0:2 * TG, 0:P], ACT.Copy).then_inc(read, 1)

                def spread(u, name, s):
                    o, read = filled(u, name, s)
                    A(R(s), o[:].rearrange("p (b n) -> p b n", b=G), ACT.Copy).then_inc(read, 1)

                def attend(u, name, s, b):
                    slot, k = u.tile("spread" + name[3])
                    act.wait_ge(taken[slot], k + 2)
                    act.wait_ge(sig["r_split"][s], count(u.g, 2, ATT[name[3]]))
                    r, k = u.matrix(name)
                    act.wait_ge(p_taken[r], k + 1)
                    for j in range(T):
                        c = j * G + b
                        a = A(PT[r][:, j, :], R(s)[:, b, :], ACT.Relu, scale=CE[s][:, TG + c:TG + c + 1],
                              bias=NF[s][:, c:c + 1])
                    a.then_inc(sig["raised"][s], 1)

                def collect(u, name, s, b):
                    att = name.replace("collect", "att")
                    slot, k = u.tile(att)
                    act.wait_ge(full[slot], k + 1)
                    r, k = u.matrix(att)
                    v = ps[slot][:].rearrange("p (t c) -> p t c", c=2 * P)
                    for h in range(2):
                        y = Y[s][:].rearrange("p (t b) c -> p t b c", b=G)[:, 2 * h:2 * h + 2, b, 0:F + 1]
                        A(y, v[:, 2 * h:2 * h + 2, 0:F + 1], ACT.Copy).then_inc((p_taken[r], taken[slot])[h], 1)

                def gat1(u, s):
                    act.wait_ge(sig["gated"][s], count(u.g, 2, 0))
                    A(HI[s][:], VA[s], ACT.Relu).then_inc(sig["hi"][s], 1)

                def gin1(u, s):
                    o, read = filled(u, "gin1", s)
                    A(HT[s][:], o[:].rearrange("p (b n) -> p b n", b=G), ACT.Copy).then_inc(read, 1)

                def mlpa1(u, s):
                    o, read = filled(u, "mlpa1", s)
                    A(Y[s][:, :, 0:F], o[:].rearrange("p (r f) -> p r f", f=F), ACT.Copy).then_inc(read, 1)

                def elu2(u, s):
                    act.wait_ge(sig["gated"][s], count(u.g, 2, 1))
                    A(SC[s][:], VA[s], ACT.Exp).then_inc(sig["eluexp"][s], 1)

                def feat3(u, s):
                    for h in range(2):
                        slot, k = u.tile("feat3", h)
                        act.wait_ge(full[slot], k + 1)
                        v = ps[slot][:].rearrange("p (r c) -> p r c", c=2 * P)
                        A(HI[s][:, 4 * h:4 * h + 4, :], v[:, :, F:2 * F], ACT.Copy).then_inc(sig["hi"][s], 1)

                run = {
                    "coefb0": coefb0, "split0": split0, "scale0": lambda u, s: normalise(u, "norm0", s, XL),
                    "scale2": lambda u, s: normalise(u, "norm2", s, X[s]), "mlpc1": mlpc1,
                    "gat1": gat1, "gin1": gin1, "mlpa1": mlpa1, "elu2": elu2,
                    "feat3": feat3,
                    "norm0": lambda u, s: turn_rows(u, "norm0", s),
                    "norm1": lambda u, s: turn_rows(u, "norm1", s),
                    "norm2": lambda u, s: turn_rows(u, "norm2", s),
                    "norm3": lambda u, s: turn_rows(u, "norm3", s),
                    "mlpb1": lambda u, s: turn_rows(u, "mlpb1", s),
                    "feat1": lambda u, s: feat(u, "feat1", s),
                    "feat2": lambda u, s: feat(u, "feat2", s),
                    "score1": lambda u, s: score(u, "score1", s),
                    "score2": lambda u, s: score(u, "score2", s),
                    "turn1": lambda u, s: turn_r(u, "turn1", s),
                    "turn2": lambda u, s: turn_r(u, "turn2", s),
                    "spread1": lambda u, s: spread(u, "spread1", s),
                    "spread2": lambda u, s: spread(u, "spread2", s),
                    "att1a": lambda u, s: attend(u, "att1a", s, 0),
                    "att1b": lambda u, s: attend(u, "att1b", s, 1),
                    "att2a": lambda u, s: attend(u, "att2a", s, 0),
                    "att2b": lambda u, s: attend(u, "att2b", s, 1),
                    "collect1a": lambda u, s: collect(u, "collect1a", s, 0),
                    "collect1b": lambda u, s: collect(u, "collect1b", s, 1),
                    "collect2a": lambda u, s: collect(u, "collect2a", s, 0),
                    "collect2b": lambda u, s: collect(u, "collect2b", s, 1),
                }
                def pass_matrices(u):
                    if u.name in mat_at:
                        r, k = u.matrix(u.name)
                        act.wait_ge(p_taken[r], k + 1)
                        act.sem_inc(p_full[r], 1)
                        act.sem_inc(p_taken[r], 1)

                walk(act, "act", run, pass_matrices)

            @block.gpsimd
            def _(pool):
                TT = nc.gpsimd.tensor_tensor

                def rstd(u, name, s):
                    pool.wait_ge(sig["var"][s], count(u.g, NLN, ln_at[name]))
                    TT(SM[s][:, S_RSTD, :], SM[s][:, S_VAR, :], minus_half[:], ALU.pow).then_inc(sig["rstd"][s], 1)

                def rstd_shift(u, name, s):
                    pool.wait_ge(sig["var"][s], count(u.g, NLN, ln_at[name]))
                    TT(SM[s][:, S_RSTD, :], SM[s][:, S_VAR, :], minus_half[:], ALU.pow).then_inc(pool_order, 1)
                    pool.wait_ge(pool_order, 1)
                    TT(SM[s][:, S_SHIFT, :], SM[s][:, S_RSTD, :], SM[s][:, S_MEAN, :], ALU.mult).then_inc(
                        sig["rstd"][s], 1)
                    pool.sem_clear(pool_order)

                def divide(u, name, s):
                    pool.wait_ge(sig["rstd"][s], count(u.g, NLN, ln_at[name]))
                    pool.wait_ge(sig["centred"][s], count(u.g, 3, ["norm1", "mlpb1", "norm3"].index(name)))
                    TT(Y[s][:, :, 0:F], Y[s][:, :, 0:F], bcast(SM[s][:, S_RSTD, :], F), ALU.mult).then_inc(
                        sig["normed"][s], 1)

                def gat1(u, s):
                    pool.wait_ge(sig["normed"][s], count(u.g, len(NORMED), nd_at["gat1"]))
                    TT(VA[s], VA[s], repeat(gat_g[:], TG), ALU.mult).then_inc(pool_order, 1)
                    pool.wait_ge(pool_order, 1)
                    TT(VA[s], VA[s], repeat(gat_b[:], TG), ALU.add).then_inc(sig["gated"][s], 1)
                    pool.sem_clear(pool_order)

                def mlpc1(u, s):
                    pool.wait_ge(sig["mlp_relu"][s], count(u.g, 1, 0))
                    TT(X[s][:], X[s][:], VA[s], ALU.add).then_inc(sig["x_added"][s], 1)

                def all_max(s, done):
                    TT(MX[s][:, 6:8], MX[s][:, 0:2], ones[:, 0:2], ALU.mult).then_inc(pool_order, 1)
                    pool.wait_ge(pool_order, 1)
                    nc.gpsimd.partition_all_reduce(MX[s][:, 2:4], MX[s][:, 6:8], P, RMAX).then_inc(done, 1)
                    pool.sem_clear(pool_order)

                def cmax(u, s):
                    pool.wait_ge(sig["cmax"][s], count(u.g, 1, 0))
                    all_max(s, sig["cmax_all"][s])

                def dmax(u, name, s):
                    pool.wait_ge(sig["dmax"][s], count(u.g, 2, ATT[name[-1]]))
                    all_max(s, sig["dmax_all"][s])

                def low0(u, s):
                    pool.wait_ge(sig["hi"][s], count(u.g, len(HIS), HIS["a0"]))
                    TT(LO[s][:], SC[s][:], HI[s][:].bitcast(F32), ALU.subtract).then_inc(sig["lo"][s], 1)
                    pool.wait_ge(sig["hi"][s], count(u.g, len(HIS), HIS["b0"]))
                    TT(LOB[:], VA[s], HIB[:].bitcast(F32), ALU.subtract).then_inc(sig["lo_below"][s], 1)

                def shift2(u, s):
                    pool.wait_ge(sig["normed"][s], count(u.g, len(NORMED), nd_at["norm2"]))
                    TT(X[s][:], X[s][:], repeat(ones[:], TG), ALU.subtract).then_inc(sig["shifted"][s], 1)

                def shift3(u, s):
                    pool.wait_ge(sig["centred"][s], count(u.g, 3, 2))
                    TT(X[s][:], X[s][:], repeat(bias3[:], TG), ALU.add).then_inc(sig["shifted"][s], 1)

                run = {
                    "coef0": cmax, "low0": low0, "shift2": shift2, "shift3": shift3, "mlpc1": mlpc1, "gat1": gat1,
                    "norm1": lambda u, s: divide(u, "norm1", s),
                    "norm3": lambda u, s: divide(u, "norm3", s),
                    "mlpb1": lambda u, s: divide(u, "mlpb1", s),
                    "feat1": lambda u, s: dmax(u, "feat1", s),
                    "feat2": lambda u, s: dmax(u, "feat2", s),
                    "stat0": lambda u, s: rstd_shift(u, "norm0", s),
                    "stat1": lambda u, s: rstd(u, "norm1", s),
                    "stat2": lambda u, s: rstd_shift(u, "norm2", s),
                    "stat3": lambda u, s: rstd(u, "norm3", s),
                    "gats1": lambda u, s: rstd(u, "gat1", s),
                    "mlps1": lambda u, s: rstd(u, "mlpb1", s),
                }
                walk(pool, "pool", run)

            @block.vector
            def _(dve):
                V = nc.vector
                order = [0]

                def link(ins):
                    order[0] += 1
                    ins.then_inc(dve_order, 1)
                    dve.wait_ge(dve_order, order[0])

                def filled(u, name, s, n=0):
                    slot, k = u.tile(name, n)
                    dve.wait_ge(full[slot], k + 1)
                    return ps[slot], taken[slot]

                def read_by_act(u, name, s, n=0):
                    slot, k = u.tile(name, n)
                    dve.wait_ge(taken[slot], k + 2)

                def stats(u, s, src, sums=None, sign=1.0):
                    st, sm = ST[s], SM[s]
                    for n in range(TG):
                        a = V.bn_stats(st[:, n, :], src(n))
                    link(a)
                    V.tensor_tensor(sm[:, S_DIF, :], st[:, :, 1], st[:, :, 4], ALU.subtract)
                    V.tensor_tensor(sm[:, S_SUM, :], st[:, :, 1], st[:, :, 4], ALU.add)
                    if sums is not None:
                        V.tensor_scalar(sm[:, S_INV, :], sums, TINY, None, ALU.max)
                    link(V.scalar_tensor_tensor(out=sm[:, S_Q, :], in0=st[:, :, 2],
                                                scalar=F * LN_EPS if sums is None else 0.0, in1=st[:, :, 5],
                                                op0=ALU.add, op1=ALU.add))
                    if sums is not None:
                        V.reciprocal(sm[:, S_INV, :], sm[:, S_INV, :])
                    V.tensor_scalar(sm[:, S_MEAN, :], sm[:, S_SUM, :], sign * 0.5, None, ALU.mult)
                    link(V.scalar_tensor_tensor(out=sm[:, S_DD, :], in0=sm[:, S_DIF, :], scalar=0.25,
                                                in1=sm[:, S_DIF, :], op0=ALU.mult, op1=ALU.mult))
                    a = V.scalar_tensor_tensor(out=sm[:, S_VAR, :], in0=sm[:, S_Q, :], scalar=1.0 / F,
                                               in1=sm[:, S_DD, :], op0=ALU.mult, op1=ALU.add)
                    if sums is not None:
                        link(a)
                        for _ in range(2):
                            link(V.tensor_tensor(sm[:, S_VAR, :], sm[:, S_VAR, :], sm[:, S_INV, :], ALU.mult))
                        a = V.tensor_scalar(sm[:, S_VAR, :], sm[:, S_VAR, :], LN_EPS, None, ALU.add)
                    a.then_inc(sig["var"][s], 1)

                def centre(u, name, s, src):
                    V.tensor_tensor(Y[s][:, :, 0:F], src, bcast(SM[s][:, S_MEAN, :], F), ALU.subtract).then_inc(
                        sig["centred"][s], 1)

                def stat0(u, s):
                    dve.wait_ge(x_loaded, u.all_groups(16 * G, 16 * G))
                    stats(u, s, lambda n: XL[:, n, :], sign=-1.0)

                def stat(u, s):
                    stats(u, s, lambda n: X[s][:, n, :])

                def stat2(u, s):
                    dve.wait_ge(sig["x_added"][s], count(u.g, 1, 0))
                    stats(u, s, lambda n: X[s][:, n, :], sign=-1.0)

                def coef0(u, s):
                    o, read = filled(u, "coef0", s)
                    V.tensor_copy(US[s][:], o[:, 0:4 * TG].rearrange("p (r c) -> p r c", c=4)).then_inc(read, 1)
                    read_by_act(u, "coef0", s)
                    u4 = US[s][:].rearrange("p (t o b) c -> p t o b c", t=HALF, o=2)
                    V.tensor_copy(CD[s][:, 0:TG], US[s][:, :, 0])
                    link(V.tensor_tensor(CD[s][:, TG:12].rearrange("p (t b) -> p t b", b=G), u4[:, :, 0, :, 1],
                                         u4[:, :, 1, :, 2], ALU.add))
                    link(V.scalar_tensor_tensor(out=CD[s][:], in0=CD[s][:], scalar=0.1, in1=CD[s][:],
                                                op0=ALU.mult, op1=ALU.max))
                    V.reduce_max(MX[s][:, 0:2], CD[s][:, 0:TG].rearrange("p (r b) -> p b r", b=G),
                                 AX_X).then_inc(sig["cmax"][s], 1)

                def coefm0(u, s):
                    dve.wait_ge(sig["cmax_all"][s], count(u.g, 1, 0))
                    m = MX[s][:, 2:4]
                    d = CD[s][:, TG:12].rearrange("p (t b) -> p t b", b=G)
                    mk = SM[s][:, S_A, 0:4].rearrange("p (t b) -> p t b", b=G)
                    V.tensor_tensor(CF[s][:, 0:TG].rearrange("p (r b) -> p r b", b=G),
                                    CD[s][:, 0:TG].rearrange("p (r b) -> p r b", b=G), repeat(m, 4), ALU.subtract)
                    link(V.tensor_tensor(mk, d, repeat(m, 2), ALU.max))
                    V.tensor_tensor(CF[s][:, 8:12].rearrange("p (t b) -> p t b", b=G), repeat(m, 2), mk, ALU.subtract)
                    V.tensor_tensor(CF[s][:, 12:16].rearrange("p (t b) -> p t b", b=G), d, mk,
                                    ALU.subtract).then_inc(sig["cdiff"][s], 1)

                def coefb0(u, s):
                    o, read = filled(u, "coefb0", s)
                    sm = SM[s]
                    a2, b2 = repeat(CE[s][:, 8:12], 2), repeat(CE[s][:, 12:16], 2)

                    def two(ap):
                        return ap.rearrange("p (h r) -> p h r", h=2)
                    V.tensor_tensor(two(sm[:, S_B, :]), two(low8[:]), b2, ALU.mult)
                    V.tensor_tensor(two(sm[:, S_Z, :]), two(o[:, 0:TG]), a2, ALU.mult).then_inc(read, 1)
                    read_by_act(u, "coefb0", s)
                    link(V.tensor_tensor(sm[:, S_Z, :], sm[:, S_Z, :], sm[:, S_B, :], ALU.add))
                    link(V.tensor_tensor(sm[:, S_Z, :], sm[:, S_Z, :], empty8[:], ALU.add))
                    link(V.tensor_scalar(sm[:, S_Z, :], sm[:, S_Z, :], TINY, None, ALU.max))
                    link(V.reciprocal(sm[:, S_Z, :], sm[:, S_Z, :]))
                    V.tensor_tensor(two(sm[:, S_A, :]), two(sm[:, S_Z, :]), a2, ALU.mult)
                    link(V.tensor_tensor(two(sm[:, S_B, :]), two(sm[:, S_Z, :]), b2, ALU.mult))
                    link(V.tensor_tensor(sm[:, S_B, :], sm[:, S_B, :], full8[:], ALU.mult))
                    link(V.tensor_tensor(sm[:, S_B, :], sm[:, S_B, :], share8[:], ALU.add))

                def split0(u, s):
                    o, read = filled(u, "feat0", s)
                    v = o[:].rearrange("p (r f) -> p r f", f=F)
                    V.tensor_tensor(SC[s][:], v, bcast(SM[s][:, S_A, :], F), ALU.mult).then_inc(sig["scaled"][s], 1)
                    V.tensor_tensor(VA[s], v, bcast(SM[s][:, S_B, :], F), ALU.mult).then_inc(read, 1)

                def agg0(u, s):
                    og, read_g = filled(u, "agg0", s)
                    V.tensor_tensor(SC[s][:], og[:].rearrange("p (r f) -> p r f", f=F), bcast(CE[s][:, 0:TG], F),
                                    ALU.mult).then_inc(read_g, 1)

                def self0(u, s):
                    os_, read_s = filled(u, "self0", s)
                    dve.wait_ge(sig["stored"][s], u.g * (16 * G) + 16)
                    V.tensor_tensor(X[s][:], XL[:], os_[:].rearrange("p (r f) -> p r f", f=F),
                                    ALU.add).then_inc(read_s, 1)
                    sc = SC[s][:].rearrange("p (t h b) f -> p t h (b f)", t=HALF, h=2)
                    xt = X[s][:, 0:HALF * G, :].rearrange("p (t b) f -> p t (b f)", b=G)
                    read_by_act(u, "agg0", s)
                    read_by_act(u, "self0", s)
                    link(V.tensor_tensor(xt, xt, sc[:, :, 0, :], ALU.add))
                    V.tensor_tensor(xt, xt, sc[:, :, 1, :], ALU.add).then_inc(raw_free, 1)
                    dve.wait_ge(raw_free, u.all_groups(1, 1))

                def dmax(u, name, s):
                    read_by_act(u, name, s, 0)
                    read_by_act(u, name, s, 1)
                    V.reduce_max(MX[s][:, 0:2], HE[s][:].rearrange("p (t b) c -> p b t c", b=G)[:, :, :, F],
                                 AX_X).then_inc(sig["dmax"][s], 1)

                def ddiff(u, name, s):
                    dve.wait_ge(sig["dmax_all"][s], count(u.g, 2, ATT[name[-1]]))
                    he = HE[s][:].rearrange("p (t b) c -> p t b c", b=G)
                    cf = CF[s][:].rearrange("p (k t b) -> p k t b", k=3, b=G)
                    top = repeat(MX[s][:, 2:4], T)
                    V.tensor_tensor(cf[:, 0], he[:, :, :, F], top, ALU.subtract)
                    link(V.tensor_tensor(cf[:, 2], he[:, :, :, F + 1], top, ALU.add))
                    const = const1[:, 0:1] if name[-1] == "1" else 0.0
                    V.tensor_scalar(cf[:, 1], cf[:, 0], 0.2, None, ALU.mult)
                    link(V.tensor_scalar(cf[:, 2], cf[:, 2], const, -0.8, ALU.add, ALU.mult))
                    V.tensor_scalar(cf[:, 2], cf[:, 2], 0.0, None, ALU.min)
                    V.memset(HE[s][:, :, F:F + 1], 1.0).then_inc(sig["ddiff"][s], 1)

                def turn_r(u, name, s):
                    n = ATT[name[-1]]
                    dve.wait_ge(sig["dexp"][s], count(u.g, 2, n))
                    rr = CE[s][:, 2 * TG:3 * TG]
                    V.tensor_scalar(NF[s][:], CE[s][:, 0:TG], -1.0, None, ALU.mult)
                    if n == 1:
                        link(V.tensor_tensor(rr, rr, rescue8[:], ALU.add))
                    link(V.tensor_copy(R2[s][:, 0:TG], rr))
                    V.tensor_tensor(R2[s][:, TG:2 * TG], rr, R2[s][:, 0:TG].bitcast(F32), ALU.subtract).then_inc(
                        sig["r_split"][s], 1)

                def attend(u, name, s, b):
                    n = ATT[name[3]]
                    mask = (maskT[:].bitcast(F32), mask2[:])[n]
                    dve.wait_ge(sig["raised"][s], count(u.g, 2 * G, n * G + b))
                    r, k = u.matrix(name)
                    for j in range(T):
                        c = j * G + b
                        a = V.scalar_tensor_tensor(out=PT[r][:, j, :], in0=PT[r][:, j, :],
                                                   scalar=CE[s][:, c:c + 1], in1=mask[:, j, :], op0=ALU.add,
                                                   op1=ALU.min)
                    a.then_inc(p_full[r], 1)

                def gats1(u, s):
                    for b in range(G):
                        read_by_act(u, "att1" + "ab"[b], s)
                    stats(u, s, lambda n: Y[s][:, n, 0:F], Y[s][:, :, F])

                def gat1(u, s):
                    sm = SM[s]
                    dve.wait_ge(sig["rstd"][s], count(u.g, NLN, ln_at["gat1"]))
                    link(V.tensor_tensor(sm[:, S_RS, :], sm[:, S_RSTD, :], sm[:, S_INV, :], ALU.mult))
                    for n in range(TG):
                        a = V.tensor_scalar(VA[s][:, n, :], Y[s][:, n, 0:F], sm[:, S_MEAN, n:n + 1],
                                            sm[:, S_RS, n:n + 1], ALU.subtract, ALU.mult)
                    a.then_inc(sig["normed"][s], 1)

                def gatl1(u, s):
                    dve.wait_ge(sig["hi"][s], count(u.g, len(HIS), HIS["1"]))
                    V.scalar_tensor_tensor(out=LO[s][:], in0=VA[s], scalar=0.0, in1=HI[s][:].bitcast(F32),
                                           op0=ALU.max, op1=ALU.subtract).then_inc(sig["lo"][s], 1)

                def mlps1(u, s):
                    read_by_act(u, "mlpa1", s)
                    stats(u, s, lambda n: Y[s][:, n, 0:F])

                def mlpc1(u, s):
                    o, read = filled(u, "mlpc1", s)
                    V.scalar_tensor_tensor(out=SC[s][:], in0=VA[s], scalar=0.0,
                                           in1=o[:].rearrange("p (r f) -> p r f", f=F), op0=ALU.max,
                                           op1=ALU.add).then_inc(read, 1)

                def elud2(u, s):
                    for b in range(G):
                        read_by_act(u, "att2" + "ab"[b], s)
                    link(V.tensor_scalar(SM[s][:, S_INV, :], Y[s][:, :, F], TINY, None, ALU.max))
                    link(V.reciprocal(SM[s][:, S_INV, :], SM[s][:, S_INV, :]))
                    for n in range(TG):
                        a = V.scalar_tensor_tensor(out=VA[s][:, n, :], in0=Y[s][:, n, 0:F],
                                                   scalar=SM[s][:, S_INV, n:n + 1], in1=bias2[:], op0=ALU.mult,
                                                   op1=ALU.add)
                    a.then_inc(sig["gated"][s], 1)

                def elu2(u, s):
                    dve.wait_ge(sig["eluexp"][s], count(u.g, 1, 0))
                    dve.wait_ge(sig["shifted"][s], count(u.g, 2, 0))
                    link(V.scalar_tensor_tensor(out=SC[s][:], in0=SC[s][:], scalar=1.0, in1=X[s][:], op0=ALU.min,
                                                op1=ALU.add))
                    link(V.scalar_tensor_tensor(out=X[s][:], in0=VA[s], scalar=0.0, in1=SC[s][:], op0=ALU.max,
                                                op1=ALU.add))

                def feat3(u, s):
                    dve.wait_ge(sig["shifted"][s], count(u.g, 2, 1))
                    for h in range(2):
                        slot, k = u.tile("feat3", h)
                        dve.wait_ge(sig["hi"][s], count(u.g, len(HIS), HIS["3a"] + h))
                        v = ps[slot][:].rearrange("p (r c) -> p r c", c=2 * P)
                        a = V.tensor_tensor(LO[s][:, 4 * h:4 * h + 4, :], v[:, :, F:2 * F],
                                            HI[s][:, 4 * h:4 * h + 4, :].bitcast(F32), ALU.subtract)
                        if h == 1:
                            a.then_inc(sig["lo"][s], 1)
                        for tt in range(2):
                            t = 2 * h + tt
                            xt = X[s][:, t * G:(t + 1) * G, :]
                            a = V.scalar_tensor_tensor(out=xt, in0=v[:, tt * G:(tt + 1) * G, 0:F],
                                                       scalar=diag3[:, t:t + 1], in1=xt, op0=ALU.mult, op1=ALU.add)
                        a.then_inc(taken[slot], 1)

                def agg3(u, s):
                    for h in range(2):
                        read_by_act(u, "feat3", s, h)
                    o, read = filled(u, "agg3", s)
                    V.tensor_tensor(X[s][:], X[s][:], o[:].rearrange("p (r f) -> p r f", f=F),
                                    ALU.add).then_inc(read, 1)
                    read_by_act(u, "agg3", s)
                    dve.sem_inc(sig["result"][s], 1)

                run = {
                    "stat0": stat0, "stat1": stat, "stat2": stat2, "stat3": stat, "coef0": coef0, "coefm0": coefm0,
                    "coefb0": coefb0, "split0": split0, "agg0": agg0, "self0": self0, "gats1": gats1, "gat1": gat1, "gatl1": gatl1,
                    "mlps1": mlps1, "mlpc1": mlpc1, "elud2": elud2, "elu2": elu2, "feat3": feat3, "agg3": agg3,
                    "norm1": lambda u, s: centre(u, "norm1", s, X[s][:]),
                    "norm3": lambda u, s: centre(u, "norm3", s, X[s][:]),
                    "mlpb1": lambda u, s: centre(u, "mlpb1", s, Y[s][:, :, 0:F]),
                    "feat1": lambda u, s: dmax(u, "feat1", s),
                    "feat2": lambda u, s: dmax(u, "feat2", s),
                    "score1": lambda u, s: ddiff(u, "score1", s),
                    "score2": lambda u, s: ddiff(u, "score2", s),
                    "turn1": lambda u, s: turn_r(u, "turn1", s),
                    "turn2": lambda u, s: turn_r(u, "turn2", s),
                    "att1a": lambda u, s: attend(u, "att1a", s, 0),
                    "att1b": lambda u, s: attend(u, "att1b", s, 1),
                    "att2a": lambda u, s: attend(u, "att2a", s, 0),
                    "att2b": lambda u, s: attend(u, "att2b", s, 1),
                }
                def end_pass():
                    order[0] = 0
                    dve.sem_clear(dve_order)

                walk(dve, "dve", run, end_pass=end_pass)


_INS = ["x", "adj", "L0_gnn_others_weight", "L0_gnn_self_weight", "L0_gnn_att_weight", "L1_gnn_Wp", "L1_gnn_bp",
        "L1_gnn_a_src", "L1_gnn_a_dst", "L1_gnn_gat_g", "L1_gnn_gat_b", "L1_gnn_eps", "L1_gnn_W1", "L1_gnn_b1",
        "L1_gnn_mlp_g", "L1_gnn_mlp_b", "L1_gnn_W2", "L1_gnn_b2", "L2_gnn_W", "L2_gnn_a", "L2_gnn_bias",
        "L3_gnn_W", "L3_gnn_e", "L3_gnn_bias"]
_OUTS = [((32, 512, 128), "float32")]


def kernel(**inputs):
    import numpy as _np
    import concourse.bacc as _bacc
    from concourse import mybir as _mybir
    from concourse.bass_utils import run_bass_kernel_spmd as _run

    nc = _bacc.Bacc("TRN2", target_bir_lowering=False, num_devices=1)
    arrays, args = {}, []
    for name in _INS:
        a = _np.ascontiguousarray(inputs[name])
        arrays[f"in_{name}_dram"] = a
        args.append(nc.dram_tensor(f"in_{name}_dram", a.shape, _mybir.dt.from_np(a.dtype), kind="ExternalInput").ap())
    for i, (shape, dtype) in enumerate(_OUTS):
        dt = _mybir.dt.from_np(_np.dtype(dtype))
        args.append(nc.dram_tensor(f"out_{i}_dram", shape, dt, kind="ExternalOutput").ap())
    gnn_kernel(nc, *args)
    r = _run(nc, [arrays], core_ids=[0])
    got = tuple(r.results[0][f"out_{i}_dram"] for i in range(len(_OUTS)))
    return got[0]
```
